# Optimizing a Trainium2 kernel written in Bass

```python
import numpy as np
import jax
import jax.numpy as jnp

def _softmax(x, axis=-1):
    return jax.nn.softmax(x, axis=axis)

def _gelu(x):
    return jax.nn.gelu(x, approximate=True)

def _silu(x):
    return jax.nn.silu(x)

def _sigmoid(x):
    return jax.nn.sigmoid(x)

def _layernorm(x, axis=-1, eps=1e-05):
    m = jnp.mean(x, axis=axis, keepdims=True)
    v = jnp.var(x, axis=axis, keepdims=True)
    return (x - m) / jnp.sqrt(v + eps)

def _scatter_add(tgt, idx, src, axis=0):
    return tgt.at[idx].add(src)

def _segment_sum(src, seg, n):
    return jax.ops.segment_sum(src, seg, n)
kernel_name = 'mk_decoder_postln_d2_seqx_r4_9e2a17'

def setup_inputs(seed: int=0):
    np.random.seed(seed)
    _w = jnp.asarray

    def _rec_inputs():
        import jax
        import jax.numpy as jnp
        _rk = jax.random.key(seed)
        x = -0.0005207 + 1.001 * jax.random.normal(jax.random.fold_in(_rk, 1), (16, 128, 256), jnp.float32)
        _lenS = 128 - jax.random.randint(jax.random.fold_in(_rk, 7), (16,), 0, max(1, 128 // 4) + 1, jnp.int32)
        _lenS2 = 128 - jax.random.randint(jax.random.fold_in(_rk, 8), (16,), 0, max(1, 128 // 4) + 1, jnp.int32)
        _ctx_512P = jax.random.normal(jax.random.fold_in(_rk, 11), (16, 16, 128), jnp.float32)
        _ctx_512c = jax.random.dirichlet(jax.random.fold_in(_rk, 511), 0.3 * jnp.ones((16,), jnp.float32), (16, 128))
        _ctx_512t = jnp.einsum('bsk,bkd->bsd', _ctx_512c, _ctx_512P)
        _ctx_512t = _ctx_512t * jax.lax.rsqrt(jnp.mean(jnp.square(_ctx_512t)) + 1e-12) * 0.953939
        ctx_512 = 0.502058 + 0.29099 * (_ctx_512t + 0.3 * jax.random.normal(jax.random.fold_in(_rk, 611), (16, 128, 128), jnp.float32))
        itok_BxS2xS_0_7 = jax.random.randint(jax.random.fold_in(_rk, 12), (16, 128, 128), 0, 8, jnp.int32)
        return (x, ctx_512, itok_BxS2xS_0_7)
    x, ctx_512, itok_BxS2xS_0_7 = _rec_inputs()

    def _L0_attn_setup():
        import jax, jax.numpy as jnp
        import numpy as np
        import math
        B, S, H, NH = (2, 512, 256, 16)
        DK = H // NH
        key = jax.random.key(seed)
        k1, k2, k3 = jax.random.split(key, 3)
        scale = 1.0 / math.sqrt(H)
        return {'x': jax.random.normal(k1, (B, S, H), dtype=jnp.float32), 'w_attn': jax.random.normal(k2, (H, 3 * H), dtype=jnp.float32) * scale, 'b_attn': jnp.zeros((3 * H,), dtype=jnp.float32), 'w_proj': jax.random.normal(k3, (H, H), dtype=jnp.float32) * scale, 'b_proj': jnp.zeros((H,), dtype=jnp.float32)}
    _L0_attn_all = _L0_attn_setup()
    _L0_attn_in = {k: v for k, v in _L0_attn_all.items() if k in ('w_attn', 'b_attn', 'w_proj', 'b_proj')}
    del _L0_attn_all

    def _L0_xattn_setup():
        import jax, jax.numpy as jnp
        import numpy as np
        key = jax.random.key(seed)
        k1, k2, k3, k4, k5 = jax.random.split(key, 5)
        B, K, S, E, I, D = (4, 2, 128, 8, 256, 512)
        x = jax.random.normal(k1, (B, S, I), dtype=jnp.float32)
        weights = jax.random.uniform(k2, (B, K, S), dtype=jnp.float32)
        ensembles = jax.random.randint(k3, (B, K, S), 0, E, dtype=jnp.int64)
        lim1 = float(np.sqrt(6.0 / (D + I)))
        proj_in = jax.random.uniform(k4, (E, D, I), dtype=jnp.float32, minval=-lim1, maxval=lim1)
        proj_out = jax.random.uniform(k5, (E, I, D), dtype=jnp.float32, minval=-lim1, maxval=lim1)
        return {'x': x, 'weights': weights, 'ensembles': ensembles, 'proj_in': proj_in, 'proj_out': proj_out}
    _L0_xattn_all = _L0_xattn_setup()
    _L0_xattn_in = {k: v for k, v in _L0_xattn_all.items() if k in ('proj_in', 'proj_out')}
    del _L0_xattn_all

    def _L0_ffn_setup():
        import jax, jax.numpy as jnp
        import numpy as np
        B, S, D, H, F, E = (2, 256, 256, 16, 512, 8)
        HD = D // H

        def _ln(x, g, b, eps=1e-05):
            m = x.mean(-1, keepdims=True)
            v = ((x - m) ** 2).mean(-1, keepdims=True)
            return (x - m) / jnp.sqrt(v + eps) * g + b
        key = jax.random.key(seed)
        ks = jax.random.split(key, 12)
        rn = lambda k, shp, s=0.02: jax.random.normal(k, shp, jnp.float32) * s
        return {'src': jax.random.normal(ks[0], (B, S, D), jnp.float32), 'q_w': rn(ks[1], (D, D)), 'k_w': rn(ks[2], (D, D)), 'v_w': rn(ks[3], (D, D)), 'out_w': rn(ks[4], (D, D)), 'gate_w': rn(ks[5], (D, D)), 'gate_b': rn(ks[6], (D,)), 'scale_w': rn(ks[7], (H, HD)), 'n1_g': jnp.ones((D,), jnp.float32), 'n1_b': jnp.zeros((D,), jnp.float32), 'n2_g': jnp.ones((D,), jnp.float32), 'n2_b': jnp.zeros((D,), jnp.float32), 'moe_gate_w': rn(ks[8], (D, E)), 'moe_gate_b': jnp.zeros((E,), jnp.float32), 'w1': rn(ks[9], (E, D, F)), 'b1': jnp.zeros((E, F), jnp.float32), 'ln_g': jnp.ones((E, F), jnp.float32), 'ln_b': jnp.zeros((E, F), jnp.float32), 'w2': rn(ks[10], (E, F, D)), 'b2': jnp.zeros((E, D), jnp.float32), 'res_scale': jnp.ones((E,), jnp.float32)}
    _L0_ffn_all = _L0_ffn_setup()
    _L0_ffn_in = {k: v for k, v in _L0_ffn_all.items() if k in ('q_w', 'k_w', 'v_w', 'out_w', 'gate_w', 'gate_b', 'scale_w', 'n1_g', 'n1_b', 'n2_g', 'n2_b', 'moe_gate_w', 'moe_gate_b', 'w1', 'b1', 'ln_g', 'ln_b', 'w2', 'b2', 'res_scale')}
    del _L0_ffn_all

    def _L1_attn_setup():
        import jax, jax.numpy as jnp
        import numpy as np
        D = 256
        H = 16
        HD = D // H
        R = HD
        N, T = (2, 512)
        W_LEFT, W_RIGHT = (127, 128)
        ROPE_BASE = 10000.0

        def _rope(x, cos, sin):
            x1 = x[..., :R // 2]
            x2 = x[..., R // 2:R]
            rot = jnp.concatenate([x1 * cos - x2 * sin, x2 * cos + x1 * sin], axis=-1)
            if R < x.shape[-1]:
                rot = jnp.concatenate([rot, x[..., R:]], axis=-1)
            return rot
        key = jax.random.key(seed)
        k1, k2, k3, k4 = jax.random.split(key, 4)
        x = jax.random.normal(k1, (N, T, D), dtype=jnp.float32)
        w_qkv = jax.random.normal(k2, (3 * D, D), dtype=jnp.float32) * 0.02
        w_out = jax.random.normal(k3, (D, D), dtype=jnp.float32) * 0.02
        b_out = jax.random.normal(k4, (D,), dtype=jnp.float32) * 0.02
        return {'x': x, 'w_qkv': w_qkv, 'w_out': w_out, 'b_out': b_out}
    _L1_attn_all = _L1_attn_setup()
    _L1_attn_in = {k: v for k, v in _L1_attn_all.items() if k in ('w_qkv', 'w_out', 'b_out')}
    del _L1_attn_all

    def _L1_xattn_setup():
        import jax, jax.numpy as jnp
        import numpy as np
        HEADS = 16
        D_MODEL = 256
        IMG_MODEL = 128
        D_K = D_MODEL // HEADS
        key = jax.random.key(seed)
        ks = jax.random.split(key, 12)
        B, LQ, LKV = (8, 512, 256)
        s_dm = 1.0 / np.sqrt(D_MODEL)
        s_im = 1.0 / np.sqrt(IMG_MODEL)
        return {'q': jax.random.normal(ks[0], (B, LQ, D_MODEL), jnp.float32), 'k': jax.random.normal(ks[1], (B, LKV, IMG_MODEL), jnp.float32), 'v': jax.random.normal(ks[2], (B, LKV, IMG_MODEL), jnp.float32), 'Wq': jax.random.normal(ks[3], (D_MODEL, D_MODEL), jnp.float32) * s_dm, 'bq': jnp.zeros((D_MODEL,), jnp.float32), 'Wk': jax.random.normal(ks[4], (IMG_MODEL, D_MODEL), jnp.float32) * s_im, 'bk': jnp.zeros((D_MODEL,), jnp.float32), 'Wv': jax.random.normal(ks[5], (IMG_MODEL, D_MODEL), jnp.float32) * s_im, 'bv': jnp.zeros((D_MODEL,), jnp.float32), 'Wo': jax.random.normal(ks[6], (D_MODEL, D_MODEL), jnp.float32) * s_dm, 'bo': jnp.zeros((D_MODEL,), jnp.float32)}
    _L1_xattn_all = _L1_xattn_setup()
    _L1_xattn_in = {k: v for k, v in _L1_xattn_all.items() if k in ('Wq', 'bq', 'Wk', 'bk', 'Wv', 'bv', 'Wo', 'bo')}
    del _L1_xattn_all

    def _L1_ffn_setup():
        import jax, jax.numpy as jnp
        import numpy as np
        TOP_K = 6

        def _glu_mlp(x, wg, wu, wd):
            return jax.nn.silu(x @ wg) * (x @ wu) @ wd
        key = jax.random.key(seed)
        ks = jax.random.split(key, 8)
        B, S, D, E, F, FS = (2, 512, 256, 8, 128, 256)
        sc = 0.02
        return {'hidden_states': jax.random.normal(ks[0], (B, S, D), jnp.float32), 'router_w': jax.random.normal(ks[1], (D, E), jnp.float32) * sc, 'w_gate': jax.random.normal(ks[2], (E, D, F), jnp.float32) * sc, 'w_up': jax.random.normal(ks[3], (E, D, F), jnp.float32) * sc, 'w_down': jax.random.normal(ks[4], (E, F, D), jnp.float32) * sc, 'ws_gate': jax.random.normal(ks[5], (D, FS), jnp.float32) * sc, 'ws_up': jax.random.normal(ks[6], (D, FS), jnp.float32) * sc, 'ws_down': jax.random.normal(ks[7], (FS, D), jnp.float32) * sc}
    _L1_ffn_all = _L1_ffn_setup()
    _L1_ffn_in = {k: v for k, v in _L1_ffn_all.items() if k in ('router_w', 'w_gate', 'w_up', 'w_down', 'ws_gate', 'ws_up', 'ws_down')}
    del _L1_ffn_all
    return {'x': x, 'ctx_512': ctx_512, 'itok_BxS2xS_0_7': itok_BxS2xS_0_7, 'L0_attn_w_attn': _L0_attn_in['w_attn'], 'L0_attn_b_attn': _L0_attn_in['b_attn'], 'L0_attn_w_proj': _L0_attn_in['w_proj'], 'L0_attn_b_proj': _L0_attn_in['b_proj'], 'L0_xattn_proj_in': _L0_xattn_in['proj_in'], 'L0_xattn_proj_out': _L0_xattn_in['proj_out'], 'L0_ffn_q_w': _L0_ffn_in['q_w'], 'L0_ffn_k_w': _L0_ffn_in['k_w'], 'L0_ffn_v_w': _L0_ffn_in['v_w'], 'L0_ffn_out_w': _L0_ffn_in['out_w'], 'L0_ffn_gate_w': _L0_ffn_in['gate_w'], 'L0_ffn_gate_b': _L0_ffn_in['gate_b'], 'L0_ffn_scale_w': _L0_ffn_in['scale_w'], 'L0_ffn_n1_g': _L0_ffn_in['n1_g'], 'L0_ffn_n1_b': _L0_ffn_in['n1_b'], 'L0_ffn_n2_g': _L0_ffn_in['n2_g'], 'L0_ffn_n2_b': _L0_ffn_in['n2_b'], 'L0_ffn_moe_gate_w': _L0_ffn_in['moe_gate_w'], 'L0_ffn_moe_gate_b': _L0_ffn_in['moe_gate_b'], 'L0_ffn_w1': _L0_ffn_in['w1'], 'L0_ffn_b1': _L0_ffn_in['b1'], 'L0_ffn_ln_g': _L0_ffn_in['ln_g'], 'L0_ffn_ln_b': _L0_ffn_in['ln_b'], 'L0_ffn_w2': _L0_ffn_in['w2'], 'L0_ffn_b2': _L0_ffn_in['b2'], 'L0_ffn_res_scale': _L0_ffn_in['res_scale'], 'L1_attn_w_qkv': _L1_attn_in['w_qkv'], 'L1_attn_w_out': _L1_attn_in['w_out'], 'L1_attn_b_out': _L1_attn_in['b_out'], 'L1_xattn_Wq': _L1_xattn_in['Wq'], 'L1_xattn_bq': _L1_xattn_in['bq'], 'L1_xattn_Wk': _L1_xattn_in['Wk'], 'L1_xattn_bk': _L1_xattn_in['bk'], 'L1_xattn_Wv': _L1_xattn_in['Wv'], 'L1_xattn_bv': _L1_xattn_in['bv'], 'L1_xattn_Wo': _L1_xattn_in['Wo'], 'L1_xattn_bo': _L1_xattn_in['bo'], 'L1_ffn_router_w': _L1_ffn_in['router_w'], 'L1_ffn_w_gate': _L1_ffn_in['w_gate'], 'L1_ffn_w_up': _L1_ffn_in['w_up'], 'L1_ffn_w_down': _L1_ffn_in['w_down'], 'L1_ffn_ws_gate': _L1_ffn_in['ws_gate'], 'L1_ffn_ws_up': _L1_ffn_in['ws_up'], 'L1_ffn_ws_down': _L1_ffn_in['ws_down']}

def reference(x, ctx_512, itok_BxS2xS_0_7, L0_attn_w_attn, L0_attn_b_attn, L0_attn_w_proj, L0_attn_b_proj, L0_xattn_proj_in, L0_xattn_proj_out, L0_ffn_q_w, L0_ffn_k_w, L0_ffn_v_w, L0_ffn_out_w, L0_ffn_gate_w, L0_ffn_gate_b, L0_ffn_scale_w, L0_ffn_n1_g, L0_ffn_n1_b, L0_ffn_n2_g, L0_ffn_n2_b, L0_ffn_moe_gate_w, L0_ffn_moe_gate_b, L0_ffn_w1, L0_ffn_b1, L0_ffn_ln_g, L0_ffn_ln_b, L0_ffn_w2, L0_ffn_b2, L0_ffn_res_scale, L1_attn_w_qkv, L1_attn_w_out, L1_attn_b_out, L1_xattn_Wq, L1_xattn_bq, L1_xattn_Wk, L1_xattn_bk, L1_xattn_Wv, L1_xattn_bv, L1_xattn_Wo, L1_xattn_bo, L1_ffn_router_w, L1_ffn_w_gate, L1_ffn_w_up, L1_ffn_w_down, L1_ffn_ws_gate, L1_ffn_ws_up, L1_ffn_ws_down):
    import jax
    import jax.numpy as jnp

    def _L0_attn_ref(x, w_attn, b_attn, w_proj, b_proj):
        import jax, jax.numpy as jnp
        import numpy as np
        import math
        B, S, H, NH = (2, 512, 256, 16)
        DK = H // NH
        bs, seq_len, hidden = x.shape
        qkv = x @ w_attn + b_attn
        q, k, v = jnp.split(qkv, 3, axis=-1)

        def heads(t):
            return t.reshape(bs, seq_len, NH, DK).transpose(0, 2, 1, 3)
        q, k, v = (heads(q), heads(k), heads(v))
        scores = jnp.einsum('bhqd,bhkd->bhqk', q, k) / math.sqrt(DK)
        causal = jnp.tril(jnp.ones((seq_len, seq_len), dtype=bool))
        scores = jnp.where(causal[None, None], scores, -jnp.inf)
        attn = jax.nn.softmax(scores, axis=-1)
        out = jnp.einsum('bhqk,bhkd->bhqd', attn, v)
        out = out.transpose(0, 2, 1, 3).reshape(bs, seq_len, hidden)
        return out @ w_proj + b_proj

    def _L0_xattn_ref(x, weights, ensembles, proj_in, proj_out):
        import jax, jax.numpy as jnp
        import numpy as np
        E = proj_in.shape[0]
        h = jax.nn.relu(jnp.einsum('edi,bsi->bsed', proj_in, x))
        o = jnp.einsum('eid,bsed->bsei', proj_out, h)
        onehot = jax.nn.one_hot(ensembles, E, dtype=x.dtype)
        gate = jnp.einsum('bks,bkse->bse', weights, onehot)
        return jnp.einsum('bsei,bse->bsi', o, gate)

    def _L0_ffn_ref(src, q_w, k_w, v_w, out_w, gate_w, gate_b, scale_w, n1_g, n1_b, n2_g, n2_b, moe_gate_w, moe_gate_b, w1, b1, ln_g, ln_b, w2, b2, res_scale):
        import jax, jax.numpy as jnp
        import numpy as np
        B, S, D, H, F, E = (2, 256, 256, 16, 512, 8)
        HD = D // H

        def _ln(x, g, b, eps=1e-05):
            m = x.mean(-1, keepdims=True)
            v = ((x - m) ** 2).mean(-1, keepdims=True)
            return (x - m) / jnp.sqrt(v + eps) * g + b
        b, s, d = src.shape
        h = scale_w.shape[0]
        hd = d // h
        q = (src @ q_w).reshape(b, s, h, hd).transpose(0, 2, 1, 3)
        k = (src @ k_w).reshape(b, s, h, hd).transpose(0, 2, 1, 3)
        v = (src @ v_w).reshape(b, s, h, hd).transpose(0, 2, 1, 3)
        scores = jnp.einsum('bhqd,bhkd->bhqk', q, k) / np.float32(np.sqrt(hd))
        scale = jax.nn.sigmoid(jnp.einsum('bhsd,hd->bhs', q, scale_w)) * 2.0
        scores = scores * scale[..., None]
        aw = jax.nn.softmax(scores, axis=-1)
        out = jnp.einsum('bhqk,bhkd->bhqd', aw, v).transpose(0, 2, 1, 3).reshape(b, s, d)
        gate = jax.nn.sigmoid(out @ gate_w + gate_b)
        attn = out * gate @ out_w
        x = _ln(src + attn, n1_g, n1_b)
        xr = x.reshape(-1, d)
        n = xr.shape[0]
        logits = xr @ moe_gate_w + moe_gate_b
        top_v, top_i = jax.lax.top_k(logits, 2)
        wts = jax.nn.softmax(top_v, axis=-1)
        chosen = jnp.max(top_i, axis=-1)

        def expert(W1, B1, G, Bt, W2, B2, rsc):
            hh = xr @ W1 + B1
            hh = jax.nn.gelu(_ln(hh, G, Bt), approximate=False)
            return (hh @ W2 + B2) * rsc + xr
        outs = jax.vmap(expert)(w1, b1, ln_g, ln_b, w2, b2, res_scale)
        sel = jnp.take_along_axis(outs.transpose(1, 0, 2), chosen[:, None, None], axis=1)[:, 0]
        moe = sel * jnp.sum(wts, axis=-1, keepdims=True)
        return _ln(x + moe.reshape(b, s, d), n2_g, n2_b)

    def _L1_attn_ref(x, w_qkv, w_out, b_out):
        import jax, jax.numpy as jnp
        import numpy as np
        D = 256
        H = 16
        HD = D // H
        R = HD
        N, T = (2, 512)
        W_LEFT, W_RIGHT = (127, 128)
        ROPE_BASE = 10000.0

        def _rope(x, cos, sin):
            x1 = x[..., :R // 2]
            x2 = x[..., R // 2:R]
            rot = jnp.concatenate([x1 * cos - x2 * sin, x2 * cos + x1 * sin], axis=-1)
            if R < x.shape[-1]:
                rot = jnp.concatenate([rot, x[..., R:]], axis=-1)
            return rot
        n, t, _ = x.shape
        qkv = (x @ w_qkv.T).reshape(n, t, 3, H, HD)
        q, k, v = (qkv[:, :, 0], qkv[:, :, 1], qkv[:, :, 2])
        pos = jnp.arange(t, dtype=jnp.float32)
        inv_freq = 1.0 / ROPE_BASE ** (jnp.arange(0, R, 2, dtype=jnp.float32) / R)
        freqs = pos[:, None] * inv_freq[None, :]
        cos = jnp.cos(freqs)[None, :, None, :]
        sin = jnp.sin(freqs)[None, :, None, :]
        q = _rope(q, cos, sin)
        k = _rope(k, cos, sin)
        i = jnp.arange(t)[:, None]
        j = jnp.arange(t)[None, :]
        band = (j >= i - W_LEFT) & (j <= i + W_RIGHT)
        bias = jnp.where(band, 0.0, -jnp.inf).astype(x.dtype)
        scale = np.float32(1.0 / np.sqrt(HD))
        scores = jnp.einsum('nthd,nshd->nhts', q, k) * scale + bias
        probs = jax.nn.softmax(scores, axis=-1)
        attn = jnp.einsum('nhts,nshd->nthd', probs, v).reshape(n, t, D)
        return attn @ w_out.T + b_out

    def _L1_xattn_ref(q, k, v, Wq, bq, Wk, bk, Wv, bv, Wo, bo):
        import jax, jax.numpy as jnp
        import numpy as np
        HEADS = 16
        D_MODEL = 256
        IMG_MODEL = 128
        D_K = D_MODEL // HEADS
        B, LQ, _ = q.shape
        LKV = k.shape[1]
        qh = (q @ Wq + bq).reshape(B, LQ, HEADS, D_K).transpose(0, 2, 1, 3)
        kh = (k @ Wk + bk).reshape(B, LKV, HEADS, D_K).transpose(0, 2, 1, 3)
        vh = (v @ Wv + bv).reshape(B, LKV, HEADS, D_K).transpose(0, 2, 1, 3)
        scale = 1.0 / np.sqrt(D_K)
        scores = jnp.einsum('bhqd,bhkd->bhqk', qh, kh) * scale
        attn = jax.nn.softmax(scores, axis=-1)
        out = jnp.einsum('bhqk,bhkd->bhqd', attn, vh)
        concat = out.transpose(0, 2, 1, 3).reshape(B, LQ, D_MODEL)
        return concat @ Wo + bo

    def _L1_ffn_ref(hidden_states, router_w, w_gate, w_up, w_down, ws_gate, ws_up, ws_down):
        import jax, jax.numpy as jnp
        import numpy as np
        TOP_K = 6

        def _glu_mlp(x, wg, wu, wd):
            return jax.nn.silu(x @ wg) * (x @ wu) @ wd
        B, S, D = hidden_states.shape
        x = hidden_states.reshape(-1, D)
        scores = jax.nn.softmax(x @ router_w, axis=-1)
        topk_w, topk_idx = jax.lax.top_k(scores, TOP_K)
        g = jnp.einsum('td,edf->etf', x, w_gate)
        u = jnp.einsum('td,edf->etf', x, w_up)
        f_all = jnp.einsum('etf,efd->ted', jax.nn.silu(g) * u, w_down)
        picked = jnp.take_along_axis(f_all, topk_idx[:, :, None], axis=1)
        y = jnp.sum(picked * topk_w[:, :, None], axis=1).reshape(B, S, D)
        y = y + _glu_mlp(hidden_states, ws_gate, ws_up, ws_down)
        return y
    x = _layernorm(x + _L0_attn_ref(x, L0_attn_w_attn, L0_attn_b_attn, L0_attn_w_proj, L0_attn_b_proj), axis=-1)
    x = _layernorm(x + _L0_xattn_ref(x, ctx_512, itok_BxS2xS_0_7, L0_xattn_proj_in, L0_xattn_proj_out), axis=-1)
    x = _layernorm(x + _L0_ffn_ref(x, L0_ffn_q_w, L0_ffn_k_w, L0_ffn_v_w, L0_ffn_out_w, L0_ffn_gate_w, L0_ffn_gate_b, L0_ffn_scale_w, L0_ffn_n1_g, L0_ffn_n1_b, L0_ffn_n2_g, L0_ffn_n2_b, L0_ffn_moe_gate_w, L0_ffn_moe_gate_b, L0_ffn_w1, L0_ffn_b1, L0_ffn_ln_g, L0_ffn_ln_b, L0_ffn_w2, L0_ffn_b2, L0_ffn_res_scale), axis=-1)
    x = _layernorm(x + _L1_attn_ref(x, L1_attn_w_qkv, L1_attn_w_out, L1_attn_b_out), axis=-1)
    x = _layernorm(x + _L1_xattn_ref(x, ctx_512, ctx_512, L1_xattn_Wq, L1_xattn_bq, L1_xattn_Wk, L1_xattn_bk, L1_xattn_Wv, L1_xattn_bv, L1_xattn_Wo, L1_xattn_bo), axis=-1)
    x = _layernorm(x + _L1_ffn_ref(x, L1_ffn_router_w, L1_ffn_w_gate, L1_ffn_w_up, L1_ffn_w_down, L1_ffn_ws_gate, L1_ffn_ws_up, L1_ffn_ws_down), axis=-1)
    return x

_drawn_inputs = setup_inputs


def setup_inputs(seed=0):
    import zlib

    import numpy as np

    out = dict(_drawn_inputs(seed))
    spreads = {'L0_attn_b_attn': (0.0, 0.1),
     'L0_attn_b_proj': (0.0, 0.1),
     'L0_ffn_n1_g': (1.0, 0.2),
     'L0_ffn_n1_b': (0.0, 0.1),
     'L0_ffn_n2_g': (1.0, 0.2),
     'L0_ffn_n2_b': (0.0, 0.1),
     'L0_ffn_moe_gate_b': (0.0, 0.1),
     'L0_ffn_b1': (0.0, 0.349),
     'L0_ffn_ln_g': (1.0, 0.6),
     'L0_ffn_ln_b': (0.0, 0.8),
     'L0_ffn_b2': (0.0, 0.304),
     'L0_ffn_res_scale': (1.0, 0.6),
     'L1_xattn_bq': (0.0, 0.8),
     'L1_xattn_bk': (0.0, 0.8),
     'L1_xattn_bv': (0.0, 0.1),
     'L1_xattn_bo': (0.0, 0.1)}
    factors = {'L0_ffn_q_w': 8.0,
     'L0_ffn_k_w': 8.0,
     'L0_ffn_v_w': 3.005,
     'L0_ffn_out_w': 2.832,
     'L0_ffn_gate_w': 8.0,
     'L0_ffn_gate_b': 8.0,
     'L0_ffn_scale_w': 8.0,
     'L1_attn_b_out': 3.65,
     'L1_xattn_Wq': 4.103,
     'L1_xattn_Wk': 4.053,
     'L1_ffn_router_w': 8.0,
     'L1_ffn_w_gate': 8.0,
     'L1_ffn_w_up': 8.0,
     'L1_ffn_w_down': 8.0,
     'L1_ffn_ws_gate': 3.263,
     'L1_ffn_ws_up': 3.382,
     'L1_ffn_ws_down': 3.45}
    for name, (base, spread) in spreads.items():
        noise = np.random.default_rng([zlib.crc32(name.encode()), seed]).standard_normal(out[name].shape)
        drawn = base * np.exp(spread * noise) if base else spread * noise
        out[name] = jnp.asarray(drawn.astype(out[name].dtype))
    for name, factor in factors.items():
        out[name] = (out[name] * factor).astype(out[name].dtype)
    return out
```

```python
from contextlib import ExitStack

import concourse.bass as bass
import concourse.mybir as mybir
import numpy as np

F32 = mybir.dt.float32
BF16 = mybir.dt.bfloat16
I32 = mybir.dt.int32
U32 = mybir.dt.uint32
ALU = mybir.AluOpType
ACT = mybir.ActivationFunctionType
AX = mybir.AxisListType

P = 128
NB = 16
D = 256
KT = D // P
H = 16
DK = D // H
HP = 32
HG = P // HP
NG = H // HG
E = 8
HID = 512
HC = HID // P
F1 = 128
GB = 4
NGR = NB // GB
TOK = NB * P
SLOTS = (TOK + E * (P - 1)) // P
UNITS = E + D // F1
ROW = 2 * D + 4
EPS = 1e-5
BIG = 1e30
CAUSAL, SCALED, ROTARY, CROSS = range(4)


class At:

    def __init__(self, stage, b, half, parity):
        self.b, self.n, self.half, self.p = b, b + NB * stage, half, parity
        self.nhalf = half + (NB // 2) * stage


def at(stage, b):
    return At(stage, b, b // 2, b % 2)


def wait(eng, sem, value):
    if isinstance(value, int) and value <= 0:
        return
    eng.wait_ge(sem, value)


def attention_steps(eng, stage, step):
    step(at(stage, 0), None)
    step(at(stage, 1), at(stage, 0))
    with eng.Fori(0, (NB - 2) // 2) as j:
        for u in range(2):
            step(At(stage, j * 2 + (2 + u), j + 1, u), At(stage, j * 2 + (1 + u), j + u, 1 - u))
    step(None, at(stage, NB - 1))


def program(nc, t, out):
    ctx = ExitStack()
    with ctx:
        def sb(name, shape, dt=F32):
            return ctx.enter_context(nc.sbuf_tensor(name, shape, dt))

        def sem(name):
            return ctx.enter_context(nc.semaphore(name))

        def dram(name, shape, dt=F32):
            return nc.dram_tensor(name, shape, dt).ap()

        x1 = dram("x1_dram", [NB, P, D])
        x2 = dram("x2_dram", [NB, P, D])
        xr = dram("xr_dram", [NB, P, D])
        x3_rows = dram("x3_dram", [TOK, D])
        x3 = x3_rows.rearrange("(b p) d -> b p d", p=P)
        routed = dram("routed_dram", [SLOTS * P, ROW])
        x4 = dram("x4_dram", [NB, P, D])
        x5 = dram("x5_dram", [NB, P, D])
        X_IN = [t["x"], x2, x3, x4]
        X_OUT = [x1, xr, x4, x5]

        bank = [ctx.enter_context(nc.psum_tensor(f"bank{i}", [P, 512], F32)) for i in range(8)]
        QKB, VB, OTB, TB = bank[0], bank[1], bank[2], bank[3]
        SB = [bank[4], bank[5]]
        STB = [bank[6], bank[7]]

        ident = sb("ident", [P, P])
        identb = sb("identb", [P, P], BF16)
        maskq = sb("maskq", [P, HG, P], BF16)
        maskk = sb("maskk", [P, HG, P], BF16)
        maskf = sb("maskf", [P, 2, P])
        minus_half = sb("minus_half", [P, 4])
        cosb = sb("cosb", [P, DK // 2])
        sinb = sb("sinb", [P, 2, DK // 2])
        wqkv = sb("wqkv", [P, 4, KT, 3 * D])
        wo = sb("wo", [P, 4, KT, D])
        gatew = sb("gatew", [P, KT, D])
        bqkv = sb("bqkv", [P, 2, 3 * D])
        bout = sb("bout", [P, 4, D])
        scalew = sb("scalew", [P, D])
        gateb = sb("gateb", [P, D])
        n1g = sb("n1g", [P, D])
        n1b = sb("n1b", [P, D])

        wa = sb("wa", [P, KT, E, HID])
        wb = sb("wb", [P, E, HC, D])
        w7g = sb("w7g", [P, KT, UNITS, F1])
        w7u = sb("w7u", [P, KT, UNITS, F1])
        w7d = sb("w7d", [P, UNITS, D])
        w7r = sb("w7r", [P, KT, E])
        wlog = sb("wlog", [P, KT, E])
        blog = sb("blog", [P, E])
        n2g = sb("n2g", [P, D])
        n2b = sb("n2b", [P, D])
        ones = sb("ones", [P, P])
        lower = sb("lower", [P, P])
        ascend = sb("ascend", [P, E])
        descend = sb("descend", [P, E])
        iotas = sb("iotas", [P, E, NB])
        slotn = sb("slotn", [P, SLOTS, E])
        keepmask = sb("keepmask", [P, E, NB])

        loaded = sem("loaded_constants")
        init = sem("init")
        x_loaded = [sem(f"x_loaded_{i}") for i in range(2)]
        x_stored = [sem(f"x_stored_{i}") for i in range(2)]
        xT_made = sem("xT_made")
        qkv_made = sem("qkv_made")
        qkT_made = sem("qkT_made")
        s_made = sem("s_made")
        q2T_made = sem("q2T_made")
        st_made = sem("st_made")
        av_made = sem("av_made")
        o_made = sem("o_made")
        attT_made = sem("attT_made")
        proj_made = sem("proj_made")
        xT_kept = sem("xT_kept")
        probs_kept = sem("probs_kept")
        qT_kept = sem("qT_kept")
        kT_kept = sem("kT_kept")
        oT_kept = sem("oT_kept")
        attT_kept = sem("attT_kept")
        q2T_kept = sem("q2T_kept")
        qk_kept = sem("qk_kept")
        v_kept = sem("v_kept")
        max_kept = sem("max_kept")
        rden_done = sem("rden_done")
        att_kept = sem("att_kept")
        res_done = sem("res_done")
        ln_step = sem("ln_step")
        ln_done = sem("ln_done")
        xb_done = sem("xb_done")
        rstd_done = sem("rstd_done")
        passed = sem("passed")
        lin_step = sem("lin_step")
        tanh_done = sem("tanh_done")
        fac_done = sem("fac_done")
        gate_made = sem("gate_made")
        gz_done = sem("gz_done")
        gth_done = sem("gth_done")
        gated_done = sem("gated_done")
        gatedT_made = sem("gatedT_made")
        gatedT_kept = sem("gatedT_kept")
        n1_step = sem("n1_step")
        big_loaded = sem("big_loaded")
        e_loaded = sem("e_loaded")
        e_stored = sem("e_stored")
        e_xT_made = sem("e_xT_made")
        e_gate_made = sem("e_gate_made")
        e_z_made = sem("e_z_made")
        e_o_made = sem("e_o_made")
        e_xT_kept = sem("e_xT_kept")
        e_gate_kept = sem("e_gate_kept")
        e_masked = sem("e_masked")
        e_hid = sem("e_hid")
        e_res = sem("e_res")
        e_ln = sem("e_ln")
        e_xres = sem("e_xres")
        e_rstd = sem("e_rstd")
        e_done = sem("e_done")
        r_loaded = [sem(f"r_loaded_{i}") for i in range(2)]
        r_xT_made = sem("r_xT_made")
        r_xT_kept = sem("r_xT_kept")
        r_logit_made = sem("r_logit_made")
        r_logit_kept = sem("r_logit_kept")
        r_step = sem("r_step")
        r_exp = sem("r_exp")
        r_rank = sem("r_rank")
        r_meta = sem("r_meta")
        filled = sem("filled")
        row_loaded = [sem(f"row_loaded_{i}") for i in range(2)]
        row_meta = sem("row_meta")
        row_sent = [sem(f"row_sent_{i}") for i in range(2)]
        t_loaded = [sem(f"t_loaded_{i}") for i in range(4)]
        t_sent = [sem(f"t_sent_{i}") for i in range(4)]
        t_xT_made = sem("t_xT_made")
        t_h_made = sem("t_h_made")
        t_hT_made = sem("t_hT_made")
        t_o_made = sem("t_o_made")
        t_xT_kept = sem("t_xT_kept")
        t_gelu = sem("t_gelu")
        t_h = sem("t_h")
        t_hn = sem("t_hn")
        t_y = sem("t_y")
        t_w = sem("t_w")
        t_z = sem("t_z")
        t_xb = sem("t_xb")
        t_rstd = sem("t_rstd")
        t_rstd2 = sem("t_rstd2")
        f_loaded = sem("f_loaded")
        f_stored = sem("f_stored")
        f_xT_made = sem("f_xT_made")
        f_logit_made = sem("f_logit_made")
        f_gate_made = sem("f_gate_made")
        f_up_made = sem("f_up_made")
        f_wB_made = sem("f_wB_made")
        f_o_made = sem("f_o_made")
        f_xT_kept = sem("f_xT_kept")
        f_exp = sem("f_exp")
        f_silu = sem("f_silu")
        f_wB_kept = sem("f_wB_kept")
        f_step = sem("f_step")
        f_keep = sem("f_keep")
        f_prod = sem("f_prod")
        f_hid = sem("f_hid")
        f_res = sem("f_res")
        f_ln = sem("f_ln")
        f_done = sem("f_done")
        f_xres = sem("f_xres")
        f_rstd = sem("f_rstd")
        rope_step = sem("rope_step")

        consts = [(ident, t["ident"]), (maskf[:, 0], t["maskq"]), (maskf[:, 1], t["maskk"]),
                  (cosb, t["cos"]), (sinb, t["sin"]), (wqkv, t["wqkv"]), (wo, t["wo"]), (gatew, t["gatew"]),
                  (wlog, t["wlog"]), (w7r, t["w7r"]), (ones, t["ones"]), (lower, t["lower"])]
        big = [(wa, t["wa0"]), (wb, t["wb0"]), (w7g, t["w7g"]), (w7u, t["w7u"]), (w7d, t["w7d"])]
        rows = [(bqkv[:, 0, :], t["b_qkv0"]), (bqkv[:, 1, :], t["b_qkv3"]), (bout[:, 0, :], t["b_o0"]),
                (bout[:, 2, :], t["b_o2"]), (bout[:, 3, :], t["b_o3"]), (scalew[:], t["scale_w"]),
                (gateb[:], t["gate_b"]), (n1g[:], t["n1_g"]), (n1b[:], t["n1_b"]),
                (n2g[:], t["n2_g"]), (n2b[:], t["n2_b"]), (blog[:], t["b_log"]), (descend[:], t["descend"]), (ascend[:], t["ascend"]),
                (iotas[:].rearrange("p e b -> p (e b)"), t["iotas"]), (slotn[:].rearrange("p s e -> p (s e)"), t["slotn"]),
                (keepmask[:].rearrange("p e b -> p (e b)"), t["keepmask"])]
        LOADED = 16 * (len(consts) + len(rows))

        with nc.Block() as block:
            @block.sync
            def _(sp):
                for dst, src in consts:
                    sp.dma_start(dst[:], src).then_inc(loaded, 16)
                for dst, src in rows:
                    sp.dma_start(dst, src.partition_broadcast(P)).then_inc(loaded, 16)
                sp.wait_ge(loaded, LOADED)

            @block.vector
            def _(dve):
                dve.wait_ge(loaded, LOADED)
                dve.tensor_copy(identb[:], ident[:])
                for mask, i in ((maskq, 0), (maskk, 1)):
                    dve.tensor_copy(mask[:], maskf[:, i, :].unsqueeze(1).broadcast_to([P, HG, P]))

            @block.gpsimd
            def _(pool):
                pool.memset(minus_half[:], -0.5).then_inc(init, 1)
                pool.memset(bout[:, 1, :], 0.0).then_inc(init, 1)
                pool.wait_ge(init, 2)
                for s_, credit in ((e_xres, 1), (e_xT_made, KT), (e_masked, E), (e_res, GB), (e_done, GB), (e_stored, 16),
                                   (e_gate_kept, 1), (e_xT_kept, 1), (e_hid, 5), (e_o_made, 2), (e_gate_made, 2),
                                   (r_xT_kept, 1), (r_logit_kept, 1), (r_logit_made, 2),
                                   (f_xres, 1), (f_xT_made, KT), (f_res, GB), (f_done, GB), (f_stored, 16), (f_xT_kept, 1), (f_wB_kept, 1),
                                   (f_silu, 1), (f_hid, 3), (f_o_made, 2), (f_logit_made, 1), (f_wB_made, 1), (f_exp, 1)):
                    pool.sem_inc(s_, credit)

        def attention(stage, prefetch):
            scope = ExitStack()

            def sb(name, shape, dt=F32):
                return scope.enter_context(nc.sbuf_tensor(f"{name}_{stage}", shape, dt))

            x = [sb(f"x_{i}", [P, D]) for i in range(2)]
            cx = [sb(f"cx_{i}", [P, P]) for i in range(2)]
            xb = [sb(f"xb_{i}", [P, D]) for i in range(2)]
            xT = sb("xT", [P, KT + 1, P])
            qk = sb("qk", [P, 2, H, HP])
            v = [sb(f"v_{i}", [P, H, HP]) for i in range(2)]
            qT = sb("qT", [P, NG, P])
            kT = [sb(f"kT_{i}", [P, NG, P]) for i in range(2)]
            q2T = sb("q2T", [P, NG, P])
            probs = [sb(f"probs_{i}", [P, HG, P]) for i in range(2)]
            oT = sb("oT", [P, NG, P])
            rden = sb("rden", [P, H])
            att = sb("att", [P, D])
            attT = sb("attT", [P, KT, P])
            y = sb("y", [P, D])
            stats = sb("stats", [P, 6])
            mv = sb("mv", [P, 2])
            var = sb("var", [P, 1])
            rstd = sb("rstd", [P, 1])
            xo = [sb(f"xo_{i}", [P, D]) for i in range(2)]
            tmpa = sb("tmpa", [P, 2 * D])
            tmpb = sb("tmpb", [P, 2 * D])
            lin = sb("lin", [P, H])
            tanh_q = sb("tanh_q", [P, H])
            fac = sb("fac", [P, H])
            gz = sb("gz", [P, D])
            gth = sb("gth", [P, D])
            gated = sb("gated", [P, D])

            with nc.Block() as block:
                @block.gpsimd
                def _(pool):
                    pool.memset(qk[:], 0.0).then_inc(init, 1)
                    for i in range(2):
                        pool.memset(v[i][:], 0.0).then_inc(init, 1)
                    pool.wait_ge(init, 6 * stage + 5)
                    pool.memset(qk[:, 1, :, DK:DK + 1], 1.0).then_inc(init, 1)
                    for i in range(2):
                        pool.memset(v[i][:, :, DK:DK + 1], 1.0).then_inc(init, 1)
                    pool.wait_ge(init, 6 * stage + 8)

            def attention_sp(sp, stage):
                src, dst = X_IN[stage], X_OUT[stage]

                def load(a):
                    wait(sp, xT_made, a.n - 1)
                    wait(sp, xb_done, a.n - 1)
                    sp.dma_start(x[a.p][:], src[bass.ds(a.b, 1)].rearrange("a p n -> (a p) n")).then_inc(x_loaded[a.p], 16)
                    if stage == CROSS:
                        sp.dma_start(cx[a.p][:], t["ctx"][bass.ds(a.b, 1)].rearrange("a p n -> (a p) n")).then_inc(x_loaded[a.p], 16)

                def store(a):
                    sp.wait_ge(ln_done, a.n + 1)
                    sp.dma_start(dst[bass.ds(a.b, 1)].rearrange("a p n -> (a p) n"), xo[a.p][:]).then_inc(x_stored[a.p], 16)

                load(at(stage, 0))
                load(at(stage, 1))
                with sp.Fori(0, (NB - 2) // 2) as j:
                    for u in range(2):
                        load(At(stage, j * 2 + (2 + u), j + 1, u))
                        store(At(stage, j * 2 + u, j, u))
                store(at(stage, NB - 2))
                store(at(stage, NB - 1))
                for i in range(2):
                    sp.wait_ge(x_stored[i], 16 * (NB // 2) * (stage + 1))

            def x_count(a, stage):
                return (a.half + 1) * (32 if stage == CROSS else 16) + 16 * (NB // 2) * stage

            def attention_pe(pe, stage):
                def transposes(dst, src_of, n, inc):
                    for k in range(n):
                        ins = pe.transpose(dst[:, k * P:(k + 1) * P], src_of(k), ident[:])
                    ins.then_inc(inc, 1)

                def step(a, c):
                    if a:
                        pe.wait_ge(x_loaded[a.p], x_count(a, stage))
                        wait(pe, kT_kept, a.n)
                        if stage == CROSS:
                            pe.transpose(VB[:, KT * P:(KT + 1) * P], cx[a.p][:], ident[:])
                        transposes(VB, lambda k: x[a.p][:, k * P:(k + 1) * P], KT, xT_made)
                    if c:
                        scores_less_max(c, 0)
                        scores_less_max(c, 1)
                    if a:
                        pe.wait_ge(xT_kept, a.n + 1)
                        wait(pe, q2T_kept, a.n)
                        if stage == CROSS:
                            for k in range(KT):
                                pe.matmul(QKB[:, 0:D], xT[:, k, :], wqkv[:, stage, k, 0:D], start=k == 0, stop=k == KT - 1)
                            pe.matmul(QKB[:, D:2 * D], xT[:, KT, :], wqkv[:, stage, 0, D:2 * D], start=True, stop=True).then_inc(qkv_made, 1)
                            pe.matmul(VB[:, 0:D], xT[:, KT, :], wqkv[:, stage, 0, 2 * D:3 * D], start=True, stop=True).then_inc(qkv_made, 1)
                        else:
                            for k in range(KT):
                                ins = pe.matmul(QKB[:], xT[:, k, :], wqkv[:, stage, k, 0:2 * D], start=k == 0, stop=k == KT - 1)
                            ins.then_inc(qkv_made, 1)
                            for k in range(KT):
                                ins = pe.matmul(VB[:, 0:D], xT[:, k, :], wqkv[:, stage, k, 2 * D:3 * D], start=k == 0, stop=k == KT - 1)
                            ins.then_inc(qkv_made, 1)
                    if c:
                        weighted_values(c, 0)
                        scores_less_max(c, 2)
                        weighted_values(c, 1)
                        scores_less_max(c, 3)
                    if a:
                        pe.wait_ge(qk_kept, a.n + 1)
                        transposes(QKB, lambda k: qk[:, 0, HG * k:HG * (k + 1), :], NG, qkT_made)
                        pe.wait_ge(v_kept, a.n + 1)
                        transposes(VB, lambda k: qk[:, 1, HG * k:HG * (k + 1), :], NG, qkT_made)
                    if c:
                        weighted_values(c, 2)
                        weighted_values(c, 3)
                    if a:
                        scores(a, 0)
                        scores(a, 1)
                    if c:
                        pe.wait_ge(oT_kept, c.n + 1)
                        wait(pe, attT_kept, c.n)
                        if stage == SCALED:
                            wait(pe, gatedT_kept, c.b)
                        transposes(TB, lambda k: oT[:, k, :], NG, o_made)
                    if a:
                        scores(a, 2)
                        scores(a, 3)
                    if c:
                        pe.wait_ge(att_kept, c.n + 1)
                        transposes(TB, lambda k: att[:, k * P:(k + 1) * P], KT, attT_made)
                    if a:
                        pe.wait_ge(max_kept, 4 * a.n + 4)
                        pe.wait_ge(qT_kept, a.n + 1)
                        transposes(QKB, lambda k: qk[:, 0, HG * k:HG * (k + 1), :], NG, q2T_made)
                    if c:
                        pe.wait_ge(attT_kept, c.n + 1)
                        if stage == SCALED:
                            for k in range(KT):
                                ins = pe.matmul(OTB[:, 0:D], attT[:, k, :], gatew[:, k, :], start=k == 0, stop=k == KT - 1)
                            ins.then_inc(gate_made, 1)
                            pe.wait_ge(gated_done, c.b + 1)
                            transposes(TB, lambda k: gated[:, k * P:(k + 1) * P], KT, gatedT_made)
                            pe.wait_ge(gatedT_kept, c.b + 1)
                        for k in range(KT):
                            ins = pe.matmul(OTB[:, 0:D], attT[:, k, :], wo[:, stage, k, :], start=k == 0, stop=k == KT - 1)
                        ins.then_inc(proj_made, 1)

                def scores(a, r):
                    if r == 0:
                        pe.wait_ge(qT_kept, a.n + 1)
                        pe.wait_ge(kT_kept, a.n + 1)
                    wait(pe, max_kept, 4 * a.n + r - 1)
                    s = SB[r % 2]
                    if stage == CAUSAL:
                        pe.matmul(s[:], identb[:], maskq[:], start=True, stop=True)
                    rows = slice(HP * r, HP * r + DK)
                    for g in range(NG):
                        ins = pe.matmul(s[:, g * P:(g + 1) * P], qT[rows, g, :], kT[a.p][rows, g, :], start=stage != CAUSAL,
                                        stop=True, skip_group_check=True)
                    ins.then_inc(s_made, 1)

                def scores_less_max(c, r):
                    if r == 0:
                        pe.wait_ge(q2T_kept, c.n + 1)
                        pe.wait_ge(kT_kept, c.n + 1)
                    wait(pe, probs_kept, 4 * c.n + r - 1)
                    s = STB[r % 2]
                    if stage == CAUSAL:
                        pe.matmul(s[:], identb[:], maskk[:], start=True, stop=True)
                    rows = slice(HP * r, HP * r + DK + 1)
                    for g in range(NG):
                        ins = pe.matmul(s[:, g * P:(g + 1) * P], kT[c.p][rows, g, :], q2T[rows, g, :], start=stage != CAUSAL,
                                        stop=True, skip_group_check=True)
                    ins.then_inc(st_made, 1)

                def weighted_values(c, r):
                    if r == 0:
                        wait(pe, res_done, c.n)
                        pe.wait_ge(v_kept, c.n + 1)
                    pe.wait_ge(probs_kept, 4 * c.n + r + 1)
                    for g in range(NG):
                        ins = pe.matmul(OTB[HP * g:HP * (g + 1), r * P:(r + 1) * P], v[c.p][:, HG * g + r, :],
                                        probs[r % 2][:, g, :], start=True, stop=True, skip_group_check=True)
                    ins.then_inc(av_made, 1)

                attention_steps(pe, stage, step)

            def attention_act(act, stage):
                def step(a, c):
                    if a:
                        act.wait_ge(xT_made, a.n + 1)
                        wait(act, qkv_made, 2 * a.n)
                        n = KT + 1 if stage == CROSS else KT
                        act.copy(xT[:, 0:n, :], VB[:, 0:n * P]).then_inc(xT_kept, 1)
                    if stage == SCALED and a:
                        act.wait_ge(lin_step, 2 * a.b + 2)
                        wait(act, fac_done, a.b)
                        act.activation(tanh_q[:], lin[:], ACT.Tanh, scale=0.5).then_inc(tanh_done, 1)
                    if c:
                        for g in range(NG):
                            act.wait_ge(st_made, 4 * c.n + g + 1)
                            wait(act, av_made, 4 * c.n + g - 1)
                            act.activation(probs[g % 2][:], STB[g % 2][:], ACT.Exp, scale=float(DK) ** -0.5).then_inc(probs_kept, 1)
                    if a:
                        act.wait_ge(qkT_made, 2 * a.n + 1)
                        wait(act, s_made, 4 * a.n)
                        act.copy(qT[:], QKB[:]).then_inc(qT_kept, 1)
                        act.wait_ge(qkT_made, 2 * a.n + 2)
                        wait(act, st_made, 4 * a.n - 4)
                        act.copy(kT[a.p][:], VB[:]).then_inc(kT_kept, 1)
                    if c:
                        act.wait_ge(av_made, 4 * c.n + 4)
                        wait(act, o_made, c.n)
                        act.copy(oT[:], OTB[:]).then_inc(oT_kept, 1)
                        act.wait_ge(attT_made, c.n + 1)
                        wait(act, proj_made, c.n)
                        act.copy(attT[:], TB[:, 0:D]).then_inc(attT_kept, 1)
                    if a:
                        act.wait_ge(q2T_made, a.n + 1)
                        wait(act, st_made, 4 * a.n)
                        act.copy(q2T[:], QKB[:]).then_inc(q2T_kept, 1)
                    if c and stage == SCALED:
                        act.wait_ge(gz_done, c.b + 1)
                        wait(act, gated_done, c.b)
                        act.activation(gth[:], gz[:], ACT.Tanh, scale=0.5).then_inc(gth_done, 1)
                        act.wait_ge(gatedT_made, c.b + 1)
                        act.mul(attT[:], TB[:, 0:D], 0.5).then_inc(gatedT_kept, 1)

                attention_steps(act, stage, step)

            def attention_dve(dve, stage):
                def step(a, c):
                    if a:
                        dve.wait_ge(qkv_made, 2 * a.n + 1)
                        wait(dve, q2T_made, a.n)
                        heads = qk[:, :, :, 0:DK]
                        made = QKB[:].rearrange("p (a h d) -> p a h d", a=2, h=H)
                        if stage == CAUSAL or stage == CROSS:
                            bias = bqkv[:, 0 if stage == CAUSAL else 1, 0:2 * D].rearrange("p (a h d) -> p a h d", a=2, h=H)
                            dve.tensor_tensor(heads, made, bias, ALU.add).then_inc(qk_kept, 1)
                        if stage == SCALED:
                            dve.tensor_tensor(tmpa[:, 0:D], QKB[:, 0:D], scalew[:], ALU.mult).then_inc(lin_step, 1)
                            dve.wait_ge(lin_step, 2 * a.b + 1)
                            dve.tensor_reduce(lin[:], tmpa[:, 0:D].rearrange("p (h d) -> p h d", h=H), AX.X, ALU.add).then_inc(lin_step, 1)
                            dve.tensor_copy(qk[:, 1, :, 0:DK], QKB[:, D:2 * D].rearrange("p (h d) -> p h d", h=H))
                            dve.wait_ge(tanh_done, a.b + 1)
                            dve.tensor_scalar(fac[:], tanh_q[:], 1.0, None, ALU.add).then_inc(fac_done, 1)
                            dve.wait_ge(fac_done, a.b + 1)
                            dve.tensor_tensor(qk[:, 0, :, 0:DK], QKB[:, 0:D].rearrange("p (h d) -> p h d", h=H),
                                              fac[:].unsqueeze(2).broadcast_to([P, H, DK]), ALU.mult).then_inc(qk_kept, 1)
                        if stage == ROTARY:
                            made4 = QKB[:].rearrange("p (h c d) -> p h c d", h=2 * H, c=2)
                            ta = tmpa[:].rearrange("p (h c d) -> p h c d", h=2 * H, c=2)
                            tb = tmpb[:].rearrange("p (h c d) -> p h c d", h=2 * H, c=2)
                            half = DK // 2
                            dve.tensor_tensor(tmpa[:].rearrange("p (h d) -> p h d", d=half), QKB[:].rearrange("p (h d) -> p h d", d=half),
                                              cosb[:].unsqueeze(1).broadcast_to([P, 4 * H, half]), ALU.mult).then_inc(rope_step, 1)
                            for i in range(2):
                                dve.tensor_tensor(tb[:, :, i, :], made4[:, :, 1 - i, :],
                                                  sinb[:, i, :].unsqueeze(1).broadcast_to([P, 2 * H, half]), ALU.mult).then_inc(rope_step, 1)
                            dve.wait_ge(rope_step, 3 * a.b + 3)
                            dve.tensor_tensor(qk[:].rearrange("p a h d -> p (a h) d")[:, :, 0:DK], tmpa[:].rearrange("p (h d) -> p h d", d=DK),
                                              tmpb[:].rearrange("p (h d) -> p h d", d=DK), ALU.add).then_inc(qk_kept, 1)
                        dve.wait_ge(qkv_made, 2 * a.n + 2)
                        wait(dve, av_made, 4 * a.n - 4)
                        made = VB[:, 0:D].rearrange("p (h d) -> p h d", h=H)
                        if stage == CAUSAL or stage == CROSS:
                            bias = bqkv[:, 0 if stage == CAUSAL else 1, 2 * D:3 * D].rearrange("p (h d) -> p h d", h=H)
                            dve.tensor_tensor(v[a.p][:, :, 0:DK], made, bias, ALU.add).then_inc(v_kept, 1)
                        else:
                            dve.tensor_copy(v[a.p][:, :, 0:DK], made).then_inc(v_kept, 1)
                        row_max(a, 0)
                        row_max(a, 1)
                    if c:
                        dve.wait_ge(o_made, c.n + 1)
                        made = TB[:].rearrange("p (r g d) -> p g r d", r=HG, g=NG)
                        wait(dve, att_kept, c.n)
                        dve.reciprocal(rden[:].rearrange("p (g r) -> p g r", r=HG), made[:, :, :, DK]).then_inc(rden_done, 1)
                        dve.wait_ge(rden_done, c.n + 1)
                        wait(dve, attT_made, c.n)
                        dve.tensor_tensor(att[:].rearrange("p (g r d) -> p g r d", g=NG, r=HG), made[:, :, :, 0:DK],
                                          rden[:].rearrange("p (g r) -> p g r", r=HG).unsqueeze(3).broadcast_to([P, NG, HG, DK]), ALU.mult).then_inc(att_kept, 1)
                    if a:
                        row_max(a, 2)
                        row_max(a, 3)
                    if c:
                        if stage == SCALED:
                            dve.wait_ge(gate_made, c.b + 1)
                            dve.tensor_tensor(gz[:], OTB[:, 0:D], gateb[:], ALU.add).then_inc(gz_done, 1)
                            dve.wait_ge(gth_done, c.b + 1)
                            dve.scalar_tensor_tensor(gated[:], gth[:], 1.0, att[:], ALU.add, ALU.mult).then_inc(gated_done, 1)
                        dve.wait_ge(proj_made, c.n + 1)
                        dve.wait_ge(xb_done, c.n + 1)
                        dve.tensor_tensor(y[:], OTB[:, 0:D], xb[c.p][:], ALU.add).then_inc(res_done, 1)
                        dve.wait_ge(res_done, c.n + 1)
                        dve.bn_stats(stats[:], y[:]).then_inc(ln_step, 1)
                        dve.wait_ge(ln_step, 3 * c.n + 1)
                        dve.sem_inc(passed, 1)
                        dve.bn_aggr(mv[:], stats[:]).then_inc(ln_step, 1)
                        dve.wait_ge(ln_step, 3 * c.n + 2)
                        dve.tensor_scalar(var[:], mv[:, 1:2], EPS, None, ALU.add).then_inc(ln_step, 1)
                        dve.wait_ge(rstd_done, c.n + 1)
                        stored = c.half * 16 + 16 * (NB // 2) * stage
                        wait(dve, x_stored[c.p], stored)
                        if stage == SCALED:
                            dve.tensor_scalar(tmpb[:, 0:D], y[:], mv[:, 0:1], rstd[:], ALU.subtract, ALU.mult).then_inc(n1_step, 1)
                            dve.wait_ge(n1_step, 2 * c.b + 1)
                            dve.tensor_tensor(tmpb[:, D:2 * D], tmpb[:, 0:D], n1g[:], ALU.mult).then_inc(n1_step, 1)
                            dve.wait_ge(n1_step, 2 * c.b + 2)
                            dve.tensor_tensor(xo[c.p][:], tmpb[:, D:2 * D], n1b[:], ALU.add).then_inc(ln_done, 1)
                        else:
                            dve.tensor_scalar(xo[c.p][:], y[:], mv[:, 0:1], rstd[:], ALU.subtract, ALU.mult).then_inc(ln_done, 1)

                def row_max(a, r):
                    dve.wait_ge(s_made, 4 * a.n + r + 1)
                    dve.tensor_reduce(qk[:, 0, :, DK].rearrange("p (g r) -> p g r", r=HG)[:, :, r], SB[r % 2][:].rearrange("p (g k) -> p g k", g=NG),
                                      AX.X, ALU.max, negate=True).then_inc(max_kept, 1)

                attention_steps(dve, stage, step)

            def attention_pool(pool, stage):
                def step(a, c):
                    if a:
                        pool.wait_ge(x_loaded[a.p], x_count(a, stage))
                        wait(pool, res_done, a.n - 1)
                        pool.tensor_tensor(xb[a.p][:], x[a.p][:], bout[:, stage, :], ALU.add).then_inc(xb_done, 1)
                    if c:
                        pool.wait_ge(ln_step, 3 * c.n + 3)
                        wait(pool, ln_done, c.n)
                        pool.tensor_tensor(rstd[:], var[:], minus_half[:, 0:1], ALU.pow).then_inc(rstd_done, 1)

                attention_steps(pool, stage, step)

            with nc.Block() as block:
                @block.sync
                def _(sp):
                    attention_sp(sp, stage)

                @block.tensor
                def _(pe):
                    attention_pe(pe, stage)

                @block.scalar
                def _(act):
                    for dst, src in prefetch:
                        act.dma_start(dst[:], src).then_inc(big_loaded, 16)
                    attention_act(act, stage)

                @block.vector
                def _(dve):
                    attention_dve(dve, stage)

                @block.gpsimd
                def _(pool):
                    attention_pool(pool, stage)

            scope.close()

        R_ONEHOT, R_DIFF = 12, 13
        MASK_C, GATE_C, HID_C, O_C = 2, 1, 5, 2

        def experts0():
            scope = ExitStack()

            def sb(name, shape, dt=F32):
                return scope.enter_context(nc.sbuf_tensor(name, shape, dt))

            xg = sb("xg", [P, GB, D])
            xres = sb("xres", [P, GB, D])
            xgT = sb("xgT", [P, KT, GB * P])
            ctxg = sb("ctxg", [P, GB, P])
            itokg = sb("itokg", [P, GB, P], I32)
            masked = [sb(f"masked_{i}", [P, GB * P]) for i in range(2)]
            gateB = [sb(f"gateB_{i}", [P, GB * P]) for i in range(2)]
            hid = [sb(f"hid_{i}", [P, HC, GB * P]) for i in range(2)]
            yg = sb("yg", [P, GB, D])
            xog = sb("xog", [P, GB, D])
            stg = sb("stg", [P, GB, 6])
            mvg = sb("mvg", [P, GB, 2])
            varg = sb("varg", [P, GB])
            rstdg = sb("rstdg", [P, GB])

            def group(ap, g):
                return ap[bass.ds(g * GB, GB)].rearrange("b p n -> p b n")

            with nc.Block() as block:
                @block.sync
                def _(sp):
                    def load(g):
                        sp.wait_ge(e_xres, g + 1)
                        sp.wait_ge(e_xT_made, g * KT + KT)
                        sp.dma_start(xg[:], group(x1, g)).then_inc(e_loaded, 16)
                        sp.wait_ge(e_masked, g * E + E)
                        sp.dma_start(ctxg[:], group(t["ctx"], g)).then_inc(e_loaded, 16)
                        sp.dma_start(itokg[:], group(t["itok"], g)).then_inc(e_loaded, 16)

                    def store(g):
                        sp.wait_ge(e_done, g * GB + 2 * GB)
                        sp.dma_start(group(x2, g), xog[:]).then_inc(e_stored, 16)

                    load(0)
                    with sp.Fori(0, NGR - 1) as g:
                        load(g + 1)
                        store(g)
                    store(NGR - 1)
                    sp.wait_ge(e_stored, 16 * (NGR + 1))

                @block.gpsimd
                def _(pool):
                    with pool.Fori(0, NGR) as g:
                        pool.wait_ge(e_loaded, g * 48 + 48)
                        pool.wait_ge(e_res, g * GB + GB)
                        pool.sem_inc(passed, 1)
                        pool.tensor_copy(xres[:], xg[:]).then_inc(e_xres, 1)
                        pool.wait_ge(e_ln, g * 6 + 6)
                        pool.wait_ge(e_done, g * GB + GB)
                        pool.tensor_tensor(rstdg[:], varg[:], minus_half[:], ALU.pow).then_inc(e_rstd, 1)

                @block.tensor
                def _(pe):
                    pe.wait_ge(big_loaded, 16 * len(big))
                    with pe.Fori(0, NGR) as g:
                        def gates(e):
                            pe.wait_ge(e_masked, g * E + (E + e + 1))
                            pe.wait_ge(e_gate_kept, g * E + (e + 1))
                            pe.matmul(bank[6][:], ones[:], masked[e % 2][:], start=True, stop=True).then_inc(e_gate_made, 1)

                        def first(e):
                            for c in range(HC):
                                z = bank[4 + c % 2]
                                pe.wait_ge(e_hid, g * (E * HC) + (e * HC + c - 1 + HID_C))
                                for k in range(KT):
                                    ins = pe.matmul(z[:], wa[:, k, e, c * P:(c + 1) * P], xgT[:, k, :], start=k == 0, stop=k == KT - 1)
                                ins.then_inc(e_z_made, 1)

                        def second(e):
                            if e == 0:
                                pe.wait_ge(e_res, g * GB + GB)
                            pe.wait_ge(e_hid, g * (E * HC) + (e * HC + HC + HID_C))
                            for b in range(GB):
                                for c in range(HC):
                                    ins = pe.matmul(bank[b][:, 0:D], hid[e % 2][:, c, b * P:(b + 1) * P], wb[:, e, c, :],
                                                    start=e == 0 and c == 0, stop=e == E - 1 and c == HC - 1)
                            ins.then_inc(e_o_made, 1)

                        pe.wait_ge(e_loaded, g * 48 + 48)
                        for k in range(KT):
                            pe.wait_ge(e_xT_kept, g * KT + (k + 1))
                            for b in range(GB):
                                ins = pe.transpose(bank[7][:, b * P:(b + 1) * P], xg[:, b, k * P:(k + 1) * P], ident[:])
                            ins.then_inc(e_xT_made, 1)
                        gates(0)
                        pe.wait_ge(e_xT_kept, g * KT + (KT + 1))
                        for e in range(E):
                            first(e)
                            if e + 1 < E:
                                gates(e + 1)
                            if e:
                                second(e - 1)
                        second(E - 1)

                @block.scalar
                def _(act):
                    with act.Fori(0, NGR) as g:
                        for k in range(KT):
                            act.wait_ge(e_xT_made, g * KT + (k + 1 + KT))
                            act.wait_ge(e_o_made, g * E + O_C)
                            act.copy(xgT[:, k, :], bank[7][:]).then_inc(e_xT_kept, 1)
                        for e in range(E):
                            act.wait_ge(e_gate_made, g * E + (e + 1 + MASK_C))
                            act.wait_ge(e_hid, g * (E * HC) + (e * HC - HC + HID_C))
                            act.copy(gateB[e % 2][:], bank[6][:]).then_inc(e_gate_kept, 1)

                @block.vector
                def _(dve):
                    with dve.Fori(0, NGR) as g:
                        def mask(e):
                            if e == 0:
                                dve.wait_ge(e_loaded, g * 48 + 48)
                            dve.wait_ge(e_gate_made, g * E + (e - 1 + MASK_C))
                            dve.scalar_tensor_tensor(masked[e % 2][:], itokg[:].rearrange("p b s -> p (b s)"), float(e),
                                                     ctxg[:].rearrange("p b s -> p (b s)"), ALU.is_equal, ALU.mult).then_inc(e_masked, 1)

                        mask(0)
                        mask(1)
                        for e in range(E):
                            dve.wait_ge(e_gate_kept, g * E + (e + 1 + GATE_C))
                            dve.wait_ge(e_o_made, g * E + (e - 1 + O_C))
                            for c in range(HC):
                                dve.wait_ge(e_z_made, g * (E * HC) + (e * HC + c + 1))
                                dve.scalar_tensor_tensor(hid[e % 2][:, c, :], bank[4 + c % 2][:], 0.0, gateB[e % 2][:],
                                                         ALU.max, ALU.mult).then_inc(e_hid, 1)
                            if e + 2 < E:
                                mask(e + 2)
                        dve.wait_ge(e_o_made, g * E + (E + O_C))
                        dve.wait_ge(e_xres, g + 2)
                        for b in range(GB):
                            dve.tensor_tensor(yg[:, b, :], bank[b][:, 0:D], xres[:, b, :], ALU.add).then_inc(e_res, 1)
                        for b in range(GB):
                            dve.wait_ge(e_res, g * GB + (b + 1 + GB))
                            dve.bn_stats(stg[:, b, :], yg[:, b, :]).then_inc(e_ln, 1)
                        dve.wait_ge(e_ln, g * 6 + 4)
                        dve.sem_inc(passed, 1)
                        for b in range(GB):
                            ins = dve.bn_aggr(mvg[:, b, :], stg[:, b, :])
                        ins.then_inc(e_ln, 1)
                        dve.wait_ge(e_ln, g * 6 + 5)
                        dve.tensor_scalar(varg[:], mvg[:, :, 1], EPS, None, ALU.add).then_inc(e_ln, 1)
                        dve.wait_ge(e_rstd, g + 1)
                        dve.wait_ge(e_stored, g * 16 + 16)
                        for b in range(GB):
                            dve.tensor_scalar(xog[:, b, :], yg[:, b, :], mvg[:, b, 0:1], rstdg[:, b:b + 1],
                                              ALU.subtract, ALU.mult).then_inc(e_done, 1)

            scope.close()

        def routing(posu, meta, se):
            scope = ExitStack()

            def sb(name, shape, dt=F32):
                return scope.enter_context(nc.sbuf_tensor(name, shape, dt))

            xin = [sb(f"r_xin_{i}", [P, GB, D]) for i in range(2)]
            xinT = [sb(f"r_xinT_{i}", [P, KT, GB * P]) for i in range(2)]
            lg = sb("lg", [P, NB, E])
            fill = sb("fill", [P, ROW])

            with nc.Block() as block:
                @block.sync
                def _(sp):
                    def load(g, i):
                        sp.dma_start(xin[i][:], xr[bass.ds(g * GB, GB)].rearrange("b p n -> p b n")).then_inc(r_loaded[i], 16)

                    load(0, 0)
                    load(1, 1)
                    with sp.Fori(0, NGR // 2 - 1) as j:
                        for u in range(2):
                            sp.wait_ge(r_xT_made, j * 4 + (2 * u + 2))
                            load(j * 2 + (2 + u), u)

                @block.gpsimd
                def _(pool):
                    pool.memset(fill[:], 0.0).then_inc(r_meta, 1)
                    pool.wait_ge(r_meta, 1)
                    pool.memset(fill[:].bitcast(I32)[:, 2 * D + 1:2 * D + 2], TOK).then_inc(r_meta, 1)
                    pool.wait_ge(r_meta, 2)
                    pool.dma_start(routed.rearrange("(s p) r -> p s r", p=P),
                                   fill[:].unsqueeze(1).broadcast_to([P, SLOTS, ROW])).then_inc(filled, 16)
                    pool.memset(meta[:], 0.0).then_inc(r_meta, 1)
                    pool.wait_ge(r_meta, 3)
                    pool.iota(meta[:].bitcast(I32)[:, :, 1], pattern=[[P, NB]], base=0, channel_multiplier=1).then_inc(r_meta, 1)
                    pool.wait_ge(filled, 16)

                @block.tensor
                def _(pe):
                    with pe.Fori(0, NGR // 2) as j:
                        for u in range(2):
                            pe.wait_ge(r_loaded[u], j * 16 + 16)
                            pe.wait_ge(r_xT_kept, j * 4 + (2 * u + 1))
                            for k in range(KT):
                                for b in range(GB):
                                    ins = pe.transpose(bank[2 * u + k][:, b * P:(b + 1) * P], xin[u][:, b, k * P:(k + 1) * P], ident[:])
                                ins.then_inc(r_xT_made, 1)
                            pe.wait_ge(r_xT_kept, j * 4 + (2 * u + 3))
                            pe.wait_ge(r_logit_kept, j * 2 + (u + 1))
                            for b in range(GB):
                                for k in range(KT):
                                    ins = pe.matmul(bank[4 + u][:, b * E:(b + 1) * E], xinT[u][:, k, b * P:(b + 1) * P], wlog[:, k, :],
                                                    start=k == 0, stop=k == KT - 1)
                            ins.then_inc(r_logit_made, 1)

                @block.scalar
                def _(act):
                    with act.Fori(0, NGR // 2) as j:
                        for u in range(2):
                            for k in range(KT):
                                act.wait_ge(r_xT_made, j * 4 + (2 * u + k + 1))
                                act.wait_ge(r_logit_made, j * 2 + (u + 1))
                                act.copy(xinT[u][:, k, :], bank[2 * u + k][:]).then_inc(r_xT_kept, 1)

                @block.vector
                def _(dve):
                    with dve.Fori(0, NGR // 2) as j:
                        for u in range(2):
                            dve.wait_ge(r_logit_made, j * 2 + (u + 3))
                            dve.tensor_tensor(lg[:, bass.ds((j * 2 + u) * GB, GB), :], bank[4 + u][:, 0:GB * E].rearrange("p (b e) -> p b e", b=GB),
                                              blog[:].unsqueeze(1).broadcast_to([P, GB, E]), ALU.add).then_inc(r_logit_kept, 1)

            def row(name, shape=(NB, E)):
                return sb("r_" + name, [P, *shape])

            v1, v2, c1, c2, chosen = (row(n, (NB,)) for n in ("v1", "v2", "c1", "c2", "chosen"))
            diff, e2, den, r1, r2 = (row(n, (NB,)) for n in ("diff", "e2", "den", "r1", "r2"))
            eq, cand, hit, lg2, eq2, cand2 = (row(n) for n in ("eq", "cand", "hit", "lg2", "eq2", "cand2"))
            onehot, tot, upto, full, p1, p2, p3, p4 = (row(n, (E, NB)) for n in ("onehot", "tot", "upto", "full", "p1", "p2", "p3", "p4"))
            tiles, cum, base0, base = (row(n, (E,)) for n in ("tiles", "cum", "base0", "base"))
            post, started, sef = row("post", (NB,)), row("started", (SLOTS, E)), row("sef", (SLOTS,))
            flat = lambda a: a[:].rearrange("p a b -> p (a b)")
            over = lambda a: a[:].unsqueeze(2).broadcast_to([P, NB, E])
            down = descend[:].unsqueeze(1).broadcast_to([P, NB, E])

            with nc.Block() as block:
                @block.vector
                def _(dve):
                    steps = [0]

                    def link(ins):
                        steps[0] += 1
                        ins.then_inc(r_step, 1)
                        dve.wait_ge(r_step, steps[0])

                    link(dve.tensor_reduce(v1[:], lg[:], AX.X, ALU.max))
                    link(dve.tensor_tensor(eq[:], lg[:], over(v1), ALU.is_equal))
                    link(dve.tensor_tensor(cand[:], eq[:], down, ALU.mult))
                    link(dve.tensor_reduce(c1[:], cand[:], AX.X, ALU.max))
                    link(dve.tensor_tensor(hit[:], down, over(c1), ALU.is_equal))
                    link(dve.scalar_tensor_tensor(flat(lg2), flat(hit), -BIG, flat(lg), ALU.mult, ALU.add))
                    link(dve.tensor_reduce(v2[:], lg2[:], AX.X, ALU.max))
                    link(dve.tensor_tensor(eq2[:], lg2[:], over(v2), ALU.is_equal))
                    link(dve.tensor_tensor(cand2[:], eq2[:], down, ALU.mult))
                    link(dve.tensor_reduce(c2[:], cand2[:], AX.X, ALU.max))
                    link(dve.tensor_tensor(chosen[:], c1[:], c2[:], ALU.min))
                    link(dve.tensor_tensor(onehot[:].rearrange("p e b -> p b e"), down, over(chosen), ALU.is_equal))
                    assert steps[0] == R_ONEHOT
                    link(dve.tensor_tensor(diff[:], v2[:], v1[:], ALU.subtract))
                    assert steps[0] == R_DIFF
                    dve.wait_ge(r_exp, 1)
                    link(dve.tensor_scalar(den[:], e2[:], 1.0, None, ALU.add))
                    link(dve.reciprocal(r1[:], den[:]))
                    link(dve.tensor_tensor(r2[:], e2[:], r1[:], ALU.mult))
                    dve.wait_ge(r_meta, 4)
                    link(dve.tensor_tensor(meta[:, :, 0], r1[:], r2[:], ALU.add))
                    dve.wait_ge(r_rank, 2)
                    link(dve.tensor_copy(flat(tot), bank[1][:, 0:E * NB]))
                    link(dve.tensor_tensor_scan(flat(upto), flat(keepmask), flat(tot), 0.0, ALU.mult, ALU.add))
                    link(dve.tensor_tensor(full[:], upto[:, :, NB - 1].unsqueeze(2).broadcast_to([P, E, NB]), iotas[:], ALU.is_gt))
                    link(dve.tensor_reduce(tiles[:], full[:], AX.X, ALU.add))
                    link(dve.tensor_tensor_scan(cum[:], ones[:, 0:E], tiles[:], 0.0, ALU.mult, ALU.add))
                    link(dve.tensor_tensor(base0[:], cum[:], tiles[:], ALU.subtract))
                    link(dve.tensor_scalar(base[:], base0[:], float(P), None, ALU.mult))
                    link(dve.tensor_tensor(flat(p1), bank[0][:, 0:E * NB], flat(upto), ALU.add))
                    link(dve.tensor_tensor(flat(p2), flat(p1), flat(tot), ALU.subtract))
                    link(dve.tensor_tensor(p3[:], p2[:], base[:].unsqueeze(2).broadcast_to([P, E, NB]), ALU.add))
                    link(dve.tensor_tensor(flat(p4), flat(p3), flat(onehot), ALU.mult))
                    link(dve.tensor_reduce(post[:], p4[:].rearrange("p e b -> p b e"), AX.X, ALU.add))
                    link(dve.tensor_copy(posu[:], post[:]))
                    link(dve.tensor_tensor(started[:], slotn[:], cum[:].unsqueeze(1).broadcast_to([P, SLOTS, E]), ALU.is_ge))
                    link(dve.tensor_reduce(sef[:], started[:], AX.X, ALU.add))
                    link(dve.tensor_scalar(se[:], sef[:], float(E - 1), None, ALU.min))

                @block.scalar
                def _(act):
                    act.wait_ge(r_step, R_DIFF)
                    act.activation(e2[:], diff[:], ACT.Exp).then_inc(r_exp, 1)

                @block.tensor
                def _(pe):
                    pe.wait_ge(r_step, R_ONEHOT)
                    pe.matmul(bank[0][:, 0:E * NB], lower[:], flat(onehot), start=True, stop=True).then_inc(r_rank, 1)
                    pe.matmul(bank[1][:, 0:E * NB], ones[:], flat(onehot), start=True, stop=True).then_inc(r_rank, 1)

            rowt = [sb(f"rowt_{i}", [P, ROW]) for i in range(2)]
            idx = [sb(f"idx_{i}", [P, 1], U32) for i in range(2)]
            with nc.Block() as block:
                @block.sync
                def _(sp):
                    def load(b, i):
                        sp.dma_start(rowt[i][:, 0:D], xr[bass.ds(b, 1)].rearrange("a p n -> (a p) n")).then_inc(row_loaded[i], 16)
                        sp.dma_start(rowt[i][:, D:2 * D], x2[bass.ds(b, 1)].rearrange("a p n -> (a p) n")).then_inc(row_loaded[i], 16)

                    load(0, 0)
                    load(1, 1)
                    with sp.Fori(0, NB // 2 - 1) as j:
                        for u in range(2):
                            sp.wait_ge(row_sent[u], j * 16 + 16)
                            load(j * 2 + (2 + u), u)

                @block.vector
                def _(dve):
                    def put(b, i):
                        dve.tensor_copy(rowt[i][:, 2 * D:ROW].unsqueeze(1), meta[:, bass.ds(b, 1), :]).then_inc(row_meta, 1)
                        dve.tensor_copy(idx[i][:], posu[:, bass.ds(b, 1)]).then_inc(row_meta, 1)

                    put(0, 0)
                    put(1, 1)
                    with dve.Fori(0, NB // 2 - 1) as j:
                        for u in range(2):
                            dve.wait_ge(row_sent[u], j * 16 + 16)
                            dve.sem_inc(passed, 1)
                            put(j * 2 + (2 + u), u)

                @block.gpsimd
                def _(pool):
                    with pool.Fori(0, NB // 2) as j:
                        for u in range(2):
                            pool.wait_ge(row_loaded[u], j * 32 + 32)
                            pool.wait_ge(row_meta, j * 4 + (2 * u + 2))
                            pool.sem_inc(passed, 1)
                            pool.indirect_dma_start(out=routed[:, :], out_offset=bass.IndirectOffsetOnAxis(ap=idx[u][:, 0:1], axis=0),
                                                    in_=rowt[u][:], in_offset=None).then_inc(row_sent[u], 16)
                    for i in range(2):
                        pool.wait_ge(row_sent[i], 16 * (NB // 2))
            scope.close()

        def slots(se):
            scope = ExitStack()

            def sb(name, shape, dt=F32):
                return scope.enter_context(nc.sbuf_tensor(name, shape, dt))

            rowt = [sb(f"t_row_{i}", [P, ROW]) for i in range(4)]
            b1t = [sb(f"t_b1_{i}", [P, HID]) for i in range(4)]
            b2t = [sb(f"t_b2_{i}", [P, D]) for i in range(4)]
            part = [sb(f"t_par_{i}", [P, 2 * HC + 1]) for i in range(4)]
            xTt = sb("t_xT", [P, KT, P])
            hb = sb("t_hb", [P, HID])
            hn = [sb(f"t_hn_{i}", [P, HID]) for i in range(2)]
            hT = sb("t_hT", [P, HC, P])
            st, st2, st3 = (sb(f"t_st_{i}", [P, 6]) for i in range(3))
            mvt, mv2, mv3 = (sb(f"t_mv_{i}", [P, 2]) for i in range(3))
            var1, var2, var3 = (sb(f"t_var_{i}", [P, 1]) for i in range(3))
            rs1, rs2, rs3 = (sb(f"t_rs_{i}", [P, 1]) for i in range(3))
            ot, sel, res, nrm, ng, w3 = (sb(f"t_{n}", [P, D]) for n in ("ot", "sel", "res", "nrm", "ng", "w3"))
            xpb = sb("t_xpb", [P, D])
            z = [sb(f"t_z_{i}", [P, D]) for i in range(2)]
            HB, HTB, OB, XB = bank[0:2], bank[2:4], bank[4:6], bank[6]

            def steps(eng, step):
                def s(n):
                    return (n, n % 4, n // 4)

                step(s(0), None)
                for n in (1, 2):
                    step(s(n), s(n - 1))
                with eng.Fori(0, (SLOTS - 3) // 4) as j:
                    for u in range(3, 7):
                        step((j * 4 + u, u % 4, j + u // 4), (j * 4 + (u - 1), (u - 1) % 4, j + (u - 1) // 4))
                step(None, s(SLOTS - 1))

            with nc.Block() as block:
                @block.sync
                def _(sp):
                    def load(n, i, turn):
                        wait(sp, t_sent[i], turn * 16)
                        e = sp.value_load(se[0:1, bass.ds(n, 1)], min_val=0, max_val=E - 1)
                        sp.dma_start(rowt[i][:], routed[bass.ds(n * P, P), :]).then_inc(t_loaded[i], 16)
                        sp.dma_start(b1t[i][:], t["b1"][bass.ds(e, 1)].rearrange("a n -> (a n)").partition_broadcast(P)).then_inc(t_loaded[i], 16)
                        sp.dma_start(b2t[i][:], t["b2"][bass.ds(e, 1)].rearrange("a n -> (a n)").partition_broadcast(P)).then_inc(t_loaded[i], 16)
                        sp.dma_start(part[i][:], t["par"][bass.ds(e, 1)].rearrange("a p n -> (a p) n")).then_inc(t_loaded[i], 16)

                    for n in range(4):
                        load(n, n, 0)
                    with sp.Fori(0, SLOTS // 4 - 1) as j:
                        for u in range(4):
                            load(j * 4 + (4 + u), u, j + 1)
                    for n in range(SLOTS // 4 * 4, SLOTS):
                        load(n, n % 4, n // 4)

                @block.gpsimd
                def _(pool):
                    def step(a, c):
                        if a:
                            n, i, turn = a
                            pool.wait_ge(t_h, n * 4 + 4)
                            wait(pool, t_hn, n)
                            pool.tensor_tensor(rs1[:], var1[:], minus_half[:, 0:1], ALU.pow).then_inc(t_rstd, 1)
                        if c:
                            n, i, turn = c
                            pool.wait_ge(t_loaded[i], turn * 64 + 64)
                            wait(pool, t_y, n * 11)
                            pool.tensor_tensor(xpb[:], rowt[i][:, D:2 * D], n2b[:], ALU.add).then_inc(t_xb, 1)
                            pool.wait_ge(t_y, n * 11 + 6)
                            pool.tensor_tensor(rs2[:], var2[:], minus_half[:, 0:1], ALU.pow).then_inc(t_rstd2, 1)
                            pool.wait_ge(t_y, n * 11 + 11)
                            wait(pool, t_z, n)
                            pool.tensor_tensor(rs3[:], var3[:], minus_half[:, 0:1], ALU.pow).then_inc(t_rstd2, 1)
                            pool.wait_ge(t_z, n + 1)
                            pool.sem_inc(passed, 1)
                            pool.indirect_dma_start(out=x3_rows[:, :], out_offset=bass.IndirectOffsetOnAxis(
                                ap=rowt[i][:].bitcast(U32)[:, 2 * D + 1:2 * D + 2], axis=0), in_=z[i % 2][:], in_offset=None,
                                bounds_check=TOK - 1, oob_is_err=False).then_inc(t_sent[i], 16)

                    steps(pool, step)
                    for i in range(4):
                        pool.wait_ge(t_sent[i], 16 * ((SLOTS - 1 - i) // 4 + 1))

                @block.tensor
                def _(pe):
                    pe.wait_ge(big_loaded, 16 * (len(big) + 2))

                    def step(a, c):
                        if a:
                            n, i, turn = a
                            e = pe.value_load(se[0:1, bass.ds(n, 1)], min_val=0, max_val=E - 1)
                            pe.wait_ge(t_loaded[i], turn * 64 + 64)
                            wait(pe, t_xT_kept, n)
                            for k in range(KT):
                                ins = pe.transpose(XB[:, k * P:(k + 1) * P], rowt[i][:, k * P:(k + 1) * P], ident[:])
                            ins.then_inc(t_xT_made, 1)
                            pe.wait_ge(t_xT_kept, n + 1)
                            wait(pe, t_h, n * 4 - 7)
                            for k in range(KT):
                                ins = pe.matmul(HB[i % 2][:], xTt[:, k, :], wa[:, k, bass.ds(e, 1), :].rearrange("p a n -> p (a n)"),
                                                start=k == 0, stop=k == KT - 1)
                            ins.then_inc(t_h_made, 1)
                        if c:
                            n, i, turn = c
                            e = pe.value_load(se[0:1, bass.ds(n, 1)], min_val=0, max_val=E - 1)
                            pe.wait_ge(t_hn, n + 1)
                            wait(pe, t_gelu, n * HC - HC)
                            for k in range(HC):
                                ins = pe.transpose(HTB[i % 2][:, k * P:(k + 1) * P], hn[i % 2][:, k * P:(k + 1) * P], ident[:])
                            ins.then_inc(t_hT_made, 1)
                            pe.wait_ge(t_gelu, n * HC + HC)
                            wait(pe, t_y, n * 11 - 21)
                            for k in range(HC):
                                ins = pe.matmul(OB[i % 2][:, 0:D], hT[:, k, :], wb[:, bass.ds(e, 1), k, :].rearrange("p a n -> p (a n)"),
                                                start=k == 0, stop=k == HC - 1)
                            ins.then_inc(t_o_made, 1)

                    steps(pe, step)

                @block.scalar
                def _(act):
                    def step(a, c):
                        if a:
                            n, i, turn = a
                            act.wait_ge(t_xT_made, n + 1)
                            wait(act, t_h_made, n)
                            act.copy(xTt[:], XB[:, 0:D]).then_inc(t_xT_kept, 1)
                        if c:
                            n, i, turn = c
                            act.wait_ge(t_hT_made, n + 1)
                            wait(act, t_o_made, n)
                            for k in range(HC):
                                act.activation(hT[:, k, :], HTB[i % 2][:, k * P:(k + 1) * P], ACT.Gelu,
                                               scale=part[i][:, k:k + 1], bias=part[i][:, HC + k:HC + k + 1]).then_inc(t_gelu, 1)

                    steps(act, step)

                @block.vector
                def _(dve):
                    def step(a, c):
                        if a:
                            n, i, turn = a
                            dve.wait_ge(t_h_made, n + 1)
                            wait(dve, t_hn, n)
                            dve.tensor_tensor(hb[:], HB[i % 2][:], b1t[i][:], ALU.add).then_inc(t_h, 1)
                            dve.wait_ge(t_h, n * 4 + 1)
                            dve.bn_stats(st[:], hb[:]).then_inc(t_h, 1)
                            dve.wait_ge(t_h, n * 4 + 2)
                            dve.sem_inc(passed, 1)
                            dve.bn_aggr(mvt[:], st[:]).then_inc(t_h, 1)
                            dve.wait_ge(t_h, n * 4 + 3)
                            dve.tensor_scalar(var1[:], mvt[:, 1:2], EPS, None, ALU.add).then_inc(t_h, 1)
                            dve.wait_ge(t_rstd, n + 1)
                            wait(dve, t_hT_made, n - 1)
                            dve.tensor_scalar(hn[i % 2][:], hb[:], mvt[:, 0:1], rs1[:], ALU.subtract, ALU.mult).then_inc(t_hn, 1)
                        if c:
                            n, i, turn = c
                            x1r, x2r, wsum = rowt[i][:, 0:D], rowt[i][:, D:2 * D], rowt[i][:, 2 * D:2 * D + 1]
                            k = [0]

                            def link(ins):
                                k[0] += 1
                                ins.then_inc(t_y, 1)
                                dve.wait_ge(t_y, n * 11 + k[0])

                            dve.wait_ge(t_o_made, n + 1)
                            wait(dve, t_z, n)
                            link(dve.tensor_tensor(ot[:], OB[i % 2][:, 0:D], b2t[i][:], ALU.add))
                            link(dve.scalar_tensor_tensor(sel[:], ot[:], part[i][:, 2 * HC:2 * HC + 1], x1r, ALU.mult, ALU.add))
                            link(dve.scalar_tensor_tensor(res[:], sel[:], wsum, x1r, ALU.mult, ALU.add))
                            link(dve.bn_stats(st2[:], res[:]))
                            dve.sem_inc(passed, 1)
                            link(dve.bn_aggr(mv2[:], st2[:]))
                            link(dve.tensor_scalar(var2[:], mv2[:, 1:2], EPS, None, ALU.add))
                            dve.wait_ge(t_rstd2, n * 2 + 1)
                            link(dve.tensor_scalar(nrm[:], res[:], mv2[:, 0:1], rs2[:], ALU.subtract, ALU.mult))
                            link(dve.tensor_tensor(ng[:], nrm[:], n2g[:], ALU.mult))
                            dve.wait_ge(t_xb, n + 1)
                            dve.tensor_tensor(w3[:], ng[:], xpb[:], ALU.add).then_inc(t_w, 1)
                            dve.wait_ge(t_w, n + 1)
                            link(dve.bn_stats(st3[:], w3[:]))
                            dve.sem_inc(passed, 1)
                            link(dve.bn_aggr(mv3[:], st3[:]))
                            link(dve.tensor_scalar(var3[:], mv3[:, 1:2], EPS, None, ALU.add))
                            assert k[0] == 11
                            dve.wait_ge(t_rstd2, n * 2 + 2)
                            wait(dve, t_sent[(i - 2) % 4], (turn + (1 if i >= 2 else 0)) * 16)
                            dve.tensor_scalar(z[i % 2][:], w3[:], mv3[:, 0:1], rs3[:], ALU.subtract, ALU.mult).then_inc(t_z, 1)

                    steps(dve, step)
            scope.close()

        ROUTER = 19

        def experts1():
            scope = ExitStack()

            def sb(name, shape, dt=F32):
                return scope.enter_context(nc.sbuf_tensor("f_" + name, shape, dt))

            xg = sb("xg", [P, GB, D])
            xres = sb("xres", [P, GB, D])
            xgT = sb("xgT", [P, KT, GB * P])
            silu = [sb(f"silu_{i}", [P, GB * P]) for i in range(2)]
            prod = [sb(f"prod_{i}", [P, GB * P]) for i in range(2)]
            wB = [sb(f"wB_{i}", [P, GB * P]) for i in range(2)]
            hid = [sb(f"hid_{i}", [P, GB * P]) for i in range(2)]
            yg = sb("yg", [P, GB, D])
            xog = sb("xog", [P, GB, D])
            stg = sb("stg", [P, GB, 6])
            mvg = sb("mvg", [P, GB, 2])
            varg = sb("varg", [P, GB])
            rstdg = sb("rstdg", [P, GB])
            lg, sh, es, s, eq, cand, hit, s2, eq2, cand2, hit2, drop, keep, wts = (
                sb(n, [P, GB, E]) for n in ("lg", "sh", "es", "s", "eq", "cand", "hit", "s2", "eq2", "cand2", "hit2", "drop", "keep", "wts"))
            mx, sm, rc, m1, c1, m2, c2 = (sb(n, [P, GB]) for n in ("mx", "sm", "rc", "m1", "c1", "m2", "c2"))
            flat = lambda a: a[:].rearrange("p a b -> p (a b)")
            over = lambda a: a[:].unsqueeze(2).broadcast_to([P, GB, E])
            up = ascend[:].unsqueeze(1).broadcast_to([P, GB, E])
            SHARED = UNITS - E
            GBANK, UBANK, WBANK, XBANK = bank[4], bank[5], bank[6], bank[7]

            with nc.Block() as block:
                @block.sync
                def _(sp):
                    def group(ap, g):
                        return ap[bass.ds(g * GB, GB)].rearrange("b p n -> p b n")

                    def load(g):
                        sp.wait_ge(f_xres, g + 1)
                        sp.wait_ge(f_xT_made, g * KT + KT)
                        sp.dma_start(xg[:], group(x5, g)).then_inc(f_loaded, 16)

                    def store(g):
                        sp.wait_ge(f_done, g * GB + 2 * GB)
                        sp.dma_start(group(out, g), xog[:]).then_inc(f_stored, 16)

                    load(0)
                    with sp.Fori(0, NGR - 1) as g:
                        load(g + 1)
                        store(g)
                    store(NGR - 1)
                    sp.wait_ge(f_stored, 16 * (NGR + 1))

                @block.gpsimd
                def _(pool):
                    with pool.Fori(0, NGR) as g:
                        pool.wait_ge(f_loaded, g * 16 + 16)
                        pool.wait_ge(f_res, g * GB + GB)
                        pool.sem_inc(passed, 1)
                        pool.tensor_copy(xres[:], xg[:]).then_inc(f_xres, 1)
                        pool.wait_ge(f_ln, g * 6 + 6)
                        pool.wait_ge(f_done, g * GB + GB)
                        pool.tensor_tensor(rstdg[:], varg[:], minus_half[:], ALU.pow).then_inc(f_rstd, 1)

                @block.tensor
                def _(pe):
                    with pe.Fori(0, NGR) as g:
                        def in_products(k):
                            pe.wait_ge(f_silu, g * UNITS + (k + 1))
                            for i in range(KT):
                                ins = pe.matmul(GBANK[:], w7g[:, i, k, :], xgT[:, i, :], start=i == 0, stop=i == KT - 1)
                            ins.then_inc(f_gate_made, 1)
                            pe.wait_ge(f_hid, g * UNITS + (k + 3))
                            for i in range(KT):
                                ins = pe.matmul(UBANK[:], w7u[:, i, k, :], xgT[:, i, :], start=i == 0, stop=i == KT - 1)
                            ins.then_inc(f_up_made, 1)

                        def spread(k):
                            e = k - SHARED
                            if e == 0:
                                pe.wait_ge(f_step, g * ROUTER + ROUTER)
                            pe.wait_ge(f_wB_kept, g * E + (e + 1))
                            for b in range(GB):
                                ins = pe.transpose(WBANK[:, b * P:(b + 1) * P], wts[:, b, e:e + 1].broadcast_to([P, P]), ident[:])
                            ins.then_inc(f_wB_made, 1)

                        def out_product(k):
                            if k == 0:
                                pe.wait_ge(f_res, g * GB + GB)
                            pe.wait_ge(f_hid, g * UNITS + (k + 4))
                            for b in range(GB):
                                ins = pe.matmul(bank[b][:, 0:D], hid[k % 2][:, b * P:(b + 1) * P], w7d[:, k, :], start=k == 0, stop=k == UNITS - 1)
                            ins.then_inc(f_o_made, 1)

                        pe.wait_ge(f_loaded, g * 16 + 16)
                        for k in range(KT):
                            pe.wait_ge(f_xT_kept, g * KT + (k + 1))
                            for b in range(GB):
                                ins = pe.transpose(XBANK[:, b * P:(b + 1) * P], xg[:, b, k * P:(k + 1) * P], ident[:])
                            ins.then_inc(f_xT_made, 1)
                        pe.wait_ge(f_xT_kept, g * KT + (KT + 1))
                        for b in range(GB):
                            for k in range(KT):
                                ins = pe.matmul(XBANK[:, b * E:(b + 1) * E], xgT[:, k, b * P:(b + 1) * P], w7r[:, k, :],
                                                start=k == 0, stop=k == KT - 1)
                        ins.then_inc(f_logit_made, 1)
                        for k in range(UNITS):
                            in_products(k)
                            if k + 1 >= SHARED and k + 1 < UNITS:
                                spread(k + 1)
                            if k:
                                out_product(k - 1)
                        out_product(UNITS - 1)

                @block.scalar
                def _(act):
                    with act.Fori(0, NGR) as g:
                        for k in range(KT):
                            act.wait_ge(f_xT_made, g * KT + (k + 1 + KT))
                            act.wait_ge(f_o_made, g * UNITS + 2)
                            act.copy(xgT[:, k, :], XBANK[:]).then_inc(f_xT_kept, 1)
                        act.wait_ge(f_step, g * ROUTER + 3)
                        act.activation(es[:], sh[:], ACT.Exp).then_inc(f_exp, 1)
                        for k in range(UNITS):
                            act.wait_ge(f_gate_made, g * UNITS + (k + 1))
                            act.wait_ge(f_hid, g * UNITS + (k + 2))
                            act.activation(silu[k % 2][:], GBANK[:], ACT.Silu).then_inc(f_silu, 1)
                            if k + 1 >= SHARED and k + 1 < UNITS:
                                act.wait_ge(f_wB_made, g * E + (k + 1 - SHARED + 2))
                                act.copy(wB[(k + 1) % 2][:], WBANK[:]).then_inc(f_wB_kept, 1)

                @block.vector
                def _(dve):
                    with dve.Fori(0, NGR) as g:
                        k_ = [0]

                        def link(ins):
                            k_[0] += 1
                            ins.then_inc(f_step, 1)
                            dve.wait_ge(f_step, g * ROUTER + k_[0])

                        dve.wait_ge(f_logit_made, g + 2)
                        link(dve.tensor_copy(flat(lg), XBANK[:, 0:GB * E]))
                        link(dve.tensor_reduce(mx[:], lg[:], AX.X, ALU.max))
                        link(dve.tensor_tensor(sh[:], lg[:], over(mx), ALU.subtract))
                        dve.wait_ge(f_exp, g + 2)
                        link(dve.tensor_reduce(sm[:], es[:], AX.X, ALU.add))
                        link(dve.reciprocal(rc[:], sm[:]))
                        link(dve.tensor_tensor(s[:], es[:], over(rc), ALU.mult))
                        link(dve.tensor_reduce(m1[:], s[:], AX.X, ALU.min))
                        link(dve.tensor_tensor(eq[:], s[:], over(m1), ALU.is_equal))
                        link(dve.tensor_tensor(cand[:], eq[:], up, ALU.mult))
                        link(dve.tensor_reduce(c1[:], cand[:], AX.X, ALU.max))
                        link(dve.tensor_tensor(hit[:], up, over(c1), ALU.is_equal))
                        link(dve.scalar_tensor_tensor(flat(s2), flat(hit), 4.0, flat(s), ALU.mult, ALU.add))
                        link(dve.tensor_reduce(m2[:], s2[:], AX.X, ALU.min))
                        link(dve.tensor_tensor(eq2[:], s2[:], over(m2), ALU.is_equal))
                        link(dve.tensor_tensor(cand2[:], eq2[:], up, ALU.mult))
                        link(dve.tensor_reduce(c2[:], cand2[:], AX.X, ALU.max))
                        link(dve.tensor_tensor(hit2[:], up, over(c2), ALU.is_equal))
                        link(dve.tensor_tensor(drop[:], hit[:], hit2[:], ALU.add))
                        dve.wait_ge(f_wB_made, g * E + 1)
                        dve.tensor_scalar(keep[:], drop[:], -1.0, 1.0, ALU.mult, ALU.add).then_inc(f_keep, 1)
                        dve.wait_ge(f_keep, g + 1)
                        link(dve.tensor_tensor(wts[:], s[:], keep[:], ALU.mult))
                        assert k_[0] == ROUTER
                        for k in range(UNITS):
                            dve.wait_ge(f_silu, g * UNITS + (k + 2))
                            dve.wait_ge(f_up_made, g * UNITS + (k + 1))
                            dve.wait_ge(f_o_made, g * UNITS + (k + 1))
                            if k < SHARED:
                                dve.tensor_tensor(hid[k % 2][:], UBANK[:], silu[k % 2][:], ALU.mult).then_inc(f_hid, 1)
                            else:
                                dve.tensor_tensor(prod[k % 2][:], UBANK[:], silu[k % 2][:], ALU.mult).then_inc(f_prod, 1)
                                dve.wait_ge(f_prod, g * E + (k - SHARED + 1))
                                dve.wait_ge(f_wB_kept, g * E + (k - SHARED + 2))
                                dve.tensor_tensor(hid[k % 2][:], prod[k % 2][:], wB[k % 2][:], ALU.mult).then_inc(f_hid, 1)
                        dve.wait_ge(f_o_made, g * UNITS + (UNITS + 2))
                        dve.wait_ge(f_xres, g + 2)
                        for b in range(GB):
                            dve.tensor_tensor(yg[:, b, :], bank[b][:, 0:D], xres[:, b, :], ALU.add).then_inc(f_res, 1)
                        for b in range(GB):
                            dve.wait_ge(f_res, g * GB + (b + 1 + GB))
                            dve.bn_stats(stg[:, b, :], yg[:, b, :]).then_inc(f_ln, 1)
                        dve.wait_ge(f_ln, g * 6 + 4)
                        dve.sem_inc(passed, 1)
                        for b in range(GB):
                            ins = dve.bn_aggr(mvg[:, b, :], stg[:, b, :])
                        ins.then_inc(f_ln, 1)
                        dve.wait_ge(f_ln, g * 6 + 5)
                        dve.tensor_scalar(varg[:], mvg[:, :, 1], EPS, None, ALU.add).then_inc(f_ln, 1)
                        dve.wait_ge(f_rstd, g + 1)
                        dve.wait_ge(f_stored, g * 16 + 16)
                        for b in range(GB):
                            dve.tensor_scalar(xog[:, b, :], yg[:, b, :], mvg[:, b, 0:1], rstdg[:, b:b + 1],
                                              ALU.subtract, ALU.mult).then_inc(f_done, 1)
            scope.close()

        attention(CAUSAL, big)
        experts0()
        attention(SCALED, [(wa, t["wa1"]), (wb, t["wb1"])])
        with ExitStack() as scope:
            posu = scope.enter_context(nc.sbuf_tensor("posu", [P, NB], U32))
            meta = scope.enter_context(nc.sbuf_tensor("meta", [P, NB, ROW - 2 * D], F32))
            se = scope.enter_context(nc.sbuf_tensor("se", [P, SLOTS], I32))
            routing(posu, meta, se)
            slots(se)
        attention(ROTARY, [])
        attention(CROSS, [])
        experts1()


def host_layout(inputs):
    g = {k: np.asarray(a) for k, a in inputs.items()}

    def kt(w):
        return w.reshape(w.shape[0] // P, P, w.shape[1]).transpose(1, 0, 2)

    wqkv = np.zeros((P, 4, KT, 3 * D), np.float32)
    wqkv[:, 0] = kt(g["L0_attn_w_attn"])
    for i, n in enumerate(("q", "k", "v")):
        wqkv[:, 1, :, i * D:(i + 1) * D] = kt(g[f"L0_ffn_{n}_w"])
    wqkv[:, 2] = kt(g["L1_attn_w_qkv"].T)
    wqkv[:, 3, :, 0:D] = kt(g["L1_xattn_Wq"])
    wqkv[:, 3, 0, D:2 * D] = g["L1_xattn_Wk"]
    wqkv[:, 3, 0, 2 * D:] = g["L1_xattn_Wv"]
    wo = np.stack([kt(g["L0_attn_w_proj"]), kt(g["L0_ffn_out_w"]), kt(g["L1_attn_w_out"].T), kt(g["L1_xattn_Wo"])], 1)
    key, query = np.arange(P)[:, None], np.arange(P)[None, :]
    masked = np.where(key > query, -BIG, 0.0).astype(np.float32)
    inv_freq = (1.0 / 10000.0 ** (np.arange(0, DK, 2, dtype=np.float32) / DK)).astype(np.float32)
    freqs = np.arange(P, dtype=np.float32)[:, None] * inv_freq[None, :]
    def expert_in(w):
        return w.reshape(w.shape[0], -1, P, w.shape[2]).transpose(2, 1, 0, 3)

    def expert_out(w):
        return w.reshape(w.shape[0], -1, P, w.shape[2]).transpose(2, 0, 1, 3)

    def shared_in(w):
        return w.reshape(D, D // F1, F1).transpose(1, 0, 2)

    par = np.concatenate([g["L0_ffn_ln_g"].reshape(E, HC, P).transpose(0, 2, 1), g["L0_ffn_ln_b"].reshape(E, HC, P).transpose(0, 2, 1),
                          np.broadcast_to(g["L0_ffn_res_scale"][:, None, None], (E, P, 1))], 2)
    t = {
        "wa0": expert_in(g["L0_xattn_proj_in"].transpose(0, 2, 1)), "wb0": expert_out(g["L0_xattn_proj_out"].transpose(0, 2, 1)),
        "wa1": expert_in(g["L0_ffn_w1"]), "wb1": expert_out(g["L0_ffn_w2"]), "b1": g["L0_ffn_b1"], "b2": g["L0_ffn_b2"], "par": par,
        "w7g": expert_in(np.concatenate([shared_in(g["L1_ffn_ws_gate"]), g["L1_ffn_w_gate"]])),
        "w7u": expert_in(np.concatenate([shared_in(g["L1_ffn_ws_up"]), g["L1_ffn_w_up"]])),
        "w7d": np.concatenate([g["L1_ffn_ws_down"].reshape(D // F1, F1, D), g["L1_ffn_w_down"]]).transpose(1, 0, 2),
        "w7r": kt(g["L1_ffn_router_w"]), "wlog": kt(g["L0_ffn_moe_gate_w"]), "b_log": g["L0_ffn_moe_gate_b"],
        "n2_g": g["L0_ffn_n2_g"], "n2_b": g["L0_ffn_n2_b"],
        "ones": np.ones((P, P), np.float32), "lower": np.triu(np.ones((P, P), np.float32), 1),
        "ascend": 1 + np.arange(E, dtype=np.float32),
        "descend": E - np.arange(E, dtype=np.float32), "iotas": np.tile(np.arange(NB, dtype=np.float32) * P, E),
        "slotn": np.repeat(np.arange(SLOTS, dtype=np.float32), E),
        "keepmask": np.tile((np.arange(NB) > 0).astype(np.float32), E),
        "x": g["x"], "ctx": g["ctx_512"], "itok": g["itok_BxS2xS_0_7"],
        "wqkv": wqkv, "wo": wo, "gatew": kt(g["L0_ffn_gate_w"]),
        "b_qkv0": g["L0_attn_b_attn"], "b_qkv3": np.concatenate([g["L1_xattn_bq"], g["L1_xattn_bk"], g["L1_xattn_bv"]]),
        "b_o0": g["L0_attn_b_proj"], "b_o2": g["L1_attn_b_out"], "b_o3": g["L1_xattn_bo"],
        "scale_w": g["L0_ffn_scale_w"].reshape(-1), "gate_b": g["L0_ffn_gate_b"],
        "n1_g": g["L0_ffn_n1_g"], "n1_b": g["L0_ffn_n1_b"],
        "ident": np.eye(P, dtype=np.float32),
        "maskk": masked, "maskq": masked.T,
        "cos": np.cos(freqs).astype(np.float32), "sin": np.stack([-np.sin(freqs), np.sin(freqs)], 1).astype(np.float32),
    }
    return {k: np.ascontiguousarray(a) for k, a in t.items()}


def kernel(**inputs):
    import concourse.bacc as bacc
    from concourse.bass_utils import run_bass_kernel_spmd

    nc = bacc.Bacc("TRN2", target_bir_lowering=False, num_devices=1)
    arrays = host_layout(inputs)
    t = {n: nc.dram_tensor(f"in_{n}", a.shape, mybir.dt.from_np(a.dtype), kind="ExternalInput").ap() for n, a in arrays.items()}
    out = nc.dram_tensor("out_dram", (NB, P, D), F32, kind="ExternalOutput").ap()
    program(nc, t, out)
    r = run_bass_kernel_spmd(nc, [{f"in_{n}": a for n, a in arrays.items()}], core_ids=[0])
    return r.results[0]["out_dram"]
```

```python
from contextlib import ExitStack

import concourse.bass as bass
import concourse.mybir as mybir
import numpy as np

F32 = mybir.dt.float32
BF16 = mybir.dt.bfloat16
I32 = mybir.dt.int32
U32 = mybir.dt.uint32
ALU = mybir.AluOpType
ACT = mybir.ActivationFunctionType
AX = mybir.AxisListType

P = 128
NB = 16
D = 256
KT = D // P
H = 16
DK = D // H
HP = 32
HG = P // HP
NG = H // HG
E = 8
HID = 512
HC = HID // P
F1 = 128
GB = 4
NGR = NB // GB
TOK = NB * P
SLOTS = (TOK + E * (P - 1)) // P
UNITS = E + D // F1
ROW = 2 * D + 4
EPS = 1e-5
BIG = 1e30
CAUSAL, SCALED, ROTARY, CROSS = range(4)


class At:

    def __init__(self, stage, b, half, parity):
        self.b, self.n, self.half, self.p = b, b + NB * stage, half, parity
        self.nhalf = half + (NB // 2) * stage


def at(stage, b):
    return At(stage, b, b // 2, b % 2)


def wait(eng, sem, value):
    if isinstance(value, int) and value <= 0:
        return
    eng.wait_ge(sem, value)


def attention_steps(eng, stage, step):
    for b in range(3):
        step(at(stage, b), at(stage, b - 1) if b > 0 else None, at(stage, b - 2) if b > 1 else None)
    with eng.Fori(0, (NB - 4) // 2) as j:
        for u in range(2):
            step(*(At(stage, j * 2 + (3 + u - back), j + (3 + u - back) // 2, (3 + u - back) % 2) for back in range(3)))
    step(at(stage, NB - 1), at(stage, NB - 2), at(stage, NB - 3))
    step(None, at(stage, NB - 1), at(stage, NB - 2))
    step(None, None, at(stage, NB - 1))


def program(nc, t, out):
    ctx = ExitStack()
    with ctx:
        def sb(name, shape, dt=F32):
            return ctx.enter_context(nc.sbuf_tensor(name, shape, dt))

        def sem(name):
            return ctx.enter_context(nc.semaphore(name))

        def dram(name, shape, dt=F32):
            return nc.dram_tensor(name, shape, dt).ap()

        x1 = dram("x1_dram", [NB, P, D])
        x2 = dram("x2_dram", [NB, P, D])
        xr = dram("xr_dram", [NB, P, D])
        x3_rows = dram("x3_dram", [TOK, D])
        x3 = x3_rows.rearrange("(b p) d -> b p d", p=P)
        routed = dram("routed_dram", [SLOTS * P, ROW])
        x4 = dram("x4_dram", [NB, P, D])
        x5 = dram("x5_dram", [NB, P, D])
        X_IN = [t["x"], x2, x3, x4]
        X_OUT = [x1, xr, x4, x5]

        bank = [ctx.enter_context(nc.psum_tensor(f"bank{i}", [P, 512], F32)) for i in range(8)]
        QKB, VB, OTB, TB = bank[0], bank[1], bank[2], bank[3]
        SB = [bank[4], bank[5]]
        PTB = [bank[6], bank[7]]

        ident = sb("ident", [P, P])
        identb = sb("identb", [P, P], BF16)
        maskq = sb("maskq", [P, HG, P], BF16)
        maskf = sb("maskf", [P, P])
        minus_half = sb("minus_half", [P, 4])
        cosb = sb("cosb", [P, DK // 2])
        sinb = sb("sinb", [P, 2, DK // 2])
        qk = sb("qk", [P, 2, H, HP])
        v = [sb(f"v_{i}", [P, H, HP]) for i in range(2)]
        wqkv = sb("wqkv", [P, 4, KT, 3 * D])
        wo = sb("wo", [P, 4, KT, D])
        gatew = sb("gatew", [P, KT, D])
        bqkv = sb("bqkv", [P, 2, 3 * D])
        bout = sb("bout", [P, 4, D])
        scalew = sb("scalew", [P, D])
        gateb = sb("gateb", [P, D])
        n1g = sb("n1g", [P, D])
        n1b = sb("n1b", [P, D])

        wa = sb("wa", [P, KT, E, HID])
        wb = sb("wb", [P, E, HC, D])
        w7g = sb("w7g", [P, KT, UNITS, F1])
        w7u = sb("w7u", [P, KT, UNITS, F1])
        w7d = sb("w7d", [P, UNITS, D])
        w7r = sb("w7r", [P, KT, E])
        wlog = sb("wlog", [P, KT, E])
        blog = sb("blog", [P, E])
        n2g = sb("n2g", [P, D])
        n2b = sb("n2b", [P, D])
        ones = sb("ones", [P, P])
        lower = sb("lower", [P, P])
        ascend = sb("ascend", [P, E])
        descend = sb("descend", [P, E])
        iotas = sb("iotas", [P, E, NB])
        slotn = sb("slotn", [P, SLOTS, E])
        keepmask = sb("keepmask", [P, E, NB])

        loaded = sem("loaded_constants")
        init = sem("init")
        x_loaded = [sem(f"x_loaded_{i}") for i in range(2)]
        x_stored = [sem(f"x_stored_{i}") for i in range(2)]
        xT_made = sem("xT_made")
        qkv_made = sem("qkv_made")
        qkT_made = sem("qkT_made")
        s_made = sem("s_made")
        probsT_made = sem("probsT_made")
        av_made = sem("av_made")
        o_made = sem("o_made")
        attT_made = sem("attT_made")
        proj_made = sem("proj_made")
        xT_kept = sem("xT_kept")
        probs_kept = sem("probs_kept")
        qT_kept = sem("qT_kept")
        kT_kept = [sem(f"kT_kept_{i}") for i in range(2)]
        oT_kept = sem("oT_kept")
        attT_kept = sem("attT_kept")
        qk_kept = sem("qk_kept")
        v_kept = sem("v_kept")
        max_kept = sem("max_kept")
        probsT_kept = sem("probsT_kept")
        rden_done = sem("rden_done")
        att_kept = sem("att_kept")
        res_done = sem("res_done")
        ln_step = sem("ln_step")
        ln_done = sem("ln_done")
        xb_done = sem("xb_done")
        rstd_done = sem("rstd_done")
        kdiag_cleared = sem("kdiag_cleared")
        passed = sem("passed")
        lin_step = sem("lin_step")
        tanh_done = sem("tanh_done")
        fac_done = sem("fac_done")
        gate_made = sem("gate_made")
        gz_done = sem("gz_done")
        gth_done = sem("gth_done")
        gated_done = sem("gated_done")
        gatedT_made = sem("gatedT_made")
        gatedT_kept = sem("gatedT_kept")
        n1_step = sem("n1_step")
        big_loaded = sem("big_loaded")
        e_loaded = sem("e_loaded")
        e_stored = sem("e_stored")
        e_xT_made = sem("e_xT_made")
        e_gate_made = sem("e_gate_made")
        e_z_made = sem("e_z_made")
        e_o_made = sem("e_o_made")
        e_xT_kept = sem("e_xT_kept")
        e_gate_kept = sem("e_gate_kept")
        e_masked = sem("e_masked")
        e_hid = sem("e_hid")
        e_res = sem("e_res")
        e_ln = sem("e_ln")
        e_xres = sem("e_xres")
        e_rstd = sem("e_rstd")
        e_done = sem("e_done")
        r_loaded = [sem(f"r_loaded_{i}") for i in range(2)]
        r_xT_made = sem("r_xT_made")
        r_xT_kept = sem("r_xT_kept")
        r_logit_made = sem("r_logit_made")
        r_logit_kept = sem("r_logit_kept")
        r_step = sem("r_step")
        r_exp = sem("r_exp")
        r_rank = sem("r_rank")
        r_meta = sem("r_meta")
        filled = sem("filled")
        row_loaded = [sem(f"row_loaded_{i}") for i in range(2)]
        row_meta = sem("row_meta")
        row_sent = [sem(f"row_sent_{i}") for i in range(2)]
        t_loaded = [sem(f"t_loaded_{i}") for i in range(4)]
        t_sent = [sem(f"t_sent_{i}") for i in range(4)]
        t_xT_made = sem("t_xT_made")
        t_h_made = sem("t_h_made")
        t_hT_made = sem("t_hT_made")
        t_o_made = sem("t_o_made")
        t_xT_kept = sem("t_xT_kept")
        t_gelu = sem("t_gelu")
        t_h = sem("t_h")
        t_hn = sem("t_hn")
        t_y = sem("t_y")
        t_end = sem("t_end")
        t_z = sem("t_z")
        t_xb = sem("t_xb")
        t_rs1, t_rs2, t_rs3 = (sem(f"t_rs{i}") for i in (1, 2, 3))
        f_loaded = sem("f_loaded")
        f_stored = sem("f_stored")
        f_xT_made = sem("f_xT_made")
        f_logit_made = sem("f_logit_made")
        f_gate_made = sem("f_gate_made")
        f_up_made = sem("f_up_made")
        f_wB_made = sem("f_wB_made")
        f_o_made = sem("f_o_made")
        f_xT_kept = sem("f_xT_kept")
        f_exp = sem("f_exp")
        f_silu = sem("f_silu")
        f_wB_kept = sem("f_wB_kept")
        f_step = sem("f_step")
        f_keep = sem("f_keep")
        f_prod = sem("f_prod")
        f_hid = sem("f_hid")
        f_res = sem("f_res")
        f_ln = sem("f_ln")
        f_done = sem("f_done")
        f_xres = sem("f_xres")
        f_rstd = sem("f_rstd")
        rope_step = sem("rope_step")

        consts = [(ident, t["ident"]), (maskf, t["maskq"]), (cosb, t["cos"]), (sinb, t["sin"]), (wqkv, t["wqkv"]), (wo, t["wo"]), (gatew, t["gatew"]),
                  (wlog, t["wlog"]), (w7r, t["w7r"]), (ones, t["ones"]), (lower, t["lower"])]
        big = [(wa, t["wa0"]), (wb, t["wb0"]), (w7g, t["w7g"]), (w7u, t["w7u"]), (w7d, t["w7d"])]
        rows = [(bqkv[:, 0, :], t["b_qkv0"]), (bqkv[:, 1, :], t["b_qkv3"]), (bout[:, 0, :], t["b_o0"]),
                (bout[:, 2, :], t["b_o2"]), (bout[:, 3, :], t["b_o3"]), (scalew[:], t["scale_w"]),
                (gateb[:], t["gate_b"]), (n1g[:], t["n1_g"]), (n1b[:], t["n1_b"]),
                (n2g[:], t["n2_g"]), (n2b[:], t["n2_b"]), (blog[:], t["b_log"]), (descend[:], t["descend"]), (ascend[:], t["ascend"]),
                (iotas[:].rearrange("p e b -> p (e b)"), t["iotas"]), (slotn[:].rearrange("p s e -> p (s e)"), t["slotn"]),
                (keepmask[:].rearrange("p e b -> p (e b)"), t["keepmask"])]
        LOADED = 16 * (len(consts) + len(rows))

        with nc.Block() as block:
            @block.sync
            def _(sp):
                for dst, src in consts:
                    sp.dma_start(dst[:], src).then_inc(loaded, 16)
                for dst, src in rows:
                    sp.dma_start(dst, src.partition_broadcast(P)).then_inc(loaded, 16)
                sp.wait_ge(loaded, LOADED)

            @block.vector
            def _(dve):
                dve.wait_ge(loaded, LOADED)
                dve.tensor_copy(identb[:], ident[:])
                dve.tensor_copy(maskq[:], maskf[:].unsqueeze(1).broadcast_to([P, HG, P]))

            @block.gpsimd
            def _(pool):
                pool.memset(minus_half[:], -0.5).then_inc(init, 1)
                pool.memset(bout[:, 1, :], 0.0).then_inc(init, 1)
                pool.memset(qk[:], 0.0).then_inc(init, 1)
                for i in range(2):
                    pool.memset(v[i][:], 0.0).then_inc(init, 1)
                pool.wait_ge(init, 5)
                for i in range(2):
                    pool.memset(v[i][:, :, DK:DK + 1], 1.0).then_inc(init, 1)
                pool.wait_ge(init, 7)
                for s_, credit in ((x_stored[0], 16), (x_stored[1], 16), (t_y, 14), (e_xres, 1), (e_xT_made, KT), (e_masked, E), (e_res, GB), (e_done, GB), (e_stored, 16),
                                   (e_gate_kept, 1), (e_xT_kept, 1), (e_hid, 5), (e_o_made, 2), (e_gate_made, 2),
                                   (r_xT_kept, 1), (r_logit_kept, 1), (r_logit_made, 2),
                                   (f_xres, 1), (f_xT_made, KT), (f_res, GB), (f_done, GB), (f_stored, 16), (f_xT_kept, 1), (f_wB_kept, 1),
                                   (f_silu, 1), (f_hid, 3), (f_o_made, 2), (f_logit_made, 1), (f_wB_made, 1), (f_exp, 1)):
                    pool.sem_inc(s_, credit)

        def attention(stage, prefetch):
            scope = ExitStack()

            def sb(name, shape, dt=F32):
                return scope.enter_context(nc.sbuf_tensor(f"{name}_{stage}", shape, dt))

            x = [sb(f"x_{i}", [P, D]) for i in range(2)]
            cx = [sb(f"cx_{i}", [P, P]) for i in range(2)]
            xb = [sb(f"xb_{i}", [P, D]) for i in range(2)]
            xT = sb("xT", [P, KT + 1, P])
            qT = sb("qT", [P, NG, P])
            kdiag = sb("kdiag", [P, NG, HG, P])
            negmax = sb("negmax", [P, NG, HG])
            probs = [sb(f"probs_{g}", [P, HG, P]) for g in range(NG)]
            probsT = [sb(f"probsT_{i}", [P, HG, P]) for i in range(2)]
            oT = sb("oT", [P, NG, P])
            rden = sb("rden", [P, H])
            att = sb("att", [P, D])
            attT = sb("attT", [P, KT, P])
            y = sb("y", [P, D])
            stats = sb("stats", [P, 6])
            mv = sb("mv", [P, 2])
            var = sb("var", [P, 1])
            rstd = sb("rstd", [P, 1])
            xo = [sb(f"xo_{i}", [P, D]) for i in range(2)]
            tmpa = sb("tmpa", [P, 2 * D])
            tmpb = sb("tmpb", [P, 2 * D])
            lin = sb("lin", [P, H])
            tanh_q = sb("tanh_q", [P, H])
            fac = sb("fac", [P, H])
            gz = sb("gz", [P, D])
            gth = sb("gth", [P, D])
            gated = sb("gated", [P, D])
            TL, TR = TB[:, 0:D], TB[:, D:2 * D]

            def attention_sp(sp, stage):
                src, dst = X_IN[stage], X_OUT[stage]

                def load(a):
                    wait(sp, xT_made, a.n - 1)
                    wait(sp, xb_done, a.n - 1)
                    sp.dma_start(x[a.p][:], src[bass.ds(a.b, 1)].rearrange("a p n -> (a p) n")).then_inc(x_loaded[a.p], 16)
                    if stage == CROSS:
                        sp.dma_start(cx[a.p][:], t["ctx"][bass.ds(a.b, 1)].rearrange("a p n -> (a p) n")).then_inc(x_loaded[a.p], 16)

                def store(a):
                    sp.wait_ge(ln_done, a.n + 1)
                    sp.dma_start(dst[bass.ds(a.b, 1)].rearrange("a p n -> (a p) n"), xo[a.p][:]).then_inc(x_stored[a.p], 16)

                load(at(stage, 0))
                load(at(stage, 1))
                with sp.Fori(0, (NB - 2) // 2) as j:
                    for u in range(2):
                        load(At(stage, j * 2 + (2 + u), j + 1, u))
                        store(At(stage, j * 2 + u, j, u))
                store(at(stage, NB - 2))
                store(at(stage, NB - 1))
                for i in range(2):
                    sp.wait_ge(x_stored[i], 16 * (NB // 2) * (stage + 1) + 16)

            def x_count(a, stage):
                return (a.half + 1) * (32 if stage == CROSS else 16) + 16 * (NB // 2) * stage

            def keep_kT(copy, r):
                rows = slice(HP * r, HP * (r + 1))
                return copy(kdiag[rows, :, r, :], QKB[rows, :].rearrange("p (g k) -> p g k", g=NG))

            def attention_pe(pe, stage):
                def transposes(dst, src_of, n, inc):
                    for k in range(n):
                        ins = pe.transpose(dst[:, k * P:(k + 1) * P], src_of(k), ident[:])
                    ins.then_inc(inc, 1)

                def step(a, c, l):
                    if l:
                        pe.wait_ge(attT_kept, l.n + 1)
                        wait(pe, res_done, l.n)
                        w = gatew if stage == SCALED else wo[:, stage]
                        for k in range(KT):
                            ins = pe.matmul(TR, attT[:, k, :], w[:, k, :], start=k == 0, stop=k == KT - 1)
                        ins.then_inc(gate_made if stage == SCALED else proj_made, 1)
                    if a:
                        pe.wait_ge(x_loaded[a.p], x_count(a, stage))
                        wait(pe, qT_kept, a.n)
                        if stage == CROSS:
                            pe.transpose(VB[:, KT * P:(KT + 1) * P], cx[a.p][:], ident[:])
                        transposes(VB, lambda k: x[a.p][:, k * P:(k + 1) * P], KT, xT_made)
                    if c:
                        probs_to_keys(c, 0)
                        probs_to_keys(c, 1)
                    if a:
                        pe.wait_ge(xT_kept, a.n + 1)
                        for i in range(2):
                            wait(pe, kT_kept[i], 2 * a.n)
                        if stage == CROSS:
                            for k in range(KT):
                                pe.matmul(QKB[:, 0:D], xT[:, k, :], wqkv[:, stage, k, 0:D], start=k == 0, stop=k == KT - 1)
                            pe.matmul(QKB[:, D:2 * D], xT[:, KT, :], wqkv[:, stage, 0, D:2 * D], start=True, stop=True).then_inc(qkv_made, 1)
                            pe.matmul(VB[:, 0:D], xT[:, KT, :], wqkv[:, stage, 0, 2 * D:3 * D], start=True, stop=True).then_inc(qkv_made, 1)
                        else:
                            for k in range(KT):
                                ins = pe.matmul(QKB[:], xT[:, k, :], wqkv[:, stage, k, 0:2 * D], start=k == 0, stop=k == KT - 1)
                            ins.then_inc(qkv_made, 1)
                            for k in range(KT):
                                ins = pe.matmul(VB[:, 0:D], xT[:, k, :], wqkv[:, stage, k, 2 * D:3 * D], start=k == 0, stop=k == KT - 1)
                            ins.then_inc(qkv_made, 1)
                    if l and stage == SCALED:
                        pe.wait_ge(gated_done, l.b + 1)
                        transposes(TL, lambda k: gated[:, k * P:(k + 1) * P], KT, gatedT_made)
                    if c:
                        weighted_values(c, 0)
                        probs_to_keys(c, 2)
                    if l and stage == SCALED:
                        pe.wait_ge(gatedT_kept, l.b + 1)
                        for k in range(KT):
                            ins = pe.matmul(TR, attT[:, k, :], wo[:, stage, k, :], start=k == 0, stop=k == KT - 1)
                        ins.then_inc(proj_made, 1)
                    if a:
                        pe.wait_ge(qk_kept, a.n + 1)
                        transposes(QKB, lambda g: qk[:, 1, HG * g:HG * (g + 1), :], NG, qkT_made)
                        pe.wait_ge(v_kept, a.n + 1)
                        transposes(VB, lambda g: qk[:, 0, HG * g:HG * (g + 1), :], NG, qkT_made)
                    if c:
                        weighted_values(c, 1)
                        probs_to_keys(c, 3)
                        weighted_values(c, 2)
                        weighted_values(c, 3)
                    if a:
                        scores(a, 0)
                        scores(a, 1)
                    if c:
                        pe.wait_ge(oT_kept, c.n + 1)
                        wait(pe, res_done, c.n)
                        transposes(TB, lambda k: oT[:, k, :], NG, o_made)
                    if a:
                        scores(a, 2)
                    if c:
                        pe.wait_ge(att_kept, c.n + 1)
                        transposes(TL, lambda k: att[:, k * P:(k + 1) * P], KT, attT_made)
                    if a:
                        scores(a, 3)

                def scores(a, g):
                    if g == 0:
                        pe.wait_ge(qT_kept, a.n + 1)
                        for i in range(2):
                            pe.wait_ge(kT_kept[i], 2 * a.n + 2)
                    wait(pe, probs_kept, 4 * a.n + g - 1)
                    s = SB[g % 2]
                    if stage == CAUSAL:
                        pe.matmul(s[:], identb[:], maskq[:], start=True, stop=False)
                    pe.matmul(s[:], qT[:, g, :], kdiag[:, g], start=stage != CAUSAL, stop=True).then_inc(s_made, 1)

                def probs_to_keys(c, g):
                    pe.wait_ge(probs_kept, 4 * c.n + g + 1)
                    wait(pe, probsT_kept, 4 * c.n + g - 1)
                    transposes(PTB[g % 2], lambda r: probs[g][:, r, :], HG, probsT_made)

                def weighted_values(c, g):
                    if g == 0:
                        wait(pe, oT_kept, c.n)
                        pe.wait_ge(v_kept, c.n + 1)
                    pe.wait_ge(probsT_kept, 4 * c.n + g + 1)
                    for r in range(HG):
                        ins = pe.matmul(OTB[HP * r:HP * (r + 1), g * P:(g + 1) * P], v[c.p][:, HG * g + r, :],
                                        probsT[g % 2][:, r, :], start=True, stop=True, skip_group_check=True)
                    ins.then_inc(av_made, 1)

                attention_steps(pe, stage, step)

            def attention_act(act, stage):
                def softmax_numerators(a, g):
                    act.wait_ge(max_kept, 4 * a.n + g + 1)
                    wait(act, probsT_made, 4 * a.n + g - 3)
                    for r in range(HG):
                        ins = act.activation(probs[g][:, r, :], SB[g % 2][:, r * P:(r + 1) * P], ACT.Exp, bias=negmax[:, g, r:r + 1])
                    ins.then_inc(probs_kept, 1)

                def step(a, c, l):
                    if a:
                        act.wait_ge(xT_made, a.n + 1)
                        wait(act, qkv_made, 2 * a.n)
                        n = KT + 1 if stage == CROSS else KT
                        act.copy(xT[:, 0:n, :], VB[:, 0:n * P]).then_inc(xT_kept, 1)
                    if l and stage == SCALED:
                        act.wait_ge(gz_done, l.b + 1)
                        wait(act, gated_done, l.b)
                        act.activation(gth[:], gz[:], ACT.Tanh, scale=0.5).then_inc(gth_done, 1)
                        act.wait_ge(gatedT_made, l.b + 1)
                        act.mul(attT[:], TL, 0.5).then_inc(gatedT_kept, 1)
                    if a and stage == SCALED:
                        act.wait_ge(lin_step, 2 * a.b + 2)
                        wait(act, fac_done, a.b)
                        act.activation(tanh_q[:], lin[:], ACT.Tanh, scale=0.5).then_inc(tanh_done, 1)
                    if a:
                        act.wait_ge(qkT_made, 2 * a.n + 1)
                        wait(act, s_made, 4 * a.n)
                        for r in range(HG // 2):
                            keep_kT(act.copy, r).then_inc(kT_kept[0], 1)
                        act.wait_ge(qkT_made, 2 * a.n + 2)
                        act.mul(qT[:], VB[:], float(DK) ** -0.5).then_inc(qT_kept, 1)
                    if c:
                        act.wait_ge(av_made, 4 * c.n + 4)
                        wait(act, o_made, c.n)
                        act.copy(oT[:], OTB[:]).then_inc(oT_kept, 1)
                    if a:
                        softmax_numerators(a, 0)
                        softmax_numerators(a, 1)
                    if c:
                        act.wait_ge(attT_made, c.n + 1)
                        wait(act, proj_made, c.n)
                        act.copy(attT[:], TL).then_inc(attT_kept, 1)
                    if a:
                        softmax_numerators(a, 2)
                        softmax_numerators(a, 3)

                act.wait_ge(kdiag_cleared, stage + 1)
                attention_steps(act, stage, step)

            def attention_dve(dve, stage):
                def step(a, c, l):
                    if l and stage == SCALED:
                        dve.wait_ge(gate_made, l.b + 1)
                        wait(dve, gth_done, l.b)
                        dve.tensor_tensor(gz[:], TR, gateb[:], ALU.add).then_inc(gz_done, 1)
                    if c:
                        keep_probs(c, 0)
                    if l and stage == SCALED:
                        dve.wait_ge(gth_done, l.b + 1)
                        wait(dve, gatedT_made, l.b)
                        dve.scalar_tensor_tensor(gated[:], gth[:], 1.0, att[:], ALU.add, ALU.mult).then_inc(gated_done, 1)
                    if c:
                        keep_probs(c, 1)
                    if l and stage != SCALED:
                        statistics(l)
                    if a:
                        dve.wait_ge(qkv_made, 2 * a.n + 1)
                        wait(dve, qkT_made, 2 * a.n)
                        heads = qk[:, :, :, 0:DK]
                        made = QKB[:].rearrange("p (a h d) -> p a h d", a=2, h=H)
                        if stage == CAUSAL or stage == CROSS:
                            bias = bqkv[:, 0 if stage == CAUSAL else 1, 0:2 * D].rearrange("p (a h d) -> p a h d", a=2, h=H)
                            dve.tensor_tensor(heads, made, bias, ALU.add).then_inc(qk_kept, 1)
                            keep_values(a)
                        if stage == SCALED:
                            dve.tensor_tensor(tmpa[:, 0:D], QKB[:, 0:D], scalew[:], ALU.mult).then_inc(lin_step, 1)
                            dve.wait_ge(lin_step, 2 * a.b + 1)
                            dve.tensor_reduce(lin[:], tmpa[:, 0:D].rearrange("p (h d) -> p h d", h=H), AX.X, ALU.add).then_inc(lin_step, 1)
                            dve.tensor_copy(qk[:, 1, :, 0:DK], QKB[:, D:2 * D].rearrange("p (h d) -> p h d", h=H))
                            keep_values(a)
                            dve.wait_ge(tanh_done, a.b + 1)
                            dve.tensor_scalar(fac[:], tanh_q[:], 1.0, None, ALU.add).then_inc(fac_done, 1)
                            dve.wait_ge(fac_done, a.b + 1)
                            dve.tensor_tensor(qk[:, 0, :, 0:DK], QKB[:, 0:D].rearrange("p (h d) -> p h d", h=H),
                                              fac[:].unsqueeze(2).broadcast_to([P, H, DK]), ALU.mult).then_inc(qk_kept, 1)
                        if stage == ROTARY:
                            made4 = QKB[:].rearrange("p (h c d) -> p h c d", h=2 * H, c=2)
                            tb = tmpb[:].rearrange("p (h c d) -> p h c d", h=2 * H, c=2)
                            half = DK // 2
                            dve.tensor_tensor(tmpa[:].rearrange("p (h d) -> p h d", d=half), QKB[:].rearrange("p (h d) -> p h d", d=half),
                                              cosb[:].unsqueeze(1).broadcast_to([P, 4 * H, half]), ALU.mult).then_inc(rope_step, 1)
                            for i in range(2):
                                dve.tensor_tensor(tb[:, :, i, :], made4[:, :, 1 - i, :],
                                                  sinb[:, i, :].unsqueeze(1).broadcast_to([P, 2 * H, half]), ALU.mult).then_inc(rope_step, 1)
                            dve.wait_ge(rope_step, 3 * a.b + 3)
                            dve.tensor_tensor(qk[:].rearrange("p a h d -> p (a h) d")[:, :, 0:DK], tmpa[:].rearrange("p (h d) -> p h d", d=DK),
                                              tmpb[:].rearrange("p (h d) -> p h d", d=DK), ALU.add).then_inc(qk_kept, 1)
                            keep_values(a)
                    if c:
                        keep_probs(c, 2)
                    if a:
                        dve.wait_ge(qkT_made, 2 * a.n + 1)
                        wait(dve, s_made, 4 * a.n)
                        dve.sem_inc(passed, 1)
                        for r in range(HG // 2, HG):
                            keep_kT(dve.tensor_copy, r).then_inc(kT_kept[1], 1)
                    if c:
                        keep_probs(c, 3)
                    if l and stage == SCALED:
                        statistics(l)
                    if a:
                        row_max(a, 0)
                        row_max(a, 1)
                    if l:
                        normalise(l)
                    if c:
                        dve.wait_ge(o_made, c.n + 1)
                        made = TB[:].rearrange("p (h d) -> p h d", h=H)
                        wait(dve, att_kept, c.n)
                        dve.reciprocal(rden[:], made[:, :, DK]).then_inc(rden_done, 1)
                        dve.wait_ge(rden_done, c.n + 1)
                        wait(dve, attT_made, c.n)
                        if stage == SCALED:
                            wait(dve, gated_done, c.b)
                        dve.tensor_tensor(att[:].rearrange("p (h d) -> p h d", h=H), made[:, :, 0:DK],
                                          rden[:].unsqueeze(2).broadcast_to([P, H, DK]), ALU.mult).then_inc(att_kept, 1)
                    if a:
                        row_max(a, 2)
                        row_max(a, 3)

                def keep_values(a):
                    dve.wait_ge(qkv_made, 2 * a.n + 2)
                    wait(dve, av_made, 4 * a.n - 4)
                    made = VB[:, 0:D].rearrange("p (h d) -> p h d", h=H)
                    if stage == CAUSAL or stage == CROSS:
                        bias = bqkv[:, 0 if stage == CAUSAL else 1, 2 * D:3 * D].rearrange("p (h d) -> p h d", h=H)
                        dve.tensor_tensor(v[a.p][:, :, 0:DK], made, bias, ALU.add).then_inc(v_kept, 1)
                    else:
                        dve.tensor_copy(v[a.p][:, :, 0:DK], made).then_inc(v_kept, 1)

                def keep_probs(c, g):
                    dve.wait_ge(probsT_made, 4 * c.n + g + 1)
                    wait(dve, av_made, 4 * c.n + g - 1)
                    dve.tensor_copy(probsT[g % 2][:].rearrange("p r q -> p (r q)"), PTB[g % 2][:]).then_inc(probsT_kept, 1)

                def row_max(a, g):
                    dve.wait_ge(s_made, 4 * a.n + g + 1)
                    dve.tensor_reduce(negmax[:, g, :], SB[g % 2][:].rearrange("p (r k) -> p r k", r=HG),
                                      AX.X, ALU.max, negate=True).then_inc(max_kept, 1)

                def statistics(l):
                    dve.wait_ge(proj_made, l.n + 1)
                    dve.wait_ge(xb_done, l.n + 1)
                    wait(dve, ln_done, l.n)
                    dve.tensor_tensor(y[:], TR, xb[l.p][:], ALU.add).then_inc(res_done, 1)
                    dve.wait_ge(res_done, l.n + 1)
                    dve.bn_stats(stats[:], y[:]).then_inc(ln_step, 1)
                    dve.wait_ge(ln_step, 3 * l.n + 1)
                    dve.sem_inc(passed, 1)
                    dve.bn_aggr(mv[:], stats[:]).then_inc(ln_step, 1)
                    dve.wait_ge(ln_step, 3 * l.n + 2)
                    dve.tensor_scalar(var[:], mv[:, 1:2], EPS, None, ALU.add).then_inc(ln_step, 1)

                def normalise(l):
                    dve.wait_ge(rstd_done, l.n + 1)
                    stored = l.half * 16 + 16 * (NB // 2) * stage + 16
                    wait(dve, x_stored[l.p], stored)
                    if stage == SCALED:
                        dve.tensor_scalar(tmpb[:, 0:D], y[:], mv[:, 0:1], rstd[:], ALU.subtract, ALU.mult).then_inc(n1_step, 1)
                        dve.wait_ge(n1_step, 2 * l.b + 1)
                        dve.tensor_tensor(tmpb[:, D:2 * D], tmpb[:, 0:D], n1g[:], ALU.mult).then_inc(n1_step, 1)
                        dve.wait_ge(n1_step, 2 * l.b + 2)
                        dve.tensor_tensor(xo[l.p][:], tmpb[:, D:2 * D], n1b[:], ALU.add).then_inc(ln_done, 1)
                    else:
                        dve.tensor_scalar(xo[l.p][:], y[:], mv[:, 0:1], rstd[:], ALU.subtract, ALU.mult).then_inc(ln_done, 1)

                dve.memset(kdiag[:].rearrange("p g r k -> p (g r k)"), 0.0).then_inc(kdiag_cleared, 1)
                dve.wait_ge(kdiag_cleared, stage + 1)
                attention_steps(dve, stage, step)

            def attention_pool(pool, stage):
                def step(a, c, l):
                    if a:
                        pool.wait_ge(x_loaded[a.p], x_count(a, stage))
                        wait(pool, res_done, a.n - 1)
                        pool.tensor_tensor(xb[a.p][:], x[a.p][:], bout[:, stage, :], ALU.add).then_inc(xb_done, 1)
                    if l:
                        pool.wait_ge(ln_step, 3 * l.n + 3)
                        wait(pool, ln_done, l.n)
                        pool.tensor_tensor(rstd[:], var[:], minus_half[:, 0:1], ALU.pow).then_inc(rstd_done, 1)

                attention_steps(pool, stage, step)

            with nc.Block() as block:
                @block.sync
                def _(sp):
                    attention_sp(sp, stage)

                @block.tensor
                def _(pe):
                    attention_pe(pe, stage)

                @block.scalar
                def _(act):
                    for dst, src in prefetch:
                        act.dma_start(dst[:], src).then_inc(big_loaded, 16)
                    attention_act(act, stage)

                @block.vector
                def _(dve):
                    attention_dve(dve, stage)

                @block.gpsimd
                def _(pool):
                    attention_pool(pool, stage)

            scope.close()

        R_ONEHOT, R_DIFF = 12, 13
        Y_C = 14
        MASK_C, GATE_C, HID_C, O_C = 2, 1, 5, 2

        def experts0():
            scope = ExitStack()

            def sb(name, shape, dt=F32):
                return scope.enter_context(nc.sbuf_tensor(name, shape, dt))

            xg = sb("xg", [P, GB, D])
            xres = sb("xres", [P, GB, D])
            xgT = sb("xgT", [P, KT, GB * P])
            ctxg = sb("ctxg", [P, GB, P])
            itokg = sb("itokg", [P, GB, P], I32)
            masked = [sb(f"masked_{i}", [P, GB * P]) for i in range(2)]
            gateB = [sb(f"gateB_{i}", [P, GB * P]) for i in range(2)]
            hid = [sb(f"hid_{i}", [P, HC, GB * P]) for i in range(2)]
            yg = sb("yg", [P, GB, D])
            xog = sb("xog", [P, GB, D])
            stg = sb("stg", [P, GB, 6])
            mvg = sb("mvg", [P, GB, 2])
            varg = sb("varg", [P, GB])
            rstdg = sb("rstdg", [P, GB])

            def group(ap, g):
                return ap[bass.ds(g * GB, GB)].rearrange("b p n -> p b n")

            with nc.Block() as block:
                @block.sync
                def _(sp):
                    def load(g):
                        sp.wait_ge(e_xres, g + 1)
                        sp.wait_ge(e_xT_made, g * KT + KT)
                        sp.dma_start(xg[:], group(x1, g)).then_inc(e_loaded, 16)
                        sp.wait_ge(e_masked, g * E + E)
                        sp.dma_start(ctxg[:], group(t["ctx"], g)).then_inc(e_loaded, 16)
                        sp.dma_start(itokg[:], group(t["itok"], g)).then_inc(e_loaded, 16)

                    def store(g):
                        sp.wait_ge(e_done, g * GB + 2 * GB)
                        sp.dma_start(group(x2, g), xog[:]).then_inc(e_stored, 16)

                    load(0)
                    with sp.Fori(0, NGR - 1) as g:
                        load(g + 1)
                        store(g)
                    store(NGR - 1)
                    sp.wait_ge(e_stored, 16 * (NGR + 1))

                @block.gpsimd
                def _(pool):
                    with pool.Fori(0, NGR) as g:
                        pool.wait_ge(e_loaded, g * 48 + 48)
                        pool.wait_ge(e_res, g * GB + GB)
                        pool.sem_inc(passed, 1)
                        pool.tensor_copy(xres[:], xg[:]).then_inc(e_xres, 1)
                        pool.wait_ge(e_ln, g * 6 + 6)
                        pool.wait_ge(e_done, g * GB + GB)
                        pool.tensor_tensor(rstdg[:], varg[:], minus_half[:], ALU.pow).then_inc(e_rstd, 1)

                @block.tensor
                def _(pe):
                    pe.wait_ge(big_loaded, 16 * len(big))
                    with pe.Fori(0, NGR) as g:
                        def gates(e):
                            pe.wait_ge(e_masked, g * E + (E + e + 1))
                            pe.wait_ge(e_gate_kept, g * E + (e + 1))
                            pe.matmul(bank[6][:], ones[:], masked[e % 2][:], start=True, stop=True).then_inc(e_gate_made, 1)

                        def first(e):
                            for c in range(HC):
                                z = bank[4 + c % 2]
                                pe.wait_ge(e_hid, g * (E * HC) + (e * HC + c - 1 + HID_C))
                                for k in range(KT):
                                    ins = pe.matmul(z[:], wa[:, k, e, c * P:(c + 1) * P], xgT[:, k, :], start=k == 0, stop=k == KT - 1)
                                ins.then_inc(e_z_made, 1)

                        def second(e):
                            if e == 0:
                                pe.wait_ge(e_res, g * GB + GB)
                            pe.wait_ge(e_hid, g * (E * HC) + (e * HC + HC + HID_C))
                            for b in range(GB):
                                for c in range(HC):
                                    ins = pe.matmul(bank[b][:, 0:D], hid[e % 2][:, c, b * P:(b + 1) * P], wb[:, e, c, :],
                                                    start=e == 0 and c == 0, stop=e == E - 1 and c == HC - 1)
                            ins.then_inc(e_o_made, 1)

                        pe.wait_ge(e_loaded, g * 48 + 48)
                        for k in range(KT):
                            pe.wait_ge(e_xT_kept, g * KT + (k + 1))
                            for b in range(GB):
                                ins = pe.transpose(bank[7][:, b * P:(b + 1) * P], xg[:, b, k * P:(k + 1) * P], ident[:])
                            ins.then_inc(e_xT_made, 1)
                        gates(0)
                        pe.wait_ge(e_xT_kept, g * KT + (KT + 1))
                        for e in range(E):
                            first(e)
                            if e + 1 < E:
                                gates(e + 1)
                            if e:
                                second(e - 1)
                        second(E - 1)

                @block.scalar
                def _(act):
                    with act.Fori(0, NGR) as g:
                        for k in range(KT):
                            act.wait_ge(e_xT_made, g * KT + (k + 1 + KT))
                            act.wait_ge(e_o_made, g * E + O_C)
                            act.copy(xgT[:, k, :], bank[7][:]).then_inc(e_xT_kept, 1)
                        for e in range(E):
                            act.wait_ge(e_gate_made, g * E + (e + 1 + MASK_C))
                            act.wait_ge(e_hid, g * (E * HC) + (e * HC - HC + HID_C))
                            act.copy(gateB[e % 2][:], bank[6][:]).then_inc(e_gate_kept, 1)

                @block.vector
                def _(dve):
                    with dve.Fori(0, NGR) as g:
                        def mask(e):
                            if e == 0:
                                dve.wait_ge(e_loaded, g * 48 + 48)
                            dve.wait_ge(e_gate_made, g * E + (e - 1 + MASK_C))
                            dve.scalar_tensor_tensor(masked[e % 2][:], itokg[:].rearrange("p b s -> p (b s)"), float(e),
                                                     ctxg[:].rearrange("p b s -> p (b s)"), ALU.is_equal, ALU.mult).then_inc(e_masked, 1)

                        mask(0)
                        mask(1)
                        for e in range(E):
                            dve.wait_ge(e_gate_kept, g * E + (e + 1 + GATE_C))
                            dve.wait_ge(e_o_made, g * E + (e - 1 + O_C))
                            for c in range(HC):
                                dve.wait_ge(e_z_made, g * (E * HC) + (e * HC + c + 1))
                                dve.scalar_tensor_tensor(hid[e % 2][:, c, :], bank[4 + c % 2][:], 0.0, gateB[e % 2][:],
                                                         ALU.max, ALU.mult).then_inc(e_hid, 1)
                            if e + 2 < E:
                                mask(e + 2)
                        dve.wait_ge(e_o_made, g * E + (E + O_C))
                        dve.wait_ge(e_xres, g + 2)
                        for b in range(GB):
                            dve.tensor_tensor(yg[:, b, :], bank[b][:, 0:D], xres[:, b, :], ALU.add).then_inc(e_res, 1)
                        for b in range(GB):
                            dve.wait_ge(e_res, g * GB + (b + 1 + GB))
                            dve.bn_stats(stg[:, b, :], yg[:, b, :]).then_inc(e_ln, 1)
                        dve.wait_ge(e_ln, g * 6 + 4)
                        dve.sem_inc(passed, 1)
                        for b in range(GB):
                            ins = dve.bn_aggr(mvg[:, b, :], stg[:, b, :])
                        ins.then_inc(e_ln, 1)
                        dve.wait_ge(e_ln, g * 6 + 5)
                        dve.tensor_scalar(varg[:], mvg[:, :, 1], EPS, None, ALU.add).then_inc(e_ln, 1)
                        dve.wait_ge(e_rstd, g + 1)
                        dve.wait_ge(e_stored, g * 16 + 16)
                        for b in range(GB):
                            dve.tensor_scalar(xog[:, b, :], yg[:, b, :], mvg[:, b, 0:1], rstdg[:, b:b + 1],
                                              ALU.subtract, ALU.mult).then_inc(e_done, 1)

            scope.close()

        def routing(posu, meta, se):
            scope = ExitStack()

            def sb(name, shape, dt=F32):
                return scope.enter_context(nc.sbuf_tensor(name, shape, dt))

            xin = [sb(f"r_xin_{i}", [P, GB, D]) for i in range(2)]
            xinT = [sb(f"r_xinT_{i}", [P, KT, GB * P]) for i in range(2)]
            lg = sb("lg", [P, NB, E])
            fill = sb("fill", [P, ROW])

            with nc.Block() as block:
                @block.sync
                def _(sp):
                    def load(g, i):
                        sp.dma_start(xin[i][:], xr[bass.ds(g * GB, GB)].rearrange("b p n -> p b n")).then_inc(r_loaded[i], 16)

                    load(0, 0)
                    load(1, 1)
                    with sp.Fori(0, NGR // 2 - 1) as j:
                        for u in range(2):
                            sp.wait_ge(r_xT_made, j * 4 + (2 * u + 2))
                            load(j * 2 + (2 + u), u)

                @block.gpsimd
                def _(pool):
                    pool.memset(fill[:], 0.0).then_inc(r_meta, 1)
                    pool.wait_ge(r_meta, 1)
                    pool.memset(fill[:].bitcast(I32)[:, 2 * D + 1:2 * D + 2], TOK).then_inc(r_meta, 1)
                    pool.wait_ge(r_meta, 2)
                    pool.dma_start(routed.rearrange("(s p) r -> p s r", p=P),
                                   fill[:].unsqueeze(1).broadcast_to([P, SLOTS, ROW])).then_inc(filled, 16)
                    pool.memset(meta[:], 0.0).then_inc(r_meta, 1)
                    pool.wait_ge(r_meta, 3)
                    pool.iota(meta[:].bitcast(I32)[:, :, 1], pattern=[[P, NB]], base=0, channel_multiplier=1).then_inc(r_meta, 1)
                    pool.wait_ge(filled, 16)

                @block.tensor
                def _(pe):
                    with pe.Fori(0, NGR // 2) as j:
                        for u in range(2):
                            pe.wait_ge(r_loaded[u], j * 16 + 16)
                            pe.wait_ge(r_xT_kept, j * 4 + (2 * u + 1))
                            for k in range(KT):
                                for b in range(GB):
                                    ins = pe.transpose(bank[2 * u + k][:, b * P:(b + 1) * P], xin[u][:, b, k * P:(k + 1) * P], ident[:])
                                ins.then_inc(r_xT_made, 1)
                            pe.wait_ge(r_xT_kept, j * 4 + (2 * u + 3))
                            pe.wait_ge(r_logit_kept, j * 2 + (u + 1))
                            for b in range(GB):
                                for k in range(KT):
                                    ins = pe.matmul(bank[4 + u][:, b * E:(b + 1) * E], xinT[u][:, k, b * P:(b + 1) * P], wlog[:, k, :],
                                                    start=k == 0, stop=k == KT - 1)
                            ins.then_inc(r_logit_made, 1)

                @block.scalar
                def _(act):
                    with act.Fori(0, NGR // 2) as j:
                        for u in range(2):
                            for k in range(KT):
                                act.wait_ge(r_xT_made, j * 4 + (2 * u + k + 1))
                                act.wait_ge(r_logit_made, j * 2 + (u + 1))
                                act.copy(xinT[u][:, k, :], bank[2 * u + k][:]).then_inc(r_xT_kept, 1)

                @block.vector
                def _(dve):
                    with dve.Fori(0, NGR // 2) as j:
                        for u in range(2):
                            dve.wait_ge(r_logit_made, j * 2 + (u + 3))
                            dve.tensor_tensor(lg[:, bass.ds((j * 2 + u) * GB, GB), :], bank[4 + u][:, 0:GB * E].rearrange("p (b e) -> p b e", b=GB),
                                              blog[:].unsqueeze(1).broadcast_to([P, GB, E]), ALU.add).then_inc(r_logit_kept, 1)

            def row(name, shape=(NB, E)):
                return sb("r_" + name, [P, *shape])

            v1, v2, c1, c2, chosen = (row(n, (NB,)) for n in ("v1", "v2", "c1", "c2", "chosen"))
            diff, e2, den, r1, r2 = (row(n, (NB,)) for n in ("diff", "e2", "den", "r1", "r2"))
            eq, cand, hit, lg2, eq2, cand2 = (row(n) for n in ("eq", "cand", "hit", "lg2", "eq2", "cand2"))
            onehot, tot, upto, full, p1, p2, p3, p4 = (row(n, (E, NB)) for n in ("onehot", "tot", "upto", "full", "p1", "p2", "p3", "p4"))
            tiles, cum, base0, base = (row(n, (E,)) for n in ("tiles", "cum", "base0", "base"))
            post, started, sef = row("post", (NB,)), row("started", (SLOTS, E)), row("sef", (SLOTS,))
            flat = lambda a: a[:].rearrange("p a b -> p (a b)")
            over = lambda a: a[:].unsqueeze(2).broadcast_to([P, NB, E])
            down = descend[:].unsqueeze(1).broadcast_to([P, NB, E])

            with nc.Block() as block:
                @block.vector
                def _(dve):
                    steps = [0]

                    def link(ins):
                        steps[0] += 1
                        ins.then_inc(r_step, 1)
                        dve.wait_ge(r_step, steps[0])

                    link(dve.tensor_reduce(v1[:], lg[:], AX.X, ALU.max))
                    link(dve.tensor_tensor(eq[:], lg[:], over(v1), ALU.is_equal))
                    link(dve.tensor_tensor(cand[:], eq[:], down, ALU.mult))
                    link(dve.tensor_reduce(c1[:], cand[:], AX.X, ALU.max))
                    link(dve.tensor_tensor(hit[:], down, over(c1), ALU.is_equal))
                    link(dve.scalar_tensor_tensor(flat(lg2), flat(hit), -BIG, flat(lg), ALU.mult, ALU.add))
                    link(dve.tensor_reduce(v2[:], lg2[:], AX.X, ALU.max))
                    link(dve.tensor_tensor(eq2[:], lg2[:], over(v2), ALU.is_equal))
                    link(dve.tensor_tensor(cand2[:], eq2[:], down, ALU.mult))
                    link(dve.tensor_reduce(c2[:], cand2[:], AX.X, ALU.max))
                    link(dve.tensor_tensor(chosen[:], c1[:], c2[:], ALU.min))
                    link(dve.tensor_tensor(onehot[:].rearrange("p e b -> p b e"), down, over(chosen), ALU.is_equal))
                    assert steps[0] == R_ONEHOT
                    link(dve.tensor_tensor(diff[:], v2[:], v1[:], ALU.subtract))
                    assert steps[0] == R_DIFF
                    dve.wait_ge(r_exp, 1)
                    link(dve.tensor_scalar(den[:], e2[:], 1.0, None, ALU.add))
                    link(dve.reciprocal(r1[:], den[:]))
                    link(dve.tensor_tensor(r2[:], e2[:], r1[:], ALU.mult))
                    dve.wait_ge(r_meta, 4)
                    link(dve.tensor_tensor(meta[:, :, 0], r1[:], r2[:], ALU.add))
                    dve.wait_ge(r_rank, 2)
                    link(dve.tensor_copy(flat(tot), bank[1][:, 0:E * NB]))
                    link(dve.tensor_tensor_scan(flat(upto), flat(keepmask), flat(tot), 0.0, ALU.mult, ALU.add))
                    link(dve.tensor_tensor(full[:], upto[:, :, NB - 1].unsqueeze(2).broadcast_to([P, E, NB]), iotas[:], ALU.is_gt))
                    link(dve.tensor_reduce(tiles[:], full[:], AX.X, ALU.add))
                    link(dve.tensor_tensor_scan(cum[:], ones[:, 0:E], tiles[:], 0.0, ALU.mult, ALU.add))
                    link(dve.tensor_tensor(base0[:], cum[:], tiles[:], ALU.subtract))
                    link(dve.tensor_scalar(base[:], base0[:], float(P), None, ALU.mult))
                    link(dve.tensor_tensor(flat(p1), bank[0][:, 0:E * NB], flat(upto), ALU.add))
                    link(dve.tensor_tensor(flat(p2), flat(p1), flat(tot), ALU.subtract))
                    link(dve.tensor_tensor(p3[:], p2[:], base[:].unsqueeze(2).broadcast_to([P, E, NB]), ALU.add))
                    link(dve.tensor_tensor(flat(p4), flat(p3), flat(onehot), ALU.mult))
                    link(dve.tensor_reduce(post[:], p4[:].rearrange("p e b -> p b e"), AX.X, ALU.add))
                    link(dve.tensor_copy(posu[:], post[:]))
                    link(dve.tensor_tensor(started[:], slotn[:], cum[:].unsqueeze(1).broadcast_to([P, SLOTS, E]), ALU.is_ge))
                    link(dve.tensor_reduce(sef[:], started[:], AX.X, ALU.add))
                    link(dve.tensor_scalar(se[:], sef[:], float(E - 1), None, ALU.min))

                @block.scalar
                def _(act):
                    act.wait_ge(r_step, R_DIFF)
                    act.activation(e2[:], diff[:], ACT.Exp).then_inc(r_exp, 1)

                @block.tensor
                def _(pe):
                    pe.wait_ge(r_step, R_ONEHOT)
                    pe.matmul(bank[0][:, 0:E * NB], lower[:], flat(onehot), start=True, stop=True).then_inc(r_rank, 1)
                    pe.matmul(bank[1][:, 0:E * NB], ones[:], flat(onehot), start=True, stop=True).then_inc(r_rank, 1)

            rowt = [sb(f"rowt_{i}", [P, ROW]) for i in range(2)]
            idx = [sb(f"idx_{i}", [P, 1], U32) for i in range(2)]
            with nc.Block() as block:
                @block.sync
                def _(sp):
                    def load(b, i):
                        sp.dma_start(rowt[i][:, 0:D], xr[bass.ds(b, 1)].rearrange("a p n -> (a p) n")).then_inc(row_loaded[i], 16)
                        sp.dma_start(rowt[i][:, D:2 * D], x2[bass.ds(b, 1)].rearrange("a p n -> (a p) n")).then_inc(row_loaded[i], 16)

                    load(0, 0)
                    load(1, 1)
                    with sp.Fori(0, NB // 2 - 1) as j:
                        for u in range(2):
                            sp.wait_ge(row_sent[u], j * 16 + 16)
                            load(j * 2 + (2 + u), u)

                @block.vector
                def _(dve):
                    def put(b, i):
                        dve.tensor_copy(rowt[i][:, 2 * D:ROW].unsqueeze(1), meta[:, bass.ds(b, 1), :]).then_inc(row_meta, 1)
                        dve.tensor_copy(idx[i][:], posu[:, bass.ds(b, 1)]).then_inc(row_meta, 1)

                    put(0, 0)
                    put(1, 1)
                    with dve.Fori(0, NB // 2 - 1) as j:
                        for u in range(2):
                            dve.wait_ge(row_sent[u], j * 16 + 16)
                            dve.sem_inc(passed, 1)
                            put(j * 2 + (2 + u), u)

                @block.gpsimd
                def _(pool):
                    with pool.Fori(0, NB // 2) as j:
                        for u in range(2):
                            pool.wait_ge(row_loaded[u], j * 32 + 32)
                            pool.wait_ge(row_meta, j * 4 + (2 * u + 2))
                            pool.sem_inc(passed, 1)
                            pool.indirect_dma_start(out=routed[:, :], out_offset=bass.IndirectOffsetOnAxis(ap=idx[u][:, 0:1], axis=0),
                                                    in_=rowt[u][:], in_offset=None).then_inc(row_sent[u], 16)
                    for i in range(2):
                        pool.wait_ge(row_sent[i], 16 * (NB // 2))
            scope.close()

        def slots(se):
            scope = ExitStack()

            def sb(name, shape, dt=F32):
                return scope.enter_context(nc.sbuf_tensor(name, shape, dt))

            rowt = [sb(f"t_row_{i}", [P, ROW]) for i in range(4)]
            b1t = [sb(f"t_b1_{i}", [P, HID]) for i in range(4)]
            b2t = [sb(f"t_b2_{i}", [P, D]) for i in range(4)]
            part = [sb(f"t_par_{i}", [P, 2 * HC + 1]) for i in range(4)]
            xTt = sb("t_xT", [P, KT, P])
            hb = sb("t_hb", [P, HID])
            hn = [sb(f"t_hn_{i}", [P, HID]) for i in range(2)]
            hT = sb("t_hT", [P, HC, P])
            st, st2, st3 = (sb(f"t_st_{i}", [P, 6]) for i in range(3))
            mvt, mv2, mv3 = (sb(f"t_mv_{i}", [P, 2]) for i in range(3))
            var1, var2, var3 = (sb(f"t_var_{i}", [P, 1]) for i in range(3))
            rs1, rs2, rs3 = (sb(f"t_rs_{i}", [P, 1]) for i in range(3))
            ot, sel, res, nrm, ng, w3 = (sb(f"t_{n}", [P, D]) for n in ("ot", "sel", "res", "nrm", "ng", "w3"))
            token = [sb(f"t_token_{i}", [P, 1], U32) for i in range(4)]
            xpb = sb("t_xpb", [P, D])
            z = [sb(f"t_z_{i}", [P, D]) for i in range(2)]
            HB, HTB, OB, XB = bank[0:2], bank[2:4], bank[4:6], bank[6]

            def steps(eng, step):
                def s(n):
                    return (n, n % 4, n // 4) if 0 <= n < SLOTS else None

                for n in range(3):
                    step(*(s(n - back) for back in range(4)))
                with eng.Fori(0, (SLOTS - 3) // 4) as j:
                    for u in range(3, 7):
                        step(*((j * 4 + (u - back), (u - back) % 4, j + (u - back) // 4) for back in range(4)))
                for n in range(SLOTS, SLOTS + 3):
                    step(*(s(n - back) for back in range(4)))

            with nc.Block() as block:
                @block.sync
                def _(sp):
                    def load(n, i, turn):
                        e = sp.value_load(se[0:1, bass.ds(n, 1)], min_val=0, max_val=E - 1)
                        wait(sp, t_end, n * 6 - 21)
                        sp.dma_start(rowt[i][:], routed[bass.ds(n * P, P), :]).then_inc(t_loaded[i], 16)
                        sp.dma_start(b1t[i][:], t["b1"][bass.ds(e, 1)].rearrange("a n -> (a n)").partition_broadcast(P)).then_inc(t_loaded[i], 16)
                        sp.dma_start(b2t[i][:], t["b2"][bass.ds(e, 1)].rearrange("a n -> (a n)").partition_broadcast(P)).then_inc(t_loaded[i], 16)
                        sp.dma_start(part[i][:], t["par"][bass.ds(e, 1)].rearrange("a p n -> (a p) n")).then_inc(t_loaded[i], 16)

                    for n in range(4):
                        load(n, n, 0)
                    with sp.Fori(0, SLOTS // 4 - 1) as j:
                        for u in range(4):
                            load(j * 4 + (4 + u), u, j + 1)
                    for n in range(SLOTS // 4 * 4, SLOTS):
                        load(n, n % 4, n // 4)

                @block.gpsimd
                def _(pool):
                    def step(x, a, c, d):
                        if a:
                            n, i, turn = a
                            pool.wait_ge(t_h, n * 4 + 4)
                            wait(pool, t_hn, n)
                            pool.tensor_tensor(rs1[:], var1[:], minus_half[:, 0:1], ALU.pow).then_inc(t_rs1, 1)
                        if d:
                            n, i, turn = d
                            pool.wait_ge(t_end, n * 6 + 6)
                            wait(pool, t_z, n)
                            pool.tensor_tensor(rs3[:], var3[:], minus_half[:, 0:1], ALU.pow).then_inc(t_rs3, 1)
                        if c:
                            n, i, turn = c
                            pool.wait_ge(t_y, n * 7 + (Y_C + 7))
                            pool.tensor_tensor(rs2[:], var2[:], minus_half[:, 0:1], ALU.pow).then_inc(t_rs2, 1)
                        if d:
                            n, i, turn = d
                            pool.wait_ge(t_z, n + 1)
                            pool.sem_inc(passed, 1)
                            pool.indirect_dma_start(out=x3_rows[:, :], out_offset=bass.IndirectOffsetOnAxis(
                                ap=token[i][:, 0:1], axis=0), in_=z[i % 2][:], in_offset=None,
                                bounds_check=TOK - 1, oob_is_err=False).then_inc(t_sent[i], 16)
                        if c:
                            n, i, turn = c
                            pool.wait_ge(t_loaded[i], turn * 64 + 64)
                            wait(pool, t_end, n * 6)
                            pool.tensor_tensor(xpb[:], rowt[i][:, D:2 * D], n2b[:], ALU.add).then_inc(t_xb, 1)

                    steps(pool, step)
                    for i in range(4):
                        pool.wait_ge(t_sent[i], 16 * ((SLOTS - 1 - i) // 4 + 1))

                @block.tensor
                def _(pe):
                    pe.wait_ge(big_loaded, 16 * (len(big) + 2))

                    def step(x, a, c, d):
                        if a:
                            n, i, turn = a
                            e = pe.value_load(se[0:1, bass.ds(n, 1)], min_val=0, max_val=E - 1)
                            pe.wait_ge(t_xT_kept, n + 1)
                            wait(pe, t_h, n * 4 - 7)
                            for k in range(KT):
                                ins = pe.matmul(HB[i % 2][:], xTt[:, k, :], wa[:, k, bass.ds(e, 1), :].rearrange("p a n -> p (a n)"),
                                                start=k == 0, stop=k == KT - 1)
                            ins.then_inc(t_h_made, 1)
                        if c:
                            n, i, turn = c
                            pe.wait_ge(t_hn, n + 1)
                            wait(pe, t_gelu, n * HC - HC)
                            for k in range(HC):
                                ins = pe.transpose(HTB[i % 2][:, k * P:(k + 1) * P], hn[i % 2][:, k * P:(k + 1) * P], ident[:])
                            ins.then_inc(t_hT_made, 1)
                        if x:
                            n, i, turn = x
                            pe.wait_ge(t_loaded[i], turn * 64 + 64)
                            wait(pe, t_xT_kept, n)
                            for k in range(KT):
                                ins = pe.transpose(XB[:, k * P:(k + 1) * P], rowt[i][:, k * P:(k + 1) * P], ident[:])
                            ins.then_inc(t_xT_made, 1)
                        if c:
                            n, i, turn = c
                            e = pe.value_load(se[0:1, bass.ds(n, 1)], min_val=0, max_val=E - 1)
                            pe.wait_ge(t_gelu, n * HC + HC)
                            wait(pe, t_y, n * 7 + (Y_C - 12))
                            for k in range(HC):
                                ins = pe.matmul(OB[i % 2][:, 0:D], hT[:, k, :], wb[:, bass.ds(e, 1), k, :].rearrange("p a n -> p (a n)"),
                                                start=k == 0, stop=k == HC - 1)
                            ins.then_inc(t_o_made, 1)

                    steps(pe, step)

                @block.scalar
                def _(act):
                    def step(x, a, c, d):
                        if c:
                            n, i, turn = c
                            act.wait_ge(t_hT_made, n + 1)
                            wait(act, t_o_made, n)
                            for k in range(HC):
                                act.activation(hT[:, k, :], HTB[i % 2][:, k * P:(k + 1) * P], ACT.Gelu,
                                               scale=part[i][:, k:k + 1], bias=part[i][:, HC + k:HC + k + 1]).then_inc(t_gelu, 1)
                        if x:
                            n, i, turn = x
                            act.wait_ge(t_xT_made, n + 1)
                            wait(act, t_h_made, n)
                            act.copy(xTt[:], XB[:, 0:D]).then_inc(t_xT_kept, 1)

                    steps(act, step)

                @block.vector
                def _(dve):
                    def chain(done, count, more=0):
                        k = [0]

                        def link(instruction):
                            if k[0]:
                                dve.wait_ge(done, count + (more + k[0]))
                            k[0] += 1
                            instruction().then_inc(done, 1)

                        return link

                    def aggregate(mean_var, statistics):
                        dve.sem_inc(passed, 1)
                        return dve.bn_aggr(mean_var[:], statistics[:])

                    def step(x, a, c, d):
                        if a:
                            n, i, turn = a
                            first = chain(t_h, n * 4)
                            dve.wait_ge(t_h_made, n + 1)
                            wait(dve, t_hn, n)
                            first(lambda: dve.tensor_tensor(hb[:], HB[i % 2][:], b1t[i][:], ALU.add))
                        if d:
                            end = chain(t_end, d[0] * 6)
                            dve.wait_ge(t_rs2, d[0] + 1)
                            end(lambda: dve.tensor_scalar(nrm[:], res[:], mv2[:, 0:1], rs2[:], ALU.subtract, ALU.mult))
                        if a:
                            first(lambda: dve.bn_stats(st[:], hb[:]))
                        if d:
                            end(lambda: dve.tensor_tensor(ng[:], nrm[:], n2g[:], ALU.mult))
                        if a:
                            first(lambda: aggregate(mvt, st))
                        if d:
                            dve.wait_ge(t_xb, d[0] + 1)
                            wait(dve, t_z, d[0])
                            end(lambda: dve.tensor_tensor(w3[:], ng[:], xpb[:], ALU.add))
                        if a:
                            first(lambda: dve.tensor_scalar(var1[:], mvt[:, 1:2], EPS, None, ALU.add))
                        if d:
                            end(lambda: dve.bn_stats(st3[:], w3[:]))
                        if c:
                            n, i, turn = c
                            x1r, wsum = rowt[i][:, 0:D], rowt[i][:, 2 * D:2 * D + 1]
                            dve.tensor_copy(token[i][:], rowt[i][:].bitcast(U32)[:, 2 * D + 1:2 * D + 2]).then_inc(t_y, 1)
                            middle = chain(t_y, n * 7, Y_C + 1)
                            dve.wait_ge(t_o_made, n + 1)
                            middle(lambda: dve.tensor_tensor(ot[:], OB[i % 2][:, 0:D], b2t[i][:], ALU.add))
                        if d:
                            end(lambda: aggregate(mv3, st3))
                        if c:
                            middle(lambda: dve.scalar_tensor_tensor(sel[:], ot[:], part[i][:, 2 * HC:2 * HC + 1], x1r, ALU.mult, ALU.add))
                        if d:
                            end(lambda: dve.tensor_scalar(var3[:], mv3[:, 1:2], EPS, None, ALU.add))
                        if c:
                            middle(lambda: dve.scalar_tensor_tensor(res[:], sel[:], wsum, x1r, ALU.mult, ALU.add))
                        if a:
                            m = a[1]
                            dve.wait_ge(t_rs1, a[0] + 1)
                            wait(dve, t_hT_made, a[0] - 1)
                            dve.tensor_scalar(hn[m % 2][:], hb[:], mvt[:, 0:1], rs1[:], ALU.subtract, ALU.mult).then_inc(t_hn, 1)
                        if c:
                            middle(lambda: dve.bn_stats(st2[:], res[:]))
                        if d:
                            m = d[1]
                            dve.wait_ge(t_rs3, d[0] + 1)
                            wait(dve, t_sent[(m - 2) % 4], (d[2] + (1 if m >= 2 else 0)) * 16)
                            dve.tensor_scalar(z[m % 2][:], w3[:], mv3[:, 0:1], rs3[:], ALU.subtract, ALU.mult).then_inc(t_z, 1)
                        if c:
                            middle(lambda: aggregate(mv2, st2))
                            middle(lambda: dve.tensor_scalar(var2[:], mv2[:, 1:2], EPS, None, ALU.add))

                    steps(dve, step)
            scope.close()

        ROUTER = 19

        def experts1():
            scope = ExitStack()

            def sb(name, shape, dt=F32):
                return scope.enter_context(nc.sbuf_tensor("f_" + name, shape, dt))

            xg = sb("xg", [P, GB, D])
            xres = sb("xres", [P, GB, D])
            xgT = sb("xgT", [P, KT, GB * P])
            silu = [sb(f"silu_{i}", [P, GB * P]) for i in range(2)]
            prod = [sb(f"prod_{i}", [P, GB * P]) for i in range(2)]
            wB = [sb(f"wB_{i}", [P, GB * P]) for i in range(2)]
            hid = [sb(f"hid_{i}", [P, GB * P]) for i in range(2)]
            yg = sb("yg", [P, GB, D])
            xog = sb("xog", [P, GB, D])
            stg = sb("stg", [P, GB, 6])
            mvg = sb("mvg", [P, GB, 2])
            varg = sb("varg", [P, GB])
            rstdg = sb("rstdg", [P, GB])
            lg, sh, es, s, eq, cand, hit, s2, eq2, cand2, hit2, drop, keep, wts = (
                sb(n, [P, GB, E]) for n in ("lg", "sh", "es", "s", "eq", "cand", "hit", "s2", "eq2", "cand2", "hit2", "drop", "keep", "wts"))
            mx, sm, rc, m1, c1, m2, c2 = (sb(n, [P, GB]) for n in ("mx", "sm", "rc", "m1", "c1", "m2", "c2"))
            flat = lambda a: a[:].rearrange("p a b -> p (a b)")
            over = lambda a: a[:].unsqueeze(2).broadcast_to([P, GB, E])
            up = ascend[:].unsqueeze(1).broadcast_to([P, GB, E])
            SHARED = UNITS - E
            GBANK, UBANK, WBANK, XBANK = bank[4], bank[5], bank[6], bank[7]

            with nc.Block() as block:
                @block.sync
                def _(sp):
                    def group(ap, g):
                        return ap[bass.ds(g * GB, GB)].rearrange("b p n -> p b n")

                    def load(g):
                        sp.wait_ge(f_xres, g + 1)
                        sp.wait_ge(f_xT_made, g * KT + KT)
                        sp.dma_start(xg[:], group(x5, g)).then_inc(f_loaded, 16)

                    def store(g):
                        sp.wait_ge(f_done, g * GB + 2 * GB)
                        sp.dma_start(group(out, g), xog[:]).then_inc(f_stored, 16)

                    load(0)
                    with sp.Fori(0, NGR - 1) as g:
                        load(g + 1)
                        store(g)
                    store(NGR - 1)
                    sp.wait_ge(f_stored, 16 * (NGR + 1))

                @block.gpsimd
                def _(pool):
                    with pool.Fori(0, NGR) as g:
                        pool.wait_ge(f_loaded, g * 16 + 16)
                        pool.wait_ge(f_res, g * GB + GB)
                        pool.sem_inc(passed, 1)
                        pool.tensor_copy(xres[:], xg[:]).then_inc(f_xres, 1)
                        pool.wait_ge(f_ln, g * 6 + 6)
                        pool.wait_ge(f_done, g * GB + GB)
                        pool.tensor_tensor(rstdg[:], varg[:], minus_half[:], ALU.pow).then_inc(f_rstd, 1)

                @block.tensor
                def _(pe):
                    with pe.Fori(0, NGR) as g:
                        def in_products(k):
                            pe.wait_ge(f_silu, g * UNITS + (k + 1))
                            for i in range(KT):
                                ins = pe.matmul(GBANK[:], w7g[:, i, k, :], xgT[:, i, :], start=i == 0, stop=i == KT - 1)
                            ins.then_inc(f_gate_made, 1)
                            pe.wait_ge(f_hid, g * UNITS + (k + 3))
                            for i in range(KT):
                                ins = pe.matmul(UBANK[:], w7u[:, i, k, :], xgT[:, i, :], start=i == 0, stop=i == KT - 1)
                            ins.then_inc(f_up_made, 1)

                        def spread(k):
                            e = k - SHARED
                            if e == 0:
                                pe.wait_ge(f_step, g * ROUTER + ROUTER)
                            pe.wait_ge(f_wB_kept, g * E + (e + 1))
                            for b in range(GB):
                                ins = pe.transpose(WBANK[:, b * P:(b + 1) * P], wts[:, b, e:e + 1].broadcast_to([P, P]), ident[:])
                            ins.then_inc(f_wB_made, 1)

                        def out_product(k):
                            if k == 0:
                                pe.wait_ge(f_res, g * GB + GB)
                            pe.wait_ge(f_hid, g * UNITS + (k + 4))
                            for b in range(GB):
                                ins = pe.matmul(bank[b][:, 0:D], hid[k % 2][:, b * P:(b + 1) * P], w7d[:, k, :], start=k == 0, stop=k == UNITS - 1)
                            ins.then_inc(f_o_made, 1)

                        pe.wait_ge(f_loaded, g * 16 + 16)
                        for k in range(KT):
                            pe.wait_ge(f_xT_kept, g * KT + (k + 1))
                            for b in range(GB):
                                ins = pe.transpose(XBANK[:, b * P:(b + 1) * P], xg[:, b, k * P:(k + 1) * P], ident[:])
                            ins.then_inc(f_xT_made, 1)
                        pe.wait_ge(f_xT_kept, g * KT + (KT + 1))
                        for b in range(GB):
                            for k in range(KT):
                                ins = pe.matmul(XBANK[:, b * E:(b + 1) * E], xgT[:, k, b * P:(b + 1) * P], w7r[:, k, :],
                                                start=k == 0, stop=k == KT - 1)
                        ins.then_inc(f_logit_made, 1)
                        for k in range(UNITS):
                            in_products(k)
                            if k + 1 >= SHARED and k + 1 < UNITS:
                                spread(k + 1)
                            if k:
                                out_product(k - 1)
                        out_product(UNITS - 1)

                @block.scalar
                def _(act):
                    with act.Fori(0, NGR) as g:
                        for k in range(KT):
                            act.wait_ge(f_xT_made, g * KT + (k + 1 + KT))
                            act.wait_ge(f_o_made, g * UNITS + 2)
                            act.copy(xgT[:, k, :], XBANK[:]).then_inc(f_xT_kept, 1)
                        act.wait_ge(f_step, g * ROUTER + 3)
                        act.activation(es[:], sh[:], ACT.Exp).then_inc(f_exp, 1)
                        for k in range(UNITS):
                            act.wait_ge(f_gate_made, g * UNITS + (k + 1))
                            act.wait_ge(f_hid, g * UNITS + (k + 2))
                            act.activation(silu[k % 2][:], GBANK[:], ACT.Silu).then_inc(f_silu, 1)
                            if k + 1 >= SHARED and k + 1 < UNITS:
                                act.wait_ge(f_wB_made, g * E + (k + 1 - SHARED + 2))
                                act.copy(wB[(k + 1) % 2][:], WBANK[:]).then_inc(f_wB_kept, 1)

                @block.vector
                def _(dve):
                    with dve.Fori(0, NGR) as g:
                        k_ = [0]

                        def link(ins):
                            k_[0] += 1
                            ins.then_inc(f_step, 1)
                            dve.wait_ge(f_step, g * ROUTER + k_[0])

                        dve.wait_ge(f_logit_made, g + 2)
                        link(dve.tensor_copy(flat(lg), XBANK[:, 0:GB * E]))
                        link(dve.tensor_reduce(mx[:], lg[:], AX.X, ALU.max))
                        link(dve.tensor_tensor(sh[:], lg[:], over(mx), ALU.subtract))
                        dve.wait_ge(f_exp, g + 2)
                        link(dve.tensor_reduce(sm[:], es[:], AX.X, ALU.add))
                        link(dve.reciprocal(rc[:], sm[:]))
                        link(dve.tensor_tensor(s[:], es[:], over(rc), ALU.mult))
                        link(dve.tensor_reduce(m1[:], s[:], AX.X, ALU.min))
                        link(dve.tensor_tensor(eq[:], s[:], over(m1), ALU.is_equal))
                        link(dve.tensor_tensor(cand[:], eq[:], up, ALU.mult))
                        link(dve.tensor_reduce(c1[:], cand[:], AX.X, ALU.max))
                        link(dve.tensor_tensor(hit[:], up, over(c1), ALU.is_equal))
                        link(dve.scalar_tensor_tensor(flat(s2), flat(hit), 4.0, flat(s), ALU.mult, ALU.add))
                        link(dve.tensor_reduce(m2[:], s2[:], AX.X, ALU.min))
                        link(dve.tensor_tensor(eq2[:], s2[:], over(m2), ALU.is_equal))
                        link(dve.tensor_tensor(cand2[:], eq2[:], up, ALU.mult))
                        link(dve.tensor_reduce(c2[:], cand2[:], AX.X, ALU.max))
                        link(dve.tensor_tensor(hit2[:], up, over(c2), ALU.is_equal))
                        link(dve.tensor_tensor(drop[:], hit[:], hit2[:], ALU.add))
                        dve.wait_ge(f_wB_made, g * E + 1)
                        dve.tensor_scalar(keep[:], drop[:], -1.0, 1.0, ALU.mult, ALU.add).then_inc(f_keep, 1)
                        dve.wait_ge(f_keep, g + 1)
                        link(dve.tensor_tensor(wts[:], s[:], keep[:], ALU.mult))
                        assert k_[0] == ROUTER
                        for k in range(UNITS):
                            dve.wait_ge(f_silu, g * UNITS + (k + 2))
                            dve.wait_ge(f_up_made, g * UNITS + (k + 1))
                            dve.wait_ge(f_o_made, g * UNITS + (k + 1))
                            if k < SHARED:
                                dve.tensor_tensor(hid[k % 2][:], UBANK[:], silu[k % 2][:], ALU.mult).then_inc(f_hid, 1)
                            else:
                                dve.tensor_tensor(prod[k % 2][:], UBANK[:], silu[k % 2][:], ALU.mult).then_inc(f_prod, 1)
                                dve.wait_ge(f_prod, g * E + (k - SHARED + 1))
                                dve.wait_ge(f_wB_kept, g * E + (k - SHARED + 2))
                                dve.tensor_tensor(hid[k % 2][:], prod[k % 2][:], wB[k % 2][:], ALU.mult).then_inc(f_hid, 1)
                        dve.wait_ge(f_o_made, g * UNITS + (UNITS + 2))
                        dve.wait_ge(f_xres, g + 2)
                        for b in range(GB):
                            dve.tensor_tensor(yg[:, b, :], bank[b][:, 0:D], xres[:, b, :], ALU.add).then_inc(f_res, 1)
                        for b in range(GB):
                            dve.wait_ge(f_res, g * GB + (b + 1 + GB))
                            dve.bn_stats(stg[:, b, :], yg[:, b, :]).then_inc(f_ln, 1)
                        dve.wait_ge(f_ln, g * 6 + 4)
                        dve.sem_inc(passed, 1)
                        for b in range(GB):
                            ins = dve.bn_aggr(mvg[:, b, :], stg[:, b, :])
                        ins.then_inc(f_ln, 1)
                        dve.wait_ge(f_ln, g * 6 + 5)
                        dve.tensor_scalar(varg[:], mvg[:, :, 1], EPS, None, ALU.add).then_inc(f_ln, 1)
                        dve.wait_ge(f_rstd, g + 1)
                        dve.wait_ge(f_stored, g * 16 + 16)
                        for b in range(GB):
                            dve.tensor_scalar(xog[:, b, :], yg[:, b, :], mvg[:, b, 0:1], rstdg[:, b:b + 1],
                                              ALU.subtract, ALU.mult).then_inc(f_done, 1)
            scope.close()

        attention(CAUSAL, big)
        experts0()
        attention(SCALED, [(wa, t["wa1"]), (wb, t["wb1"])])
        with ExitStack() as scope:
            posu = scope.enter_context(nc.sbuf_tensor("posu", [P, NB], U32))
            meta = scope.enter_context(nc.sbuf_tensor("meta", [P, NB, ROW - 2 * D], F32))
            se = scope.enter_context(nc.sbuf_tensor("se", [P, SLOTS], I32))
            routing(posu, meta, se)
            slots(se)
        attention(ROTARY, [])
        attention(CROSS, [])
        experts1()


def host_layout(inputs):
    g = {k: np.asarray(a) for k, a in inputs.items()}

    def kt(w):
        return w.reshape(w.shape[0] // P, P, w.shape[1]).transpose(1, 0, 2)

    wqkv = np.zeros((P, 4, KT, 3 * D), np.float32)
    wqkv[:, 0] = kt(g["L0_attn_w_attn"])
    for i, n in enumerate(("q", "k", "v")):
        wqkv[:, 1, :, i * D:(i + 1) * D] = kt(g[f"L0_ffn_{n}_w"])
    wqkv[:, 2] = kt(g["L1_attn_w_qkv"].T)
    wqkv[:, 3, :, 0:D] = kt(g["L1_xattn_Wq"])
    wqkv[:, 3, 0, D:2 * D] = g["L1_xattn_Wk"]
    wqkv[:, 3, 0, 2 * D:] = g["L1_xattn_Wv"]
    wo = np.stack([kt(g["L0_attn_w_proj"]), kt(g["L0_ffn_out_w"]), kt(g["L1_attn_w_out"].T), kt(g["L1_xattn_Wo"])], 1)
    key, query = np.arange(P)[:, None], np.arange(P)[None, :]
    masked = np.where(key > query, -BIG, 0.0).astype(np.float32)
    inv_freq = (1.0 / 10000.0 ** (np.arange(0, DK, 2, dtype=np.float32) / DK)).astype(np.float32)
    freqs = np.arange(P, dtype=np.float32)[:, None] * inv_freq[None, :]
    def expert_in(w):
        return w.reshape(w.shape[0], -1, P, w.shape[2]).transpose(2, 1, 0, 3)

    def expert_out(w):
        return w.reshape(w.shape[0], -1, P, w.shape[2]).transpose(2, 0, 1, 3)

    def shared_in(w):
        return w.reshape(D, D // F1, F1).transpose(1, 0, 2)

    par = np.concatenate([g["L0_ffn_ln_g"].reshape(E, HC, P).transpose(0, 2, 1), g["L0_ffn_ln_b"].reshape(E, HC, P).transpose(0, 2, 1),
                          np.broadcast_to(g["L0_ffn_res_scale"][:, None, None], (E, P, 1))], 2)
    t = {
        "wa0": expert_in(g["L0_xattn_proj_in"].transpose(0, 2, 1)), "wb0": expert_out(g["L0_xattn_proj_out"].transpose(0, 2, 1)),
        "wa1": expert_in(g["L0_ffn_w1"]), "wb1": expert_out(g["L0_ffn_w2"]), "b1": g["L0_ffn_b1"], "b2": g["L0_ffn_b2"], "par": par,
        "w7g": expert_in(np.concatenate([shared_in(g["L1_ffn_ws_gate"]), g["L1_ffn_w_gate"]])),
        "w7u": expert_in(np.concatenate([shared_in(g["L1_ffn_ws_up"]), g["L1_ffn_w_up"]])),
        "w7d": np.concatenate([g["L1_ffn_ws_down"].reshape(D // F1, F1, D), g["L1_ffn_w_down"]]).transpose(1, 0, 2),
        "w7r": kt(g["L1_ffn_router_w"]), "wlog": kt(g["L0_ffn_moe_gate_w"]), "b_log": g["L0_ffn_moe_gate_b"],
        "n2_g": g["L0_ffn_n2_g"], "n2_b": g["L0_ffn_n2_b"],
        "ones": np.ones((P, P), np.float32), "lower": np.triu(np.ones((P, P), np.float32), 1),
        "ascend": 1 + np.arange(E, dtype=np.float32),
        "descend": E - np.arange(E, dtype=np.float32), "iotas": np.tile(np.arange(NB, dtype=np.float32) * P, E),
        "slotn": np.repeat(np.arange(SLOTS, dtype=np.float32), E),
        "keepmask": np.tile((np.arange(NB) > 0).astype(np.float32), E),
        "x": g["x"], "ctx": g["ctx_512"], "itok": g["itok_BxS2xS_0_7"],
        "wqkv": wqkv, "wo": wo, "gatew": kt(g["L0_ffn_gate_w"]),
        "b_qkv0": g["L0_attn_b_attn"], "b_qkv3": np.concatenate([g["L1_xattn_bq"], g["L1_xattn_bk"], g["L1_xattn_bv"]]),
        "b_o0": g["L0_attn_b_proj"], "b_o2": g["L1_attn_b_out"], "b_o3": g["L1_xattn_bo"],
        "scale_w": g["L0_ffn_scale_w"].reshape(-1), "gate_b": g["L0_ffn_gate_b"],
        "n1_g": g["L0_ffn_n1_g"], "n1_b": g["L0_ffn_n1_b"],
        "ident": np.eye(P, dtype=np.float32),
        "maskq": masked.T,
        "cos": np.cos(freqs).astype(np.float32), "sin": np.stack([-np.sin(freqs), np.sin(freqs)], 1).astype(np.float32),
    }
    return {k: np.ascontiguousarray(a) for k, a in t.items()}


def kernel(**inputs):
    import concourse.bacc as bacc
    from concourse.bass_utils import run_bass_kernel_spmd

    nc = bacc.Bacc("TRN2", target_bir_lowering=False, num_devices=1)
    arrays = host_layout(inputs)
    t = {n: nc.dram_tensor(f"in_{n}", a.shape, mybir.dt.from_np(a.dtype), kind="ExternalInput").ap() for n, a in arrays.items()}
    out = nc.dram_tensor("out_dram", (NB, P, D), F32, kind="ExternalOutput").ap()
    program(nc, t, out)
    r = run_bass_kernel_spmd(nc, [{f"in_{n}": a for n, a in arrays.items()}], core_ids=[0])
    return r.results[0]["out_dram"]
```

```python
from contextlib import ExitStack

import concourse.bass as bass
import concourse.mybir as mybir
import numpy as np

F32 = mybir.dt.float32
BF16 = mybir.dt.bfloat16
F32R = mybir.dt.float32r
I32 = mybir.dt.int32
U32 = mybir.dt.uint32
ALU = mybir.AluOpType
ACT = mybir.ActivationFunctionType
AX = mybir.AxisListType

P = 128
NB = 16
D = 256
KT = D // P
H = 16
DK = D // H
HP = 32
HG = P // HP
NG = H // HG
E = 8
HID = 512
HC = HID // P
F1 = 128
GB = 4
NGR = NB // GB
TOK = NB * P
SLOTS = (TOK + E * (P - 1)) // P
UNITS = E + D // F1
ROW = 2 * D + 4
EPS = 1e-5
BIG = 1e30
CAUSAL, SCALED, ROTARY, CROSS = range(4)


class At:

    def __init__(self, stage, b, half, quarter):
        self.b, self.n, self.half, self.p, self.q = b, b + NB * stage, half, quarter % 2, quarter


def at(stage, b):
    return At(stage, b, b // 2, b % 4) if 0 <= b < NB else None


def wait(eng, sem, value):
    if isinstance(value, int) and value <= 0:
        return
    eng.wait_ge(sem, value)


def attention_steps(eng, stage, step):
    for b in range(3):
        step(*(at(stage, b - back) for back in range(4)))
    with eng.Fori(0, (NB - 4) // 4) as j:
        for u in range(3, 7):
            step(*(At(stage, j * 4 + (u - back), j * 2 + (u - back) // 2, (u - back) % 4) for back in range(4)))
    for b in range(NB - 1, NB + 3):
        step(*(at(stage, b - back) for back in range(4)))


def program(nc, t, out):
    ctx = ExitStack()
    with ctx:
        def sb(name, shape, dt=F32):
            return ctx.enter_context(nc.sbuf_tensor(name, shape, dt))

        def sem(name):
            return ctx.enter_context(nc.semaphore(name))

        def dram(name, shape, dt=F32):
            return nc.dram_tensor(name, shape, dt).ap()

        x1 = dram("x1_dram", [NB, P, D])
        x2 = dram("x2_dram", [NB, P, D])
        xr = dram("xr_dram", [NB, P, D])
        x3_rows = dram("x3_dram", [TOK, D])
        x3 = x3_rows.rearrange("(b p) d -> b p d", p=P)
        routed = dram("routed_dram", [SLOTS * P, ROW])
        x4 = dram("x4_dram", [NB, P, D])
        x5 = dram("x5_dram", [NB, P, D])
        X_IN = [t["x"], x2, x3, x4]
        X_OUT = [x1, xr, x4, x5]

        bank = [ctx.enter_context(nc.psum_tensor(f"bank{i}", [P, 512], F32)) for i in range(8)]
        QKB, VB, OTB, TB = bank[0], bank[1], bank[2], bank[3]
        SB = [bank[4], bank[5]]
        PTB = [bank[6], bank[7]]

        ident = sb("ident", [P, P])
        identb = sb("identb", [P, P], BF16)
        maskq = sb("maskq", [P, HG, P], BF16)
        minus_half = sb("minus_half", [P, NB])
        cosb = sb("cosb", [P, DK // 2])
        sinb = sb("sinb", [P, 2, DK // 2])
        v = [sb(f"v_{i}", [P, H, HP]) for i in range(2)]
        wqkv = sb("wqkv", [P, 4, KT, 3 * D])
        wo = sb("wo", [P, 4, KT, D])
        gatew = sb("gatew", [P, KT, D])
        bqkv = sb("bqkv", [P, 2, 3 * D])
        bout = sb("bout", [P, 4, D])
        scalew = sb("scalew", [P, D])
        gateb = sb("gateb", [P, D])
        n1g = sb("n1g", [P, D])
        n1b = sb("n1b", [P, D])

        w7r = sb("w7r", [P, KT, E])
        wlog = sb("wlog", [P, KT, E])
        blog = sb("blog", [P, E])
        n2g = sb("n2g", [P, D])
        n2b = sb("n2b", [P, D])
        ones = sb("ones", [P, P])
        lower = sb("lower", [P, P])
        ascend = sb("ascend", [P, E])
        descend = sb("descend", [P, E])
        iotas = sb("iotas", [P, E, NB])
        slotn = sb("slotn", [P, SLOTS, E])
        keepmask = sb("keepmask", [P, E, NB])

        loaded = sem("loaded_constants")
        init = sem("init")
        x_loaded = [sem(f"x_loaded_{i}") for i in range(2)]
        x_stored = [sem(f"x_stored_{i}") for i in range(2)]
        xT_made = sem("xT_made")
        qkv_made = sem("qkv_made")
        qkT_made = sem("qkT_made")
        s_made = sem("s_made")
        probsT_made = sem("probsT_made")
        av_made = sem("av_made")
        o_made = sem("o_made")
        attT_made = sem("attT_made")
        proj_made = sem("proj_made")
        xT_kept = sem("xT_kept")
        probs_kept = sem("probs_kept")
        high_kept = sem("high_kept")
        qT_kept = sem("qT_kept")
        kT_kept = [sem(f"kT_kept_{i}") for i in range(2)]
        oT_kept = sem("oT_kept")
        attT_kept = sem("attT_kept")
        qk_kept = sem("qk_kept")
        klow_kept = sem("klow_kept")
        qlow_kept = sem("qlow_kept")
        v_kept = sem("v_kept")
        max_kept = sem("max_kept")
        probsT_kept = sem("probsT_kept")
        rden_done = sem("rden_done")
        att_kept = sem("att_kept")
        res_done = sem("res_done")
        ln_step = sem("ln_step")
        ln_done = sem("ln_done")
        xb_done = sem("xb_done")
        rstd_done = sem("rstd_done")
        kdiag_cleared = sem("kdiag_cleared")
        passed = sem("passed")
        lin_step = sem("lin_step")
        tanh_done = sem("tanh_done")
        fac_done = sem("fac_done")
        gate_made = sem("gate_made")
        gz_done = sem("gz_done")
        gth_done = sem("gth_done")
        gated_done = sem("gated_done")
        gatedT_made = sem("gatedT_made")
        gatedT_kept = sem("gatedT_kept")
        n1_step = sem("n1_step")
        big_loaded = sem("big_loaded")
        e_loaded = [sem(f"e_loaded_{g}") for g in range(NGR)]
        e_wloaded = sem("e_wloaded")
        e_stored = sem("e_stored")
        e_xT_made = sem("e_xT_made")
        e_gate_made = sem("e_gate_made")
        e_z_made = sem("e_z_made")
        e_o_made = sem("e_o_made")
        e_xTh = sem("e_xTh")
        e_gate_kept = sem("e_gate_kept")
        e_hi = sem("e_hi")
        e_xTl = sem("e_xTl")
        e_itokf = sem("e_itokf")
        e_number = sem("e_number")
        e_masked = sem("e_masked")
        e_tmp = sem("e_tmp")
        e_lo = sem("e_lo")
        e_acc = sem("e_acc")
        e_ln = sem("e_ln")
        e_done = sem("e_done")
        e_whi = sem("e_whi")
        e_wlo = sem("e_wlo")
        e_rstd = sem("e_rstd")
        r_loaded = [sem(f"r_loaded_{g}") for g in range(NGR)]
        r_xT_made = sem("r_xT_made")
        r_xT_kept = sem("r_xT_kept")
        r_logit_made = sem("r_logit_made")
        r_logit_kept = sem("r_logit_kept")
        r_step = sem("r_step")
        r_exp = sem("r_exp")
        r_rank = sem("r_rank")
        r_meta = sem("r_meta")
        fill_step = sem("fill_step")
        filled = sem("filled")
        row_loaded = sem("row_loaded")
        row_meta = sem("row_meta")
        row_sent = sem("row_sent")
        t_loaded = [sem(f"t_loaded_{i}") for i in range(4)]
        t_sent = [sem(f"t_sent_{i}") for i in range(4)]
        t_xT_made = sem("t_xT_made")
        t_h_made = sem("t_h_made")
        t_hT_made = sem("t_hT_made")
        t_o_made = sem("t_o_made")
        t_xT_kept = sem("t_xT_kept")
        t_gelu = sem("t_gelu")
        t_h = sem("t_h")
        t_hn = sem("t_hn")
        t_y = sem("t_y")
        t_end = sem("t_end")
        t_z = sem("t_z")
        t_xb = sem("t_xb")
        t_rs1, t_rs2, t_rs3 = (sem(f"t_rs{i}") for i in (1, 2, 3))
        f_loaded = sem("f_loaded")
        f_stored = sem("f_stored")
        f_xT_made = sem("f_xT_made")
        f_logit_made = sem("f_logit_made")
        f_gate_made = sem("f_gate_made")
        f_up_made = sem("f_up_made")
        f_wB_made = sem("f_wB_made")
        f_o_made = sem("f_o_made")
        f_xT_kept = sem("f_xT_kept")
        f_exp = sem("f_exp")
        f_silu = sem("f_silu")
        f_wB_kept = sem("f_wB_kept")
        f_step = sem("f_step")
        f_keep = sem("f_keep")
        f_prod = sem("f_prod")
        f_hid = sem("f_hid")
        f_split = sem("f_split")
        f_hi = sem("f_hi")
        f_lo = sem("f_lo")
        f_whi = sem("f_whi")
        f_wlo = sem("f_wlo")
        f_res = sem("f_res")
        f_ln = sem("f_ln")
        f_done = sem("f_done")
        f_xres = sem("f_xres")
        f_rstd = sem("f_rstd")
        rope_step = sem("rope_step")

        start = ExitStack()
        maskf = start.enter_context(nc.sbuf_tensor("maskf", [P, P], F32))
        consts = [(ident[:], t["ident"]), (maskf[:], t["maskq"]), (wqkv[:, CAUSAL], t["wqkv"][:, CAUSAL]), (wo[:, CAUSAL], t["wo"][:, CAUSAL])]
        rows = [(bqkv[:, 0, :], t["b_qkv0"]), (bout[:, 0, :], t["b_o0"])]
        later_consts = [(wqkv[:, SCALED:], t["wqkv"][:, SCALED:]), (wo[:, SCALED:], t["wo"][:, SCALED:]), (cosb[:], t["cos"]), (sinb[:], t["sin"]),
                        (gatew[:], t["gatew"]), (wlog[:], t["wlog"]), (w7r[:], t["w7r"]), (ones[:], t["ones"]), (lower[:], t["lower"])]
        later_rows = [(bqkv[:, 1, :], t["b_qkv3"]), (bout[:, 2, :], t["b_o2"]), (bout[:, 3, :], t["b_o3"]), (scalew[:], t["scale_w"]),
                      (gateb[:], t["gate_b"]), (n1g[:], t["n1_g"]), (n1b[:], t["n1_b"]), (n2g[:], t["n2_g"]), (n2b[:], t["n2_b"]),
                      (blog[:], t["b_log"]), (descend[:], t["descend"]), (ascend[:], t["ascend"]),
                      (iotas[:].rearrange("p e b -> p (e b)"), t["iotas"]), (slotn[:].rearrange("p s e -> p (s e)"), t["slotn"]),
                      (keepmask[:].rearrange("p e b -> p (e b)"), t["keepmask"])]
        later = later_consts + [(dst, src.partition_broadcast(P)) for dst, src in later_rows]
        LOADED = 16 * (len(consts) + len(rows))

        with nc.Block() as block:
            @block.sync
            def _(sp):
                for dst, src in consts:
                    sp.dma_start(dst, src).then_inc(loaded, 16)
                for dst, src in rows:
                    sp.dma_start(dst, src.partition_broadcast(P)).then_inc(loaded, 16)
                sp.wait_ge(loaded, LOADED)

            @block.vector
            def _(dve):
                dve.wait_ge(loaded, LOADED)
                dve.tensor_copy(identb[:], ident[:])
                dve.tensor_copy(maskq[:], maskf[:].unsqueeze(1).broadcast_to([P, HG, P]))

            @block.gpsimd
            def _(pool):
                pool.memset(minus_half[:], -0.5).then_inc(init, 1)
                pool.memset(bout[:, 1, :], 0.0).then_inc(init, 1)
                for i in range(2):
                    pool.memset(v[i][:], 0.0).then_inc(init, 1)
                pool.wait_ge(init, 4)
                for i in range(2):
                    pool.memset(v[i][:, :, DK:DK + 1], 1.0).then_inc(init, 1)
                pool.wait_ge(init, 6)
                for s_, credit in ((x_stored[0], 16), (x_stored[1], 16), (t_y, 14), (e_o_made, 2), (e_gate_made, 2), (e_gate_kept, 1),
                                   (e_tmp, 2), (e_lo, 2), (e_acc, 8), (e_wlo, 2),
                                   (f_xres, 1), (f_xT_made, KT), (f_res, GB), (f_done, GB), (f_stored, 16), (f_xT_kept, 1), (f_wB_kept, 1),
                                   (f_silu, 1), (f_lo, 1), (f_hid, 3), (f_o_made, 2), (f_logit_made, 1), (f_wB_made, 1), (f_exp, 1)):
                    pool.sem_inc(s_, credit)

        start.close()

        def attention(stage, prefetch):
            scope = ExitStack()

            def sb(name, shape, dt=F32):
                return scope.enter_context(nc.sbuf_tensor(f"{name}_{stage}", shape, dt))

            x = [sb(f"x_{i}", [P, D]) for i in range(2)]
            cx = [sb(f"cx_{i}", [P, P]) for i in range(2)]
            xb = [sb(f"xb_{i}", [P, D]) for i in range(4)]
            xT = sb("xT", [P, KT + 1, P])
            qk = sb("qk", [P, 2, H, DK])
            kparts, qhigh, qlow = (sb(n, [P, H, 2, DK], F32R) for n in ("kparts", "qhigh", "qlow"))
            qhT, qlT = (sb(n, [P, NG, P], F32R) for n in ("qhT", "qlT"))
            kdiag = sb("kdiag", [P, NG, HG, P], F32R)
            negmax = sb("negmax", [P, NG, HG])
            probs = [sb(f"probs_{g}", [P, HG, P]) for g in range(NG)]
            probsT = [sb(f"probsT_{i}", [P, HG, P]) for i in range(2)]
            oT = sb("oT", [P, NG, P])
            rden = sb("rden", [P, H])
            att = sb("att", [P, D])
            attT = sb("attT", [P, KT, P])
            y = sb("y", [P, D])
            stats = sb("stats", [P, 6])
            mv = sb("mv", [P, 2])
            var = sb("var", [P, 1])
            rstd = sb("rstd", [P, 1])
            xo = [sb(f"xo_{i}", [P, D]) for i in range(2)]
            tmpa = sb("tmpa", [P, 2 * D])
            tmpb = sb("tmpb", [P, 2 * D])
            lin = sb("lin", [P, H])
            tanh_q = sb("tanh_q", [P, H])
            fac = sb("fac", [P, H])
            gz = sb("gz", [P, D])
            gth = sb("gth", [P, D])
            gated = sb("gated", [P, D])
            fill = sb("fill", [P, ROW])
            TL, TR = TB[:, 0:D], TB[:, D:2 * D]

            def attention_sp(sp, stage):
                src, dst = X_IN[stage], X_OUT[stage]

                def load(a):
                    wait(sp, xT_made, a.n - 1)
                    wait(sp, xb_done, a.n - 1)
                    sp.dma_start(x[a.p][:], src[bass.ds(a.b, 1)].rearrange("a p n -> (a p) n")).then_inc(x_loaded[a.p], 16)
                    if stage == CROSS:
                        sp.dma_start(cx[a.p][:], t["ctx"][bass.ds(a.b, 1)].rearrange("a p n -> (a p) n")).then_inc(x_loaded[a.p], 16)

                def store(a):
                    sp.wait_ge(ln_done, a.n + 1)
                    sp.dma_start(dst[bass.ds(a.b, 1)].rearrange("a p n -> (a p) n"), xo[a.p][:]).then_inc(x_stored[a.p], 16)

                for b in range(4):
                    load(at(stage, b))
                for to, what in prefetch:
                    sp.dma_start(to, what).then_inc(big_loaded, 16)
                with sp.Fori(0, (NB - 4) // 2) as j:
                    for u in range(2):
                        load(At(stage, j * 2 + (4 + u), j + 2, u))
                        store(At(stage, j * 2 + u, j, u))
                for b in range(NB - 4, NB):
                    store(at(stage, b))
                prefetched[0] += 16 * len(prefetch)
                wait(sp, big_loaded, prefetched[0])
                for i in range(2):
                    sp.wait_ge(x_stored[i], 16 * (NB // 2) * (stage + 1) + 16)

            def x_count(a, stage):
                return (a.half + 1) * (32 if stage == CROSS else 16) + 16 * (NB // 2) * stage

            def keep_kT(copy, r):
                rows = slice(HP * r, HP * (r + 1))
                return copy(kdiag[rows, :, r, :], QKB[rows, :].rearrange("p (g k) -> p g k", g=NG))

            def stored(l):
                return l.half * 16 + 16 * (NB // 2) * stage + 16

            def attention_pe(pe, stage):
                def transposes(dst, src_of, n, inc):
                    for k in range(n):
                        ins = pe.transpose(dst[:, k * P:(k + 1) * P], src_of(k), ident[:])
                    ins.then_inc(inc, 1)

                def step(p, a, c, l):
                    if a:
                        def heads(q):
                            return lambda g: q[:, HG * g:HG * (g + 1)].bitcast(F32).rearrange("p h a d -> p (h a d)")

                        pe.wait_ge(klow_kept, a.n + 1)
                        transposes(QKB, heads(kparts), NG, qkT_made)
                        pe.wait_ge(v_kept, a.n + 1)
                        pe.wait_ge(high_kept, 2 * a.n + 2)
                        transposes(VB, heads(qhigh), NG, qkT_made)
                    if l:
                        pe.wait_ge(att_kept, l.n + 1)
                        transposes(TL, lambda k: att[:, k * P:(k + 1) * P], KT, attT_made)
                    if a:
                        pe.wait_ge(qlow_kept, a.n + 1)
                        wait(pe, oT_kept, a.n - 1)
                        transposes(OTB, heads(qlow), NG, qkT_made)
                    if c:
                        probs_to_keys(c, 0)
                        probs_to_keys(c, 1)
                    if l and stage != SCALED:
                        product(l, wo[:, stage], proj_made)
                    if l and stage == SCALED:
                        product(l, gatew, gate_made)
                    if p:
                        pe.wait_ge(x_loaded[p.p], x_count(p, stage))
                        wait(pe, qT_kept, 2 * p.n - 1)
                        if stage == CROSS:
                            pe.transpose(VB[:, KT * P:(KT + 1) * P], cx[p.p][:], ident[:])
                        transposes(VB, lambda k: x[p.p][:, k * P:(k + 1) * P], KT, xT_made)
                    if a:
                        scores(a, 0)
                        scores(a, 1)
                    if c:
                        weighted_values(c, 0)
                        probs_to_keys(c, 2)
                    if l and stage == SCALED:
                        pe.wait_ge(gated_done, l.b + 1)
                        transposes(TL, lambda k: gated[:, k * P:(k + 1) * P], KT, gatedT_made)
                    if p:
                        pe.wait_ge(xT_kept, p.n + 1)
                        for i in range(2):
                            wait(pe, kT_kept[i], 2 * p.n)
                        if stage == CROSS:
                            for k in range(KT):
                                pe.matmul(QKB[:, 0:D], xT[:, k, :], wqkv[:, stage, k, 0:D], start=k == 0, stop=k == KT - 1)
                            ins = pe.matmul(QKB[:, D:2 * D], xT[:, KT, :], wqkv[:, stage, 0, D:2 * D], start=True, stop=True)
                        else:
                            for k in range(KT):
                                ins = pe.matmul(QKB[:], xT[:, k, :], wqkv[:, stage, k, 0:2 * D], start=k == 0, stop=k == KT - 1)
                        ins.then_inc(qkv_made, 1)
                    if c:
                        weighted_values(c, 1)
                        probs_to_keys(c, 3)
                    if l and stage == SCALED:
                        pe.wait_ge(gatedT_kept, l.b + 1)
                        product(l, wo[:, stage], proj_made)
                    if a:
                        scores(a, 2)
                    if p:
                        if stage == CROSS:
                            ins = pe.matmul(VB[:, 0:D], xT[:, KT, :], wqkv[:, stage, 0, 2 * D:3 * D], start=True, stop=True)
                        else:
                            for k in range(KT):
                                ins = pe.matmul(VB[:, 0:D], xT[:, k, :], wqkv[:, stage, k, 2 * D:3 * D], start=k == 0, stop=k == KT - 1)
                        ins.then_inc(qkv_made, 1)
                    if c:
                        weighted_values(c, 2)
                        weighted_values(c, 3)
                    if a:
                        scores(a, 3)
                    if c:
                        pe.wait_ge(oT_kept, c.n + 1)
                        wait(pe, res_done, c.n)
                        transposes(TB, lambda k: oT[:, k, :], NG, o_made)

                def product(l, w, inc):
                    pe.wait_ge(attT_kept, l.n + 1)
                    wait(pe, res_done, l.n)
                    for k in range(KT):
                        ins = pe.matmul(TR, attT[:, k, :], w[:, k, :], start=k == 0, stop=k == KT - 1)
                    ins.then_inc(inc, 1)

                def scores(a, g):
                    if g == 0:
                        pe.wait_ge(qT_kept, 2 * a.n + 2)
                        for i in range(2):
                            pe.wait_ge(kT_kept[i], 2 * a.n + 2)
                    wait(pe, probs_kept, 4 * a.n + g - 1)
                    s = SB[g % 2]
                    if stage == CAUSAL:
                        pe.matmul(s[:], identb[:], maskq[:], start=True, stop=False)
                    pe.matmul(s[:], qhT[:, g, :], kdiag[:, g], start=stage != CAUSAL, stop=False)
                    pe.matmul(s[:], qlT[:, g, :], kdiag[:, g], start=False, stop=True).then_inc(s_made, 1)

                def probs_to_keys(c, g):
                    pe.wait_ge(probs_kept, 4 * c.n + g + 1)
                    wait(pe, probsT_kept, 4 * c.n + g - 1)
                    transposes(PTB[g % 2], lambda r: probs[g][:, r, :], HG, probsT_made)

                def weighted_values(c, g):
                    if g == 0:
                        wait(pe, oT_kept, c.n)
                        pe.wait_ge(v_kept, c.n + 1)
                    pe.wait_ge(probsT_kept, 4 * c.n + g + 1)
                    for r in range(HG):
                        ins = pe.matmul(OTB[HP * r:HP * (r + 1), g * P:(g + 1) * P], v[c.p][:, HG * g + r, :],
                                        probsT[g % 2][:, r, :], start=True, stop=True, skip_group_check=True)
                    ins.then_inc(av_made, 1)

                attention_steps(pe, stage, step)

            def attention_act(act, stage):
                def softmax_numerators(a, g):
                    act.wait_ge(max_kept, 4 * a.n + g + 1)
                    wait(act, probsT_made, 4 * a.n + g - 3)
                    for r in range(HG):
                        ins = act.activation(probs[g][:, r, :], SB[g % 2][:, r * P:(r + 1) * P], ACT.Exp, bias=negmax[:, g, r:r + 1])
                    ins.then_inc(probs_kept, 1)

                def step(p, a, c, l):
                    if a:
                        act.wait_ge(qkT_made, 3 * a.n + 1)
                        wait(act, s_made, 4 * a.n)
                        for r in range(HG // 2):
                            keep_kT(act.copy, r).then_inc(kT_kept[0], 1)
                    if l:
                        act.wait_ge(attT_made, l.n + 1)
                        wait(act, proj_made, l.n)
                        act.copy(attT[:], TL).then_inc(attT_kept, 1)
                    if a:
                        act.wait_ge(qkT_made, 3 * a.n + 2)
                        act.mul(qhT[:], VB[:], float(DK) ** -0.5).then_inc(qT_kept, 1)
                        act.wait_ge(qkT_made, 3 * a.n + 3)
                        act.mul(qlT[:], OTB[:], float(DK) ** -0.5).then_inc(qT_kept, 1)
                    if c:
                        softmax_numerators(c, 3)
                    if p:
                        act.wait_ge(xT_made, p.n + 1)
                        wait(act, qkv_made, 2 * p.n)
                        n = KT + 1 if stage == CROSS else KT
                        act.copy(xT[:, 0:n, :], VB[:, 0:n * P]).then_inc(xT_kept, 1)
                    if l and stage == SCALED:
                        act.wait_ge(gz_done, l.b + 1)
                        wait(act, gated_done, l.b)
                        act.activation(gth[:], gz[:], ACT.Tanh, scale=0.5).then_inc(gth_done, 1)
                    if a:
                        softmax_numerators(a, 0)
                    if l and stage == SCALED:
                        act.wait_ge(gatedT_made, l.b + 1)
                        act.mul(attT[:], TL, 0.5).then_inc(gatedT_kept, 1)
                    if a:
                        softmax_numerators(a, 1)
                    if p and stage == SCALED:
                        act.wait_ge(lin_step, 2 * p.b + 2)
                        wait(act, fac_done, p.b)
                        act.activation(tanh_q[:], lin[:], ACT.Tanh, scale=0.5).then_inc(tanh_done, 1)
                    if p:
                        act.wait_ge(qk_kept, p.n + 1)
                        wait(act, qkT_made, 3 * p.n)
                        act.copy(kparts[:, :, 0, :], qk[:, 1]).then_inc(high_kept, 1)
                        act.copy(qhigh[:], qk[:, 0].unsqueeze(2).broadcast_to([P, H, 2, DK])).then_inc(high_kept, 1)
                    if c:
                        act.wait_ge(av_made, 4 * c.n + 4)
                        wait(act, o_made, c.n)
                        act.copy(oT[:], OTB[:]).then_inc(oT_kept, 1)
                    if p and (stage == SCALED or stage == ROTARY):
                        act.wait_ge(qkv_made, 2 * p.n + 2)
                        wait(act, av_made, 4 * p.n - 4)
                        act.copy(v[p.p][:, :, 0:DK], VB[:, 0:D].rearrange("p (h d) -> p h d", h=H)).then_inc(v_kept, 1)
                    if a:
                        softmax_numerators(a, 2)

                act.wait_ge(kdiag_cleared, stage + 1)
                attention_steps(act, stage, step)

            def attention_dve(dve, stage):
                def step(p, a, c, l):
                    if a:
                        dve.wait_ge(qkT_made, 3 * a.n + 1)
                        wait(dve, s_made, 4 * a.n)
                        dve.sem_inc(passed, 1)
                        for r in range(HG // 2, HG):
                            keep_kT(dve.tensor_copy, r).then_inc(kT_kept[1], 1)
                    if c:
                        keep_probs(c, 0)
                        keep_probs(c, 1)
                    if l and stage != SCALED:
                        residual(l)
                        statistics(l)
                    if l and stage == SCALED:
                        dve.wait_ge(gate_made, l.b + 1)
                        wait(dve, gth_done, l.b)
                        dve.tensor_tensor(gz[:], TR, gateb[:], ALU.add).then_inc(gz_done, 1)
                    if a:
                        row_max(a, 0)
                    if l and stage == SCALED:
                        dve.wait_ge(gth_done, l.b + 1)
                        wait(dve, gatedT_made, l.b)
                        dve.scalar_tensor_tensor(gated[:], gth[:], 1.0, att[:], ALU.add, ALU.mult).then_inc(gated_done, 1)
                    if a:
                        row_max(a, 1)
                    if c:
                        keep_probs(c, 2)
                    if p:
                        dve.wait_ge(qkv_made, 2 * p.n + 1)
                        wait(dve, klow_kept, p.n)
                        wait(dve, qlow_kept, p.n)
                        made = QKB[:].rearrange("p (a h d) -> p a h d", a=2, h=H)
                        if stage == CAUSAL or stage == CROSS:
                            bias = bqkv[:, 0 if stage == CAUSAL else 1, 0:2 * D].rearrange("p (a h d) -> p a h d", a=2, h=H)
                            dve.tensor_tensor(qk[:], made, bias, ALU.add).then_inc(qk_kept, 1)
                        if stage == SCALED:
                            dve.tensor_tensor(tmpa[:, 0:D], QKB[:, 0:D], scalew[:], ALU.mult).then_inc(lin_step, 1)
                            dve.wait_ge(lin_step, 2 * p.b + 1)
                            dve.tensor_reduce(lin[:], tmpa[:, 0:D].rearrange("p (h d) -> p h d", h=H), AX.X, ALU.add).then_inc(lin_step, 1)
                            dve.tensor_copy(qk[:, 1], QKB[:, D:2 * D].rearrange("p (h d) -> p h d", h=H))
                            dve.wait_ge(tanh_done, p.b + 1)
                            dve.tensor_scalar(fac[:], tanh_q[:], 1.0, None, ALU.add).then_inc(fac_done, 1)
                            dve.wait_ge(fac_done, p.b + 1)
                            dve.tensor_tensor(qk[:, 0], QKB[:, 0:D].rearrange("p (h d) -> p h d", h=H),
                                              fac[:].unsqueeze(2).broadcast_to([P, H, DK]), ALU.mult).then_inc(qk_kept, 1)
                        if stage == ROTARY:
                            made4 = QKB[:].rearrange("p (h c d) -> p h c d", h=2 * H, c=2)
                            tb = tmpb[:].rearrange("p (h c d) -> p h c d", h=2 * H, c=2)
                            half = DK // 2
                            dve.tensor_tensor(tmpa[:].rearrange("p (h d) -> p h d", d=half), QKB[:].rearrange("p (h d) -> p h d", d=half),
                                              cosb[:].unsqueeze(1).broadcast_to([P, 4 * H, half]), ALU.mult).then_inc(rope_step, 1)
                            for i in range(2):
                                dve.tensor_tensor(tb[:, :, i, :], made4[:, :, 1 - i, :],
                                                  sinb[:, i, :].unsqueeze(1).broadcast_to([P, 2 * H, half]), ALU.mult).then_inc(rope_step, 1)
                            dve.wait_ge(rope_step, 3 * p.b + 3)
                            dve.tensor_tensor(qk[:].rearrange("p a h d -> p (a h) d"), tmpa[:].rearrange("p (h d) -> p h d", d=DK),
                                              tmpb[:].rearrange("p (h d) -> p h d", d=DK), ALU.add).then_inc(qk_kept, 1)
                    if c:
                        keep_probs(c, 3)
                    if l and stage == SCALED:
                        residual(l)
                    if a:
                        row_max(a, 2)
                    if p:
                        dve.wait_ge(high_kept, 2 * p.n + 1)
                        wait(dve, qkT_made, 3 * p.n)
                        dve.tensor_tensor(kparts[:, :, 1, :], qk[:, 1], kparts[:, :, 0, :].bitcast(F32), ALU.subtract).then_inc(klow_kept, 1)
                    if l and stage == SCALED:
                        statistics(l)
                    if p and (stage == CAUSAL or stage == CROSS):
                        dve.wait_ge(qkv_made, 2 * p.n + 2)
                        wait(dve, av_made, 4 * p.n - 4)
                        bias = bqkv[:, 0 if stage == CAUSAL else 1, 2 * D:3 * D].rearrange("p (h d) -> p h d", h=H)
                        dve.tensor_tensor(v[p.p][:, :, 0:DK], VB[:, 0:D].rearrange("p (h d) -> p h d", h=H), bias, ALU.add).then_inc(v_kept, 1)
                    if a:
                        row_max(a, 3)
                    if c:
                        dve.wait_ge(o_made, c.n + 1)
                        made = TB[:].rearrange("p (h d) -> p h d", h=H)
                        wait(dve, att_kept, c.n)
                        dve.reciprocal(rden[:], made[:, :, DK]).then_inc(rden_done, 1)
                        dve.wait_ge(rden_done, c.n + 1)
                        wait(dve, attT_made, c.n)
                        if stage == SCALED:
                            wait(dve, gated_done, c.b)
                        dve.tensor_tensor(att[:].rearrange("p (h d) -> p h d", h=H), made[:, :, 0:DK],
                                          rden[:].unsqueeze(2).broadcast_to([P, H, DK]), ALU.mult).then_inc(att_kept, 1)
                    if l:
                        normalise(l)

                def keep_probs(c, g):
                    dve.wait_ge(probsT_made, 4 * c.n + g + 1)
                    wait(dve, av_made, 4 * c.n + g - 1)
                    dve.tensor_copy(probsT[g % 2][:].rearrange("p r q -> p (r q)"), PTB[g % 2][:]).then_inc(probsT_kept, 1)

                def row_max(a, g):
                    dve.wait_ge(s_made, 4 * a.n + g + 1)
                    dve.tensor_reduce(negmax[:, g, :], SB[g % 2][:].rearrange("p (r k) -> p r k", r=HG),
                                      AX.X, ALU.max, negate=True).then_inc(max_kept, 1)

                def residual(l):
                    dve.wait_ge(proj_made, l.n + 1)
                    dve.wait_ge(xb_done, l.n + 1)
                    wait(dve, ln_done, l.n)
                    dve.tensor_tensor(y[:], TR, xb[l.q][:], ALU.add).then_inc(res_done, 1)

                def statistics(l):
                    dve.wait_ge(res_done, l.n + 1)
                    dve.bn_stats(stats[:], y[:]).then_inc(ln_step, 1)
                    dve.wait_ge(ln_step, 3 * l.n + 1)
                    dve.sem_inc(passed, 1)
                    dve.bn_aggr(mv[:], stats[:]).then_inc(ln_step, 1)
                    dve.wait_ge(ln_step, 3 * l.n + 2)
                    dve.tensor_scalar(var[:], mv[:, 1:2], EPS, None, ALU.add).then_inc(ln_step, 1)

                def normalise(l):
                    dve.wait_ge(rstd_done, l.n + 1)
                    if stage == SCALED:
                        wait(dve, ln_done, l.n)
                        dve.tensor_scalar(tmpb[:, 0:D], y[:], mv[:, 0:1], rstd[:], ALU.subtract, ALU.mult).then_inc(n1_step, 1)
                    else:
                        wait(dve, x_stored[l.p], stored(l))
                        dve.tensor_scalar(xo[l.p][:], y[:], mv[:, 0:1], rstd[:], ALU.subtract, ALU.mult).then_inc(ln_done, 1)

                dve.memset(kdiag[:].bitcast(F32).rearrange("p g r k -> p (g r k)"), 0.0).then_inc(kdiag_cleared, 1)
                dve.wait_ge(kdiag_cleared, stage + 1)
                attention_steps(dve, stage, step)

            def attention_pool(pool, stage):
                def step(p, a, c, l):
                    if p:
                        pool.wait_ge(x_loaded[p.p], x_count(p, stage))
                        wait(pool, res_done, p.n - 3)
                        pool.tensor_tensor(xb[p.q][:], x[p.p][:], bout[:, stage, :], ALU.add).then_inc(xb_done, 1)
                        pool.wait_ge(high_kept, 2 * p.n + 2)
                        wait(pool, qkT_made, 3 * p.n)
                        pool.tensor_tensor(qlow[:], qk[:, 0].unsqueeze(2).broadcast_to([P, H, 2, DK]),
                                           qhigh[:].bitcast(F32), ALU.subtract).then_inc(qlow_kept, 1)
                    if l:
                        pool.wait_ge(ln_step, 3 * l.n + 3)
                        wait(pool, ln_done, l.n)
                        pool.tensor_tensor(rstd[:], var[:], minus_half[:, 0:1], ALU.pow).then_inc(rstd_done, 1)
                    if l and stage == SCALED:
                        pool.wait_ge(n1_step, 2 * l.b + 1)
                        pool.tensor_tensor(tmpb[:, D:2 * D], tmpb[:, 0:D], n1g[:], ALU.mult).then_inc(n1_step, 1)
                        pool.wait_ge(n1_step, 2 * l.b + 2)
                        wait(pool, x_stored[l.p], stored(l))
                        pool.tensor_tensor(xo[l.p][:], tmpb[:, D:2 * D], n1b[:], ALU.add).then_inc(ln_done, 1)

                if stage == SCALED:
                    pool.memset(fill[:], 0.0).then_inc(fill_step, 1)
                    pool.wait_ge(fill_step, 1)
                    pool.memset(fill[:].bitcast(I32)[:, 2 * D + 1:2 * D + 2], TOK).then_inc(fill_step, 1)
                    pool.wait_ge(fill_step, 2)
                    pool.dma_start(routed.rearrange("(s p) r -> p s r", p=P),
                                   fill[:].unsqueeze(1).broadcast_to([P, SLOTS, ROW])).then_inc(filled, 16)
                attention_steps(pool, stage, step)
                if stage == SCALED:
                    pool.wait_ge(filled, 16)

            with nc.Block() as block:
                @block.sync
                def _(sp):
                    attention_sp(sp, stage)

                @block.tensor
                def _(pe):
                    attention_pe(pe, stage)

                @block.scalar
                def _(act):
                    attention_act(act, stage)

                @block.vector
                def _(dve):
                    attention_dve(dve, stage)

                @block.gpsimd
                def _(pool):
                    attention_pool(pool, stage)

            scope.close()

        R_ONEHOT, R_DIFF = 12, 13
        Y_C, O_C, GATE_C, KEPT_C, TMP_C, LO_C, ACC_C, WLO_C = 14, 2, 2, 1, 2, 2, 8, 2
        STEP = 2 * NGR

        def experts0(ctxs, itok, w_raw):
            scope = ExitStack()

            def sb(name, shape, dt=F32):
                return scope.enter_context(nc.sbuf_tensor(name, shape, dt))

            acc = sb("acc", [P, NB, D])
            xTh, xTl = (sb(f"xT_{n}", [P, KT, TOK], F32R) for n in ("high", "low"))
            itokf = itok[:].bitcast(F32)
            number = [sb(f"number_{i}", [P, 1]) for i in range(2)]
            wah, wal = ([sb(f"wa_{n}_{i}", [P, KT, HID], F32R) for i in range(2)] for n in ("high", "low"))
            wbh, wbl = ([sb(f"wb_{n}_{i}", [P, HC, D], F32R) for i in range(2)] for n in ("high", "low"))
            masked = [sb(f"masked_{i}", [P, GB * P]) for i in range(2)]
            gateB = [sb(f"gateB_{i}", [P, GB * P]) for i in range(2)]
            hidden = [sb(f"hidden_{i}", [P, GB * P]) for i in range(2)]
            hidh, hidl = ([sb(f"hid_{n}_{i}", [P, HC, GB * P], F32R) for i in range(2)] for n in ("high", "low"))
            stg = sb("stg", [P, NB, 6])
            mvg = sb("mvg", [P, NB, 2])
            varg = sb("varg", [P, NB])
            rstdg = sb("rstdg", [P, NB])

            def cols(g):
                return slice(g * GB * P, (g + 1) * GB * P)

            def flat(a):
                return a.rearrange("p a b -> p (a b)")

            with nc.Block() as block:
                @block.sync
                def _(sp):
                    def load_half(e, i):
                        sp.wait_ge(e_wlo, e * 2 + (i + WLO_C))
                        sp.dma_start(w_raw[:], t[("wa0", "wb0")[i]][bass.ds(e, 1)].rearrange("a p n -> (a p) n")).then_inc(e_wloaded, 16)

                    for g in range(NGR):
                        sp.dma_start(acc[:, g * GB:(g + 1) * GB, :], x1[g * GB:(g + 1) * GB].rearrange("b p n -> p b n")).then_inc(e_loaded[g], 16)

                    def load(e):
                        for i in range(2):
                            load_half(e, i)

                    load_half(0, 1)
                    with sp.Fori(0, E - 1) as e:
                        load(e + 1)
                    for g in range(NGR):
                        sp.wait_ge(e_done, (g + 1) * GB)
                        sp.dma_start(x2[g * GB:(g + 1) * GB].rearrange("b p n -> p b n"), acc[:, g * GB:(g + 1) * GB, :]).then_inc(e_stored, 16)
                    sp.wait_ge(e_stored, 16 * NGR)

                @block.gpsimd
                def _(pool):
                    def split(e, i, last):
                        pool.wait_ge(e_o_made, last)
                        for k, (high, low) in enumerate(((wah, wal), (wbh, wbl))):
                            wait(pool, e_wloaded, e * 32 + 16 * k)
                            pool.sem_inc(passed, 1)
                            pool.tensor_copy(flat(high[i][:]), w_raw[:]).then_inc(e_whi, 1)
                            pool.wait_ge(e_whi, e * 2 + (k + 1))
                            pool.tensor_tensor(flat(low[i][:]), w_raw[:], flat(high[i][:].bitcast(F32)), ALU.subtract).then_inc(e_wlo, 1)

                    split(0, 0, O_C)
                    with pool.Fori(0, E // 2 - 1) as j:
                        for u in range(2):
                            split(j * 2 + (u + 1), 1 - u, j * STEP + (u * NGR + O_C))
                    split(E - 1, 1, (E - 2) * NGR + O_C)
                    for g in range(NGR):
                        b = slice(g * GB, (g + 1) * GB)
                        pool.wait_ge(e_ln, (g + 1) * (2 * GB + 1))
                        pool.tensor_tensor(rstdg[:, b], varg[:, b], minus_half[:, b], ALU.pow).then_inc(e_rstd, 1)

                @block.tensor
                def _(pe):
                    def gates(m, i):
                        pe.wait_ge(e_masked, m + 1)
                        pe.wait_ge(e_gate_kept, m + 1)
                        pe.matmul(bank[6][:], ones[:], masked[i % 2][:], start=True, stop=True).then_inc(e_gate_made, 1)

                    def first(m, e, i):
                        u, g = i // NGR, i % NGR
                        if g == 0:
                            pe.wait_ge(e_wlo, e * 2 + (1 + WLO_C))
                        for c in range(HC):
                            z = bank[4 + c % 2]
                            pe.wait_ge(e_tmp, m * HC + (c - 1 + TMP_C))
                            w = slice(c * P, (c + 1) * P)
                            for k in range(KT):
                                pe.matmul(z[:], wah[u][:, k, w], xTh[:, k, cols(g)], start=k == 0, stop=False)
                                pe.matmul(z[:], wah[u][:, k, w], xTl[:, k, cols(g)], start=False, stop=False)
                                ins = pe.matmul(z[:], wal[u][:, k, w], xTh[:, k, cols(g)], start=False, stop=k == KT - 1)
                            ins.then_inc(e_z_made, 1)

                    def second(m, e, i):
                        u = i // NGR
                        if i % NGR == 0:
                            pe.wait_ge(e_wlo, e * 2 + (2 + WLO_C))
                        pe.wait_ge(e_hi, m * HC + HC)
                        pe.wait_ge(e_lo, m * HC + (HC + LO_C))
                        pe.wait_ge(e_acc, m * 2 + (ACC_C - 2))
                        for b in range(GB):
                            o = bank[2 * (i % 2) + b // 2][:, (b % 2) * D:(b % 2 + 1) * D]
                            w = slice(b * P, (b + 1) * P)
                            for c in range(HC):
                                pe.matmul(o, hidh[i % 2][:, c, w], wbh[u][:, c, :], start=c == 0, stop=False)
                                pe.matmul(o, hidh[i % 2][:, c, w], wbl[u][:, c, :], start=False, stop=False)
                                ins = pe.matmul(o, hidl[i % 2][:, c, w], wbh[u][:, c, :], start=False, stop=c == HC - 1)
                        ins.then_inc(e_o_made, 1)

                    for g in range(NGR):
                        pe.wait_ge(e_loaded[g], 16)
                        for k in range(KT):
                            n = g * KT + k
                            wait(pe, e_xTl, n - 3)
                            for b in range(GB):
                                ins = pe.transpose(bank[n % 4][:, b * P:(b + 1) * P], acc[:, g * GB + b, k * P:(k + 1) * P], ident[:])
                            ins.then_inc(e_xT_made, 1)
                    gates(0, 0)
                    pe.wait_ge(e_xTl, KT * NGR)
                    with pe.Fori(0, E // 2) as j:
                        for i in range(STEP):
                            m = j * STEP + i
                            first(m, j * 2 + i // NGR, i)
                            gates(m + 1, i + 1)
                            if i:
                                second(j * STEP + (i - 1), j * 2 + (i - 1) // NGR, i - 1)
                        second(j * STEP + (STEP - 1), j * 2 + 1, STEP - 1)

                @block.scalar
                def _(act):
                    def keep_gates(m, i):
                        act.wait_ge(e_gate_made, m + (1 + GATE_C))
                        act.wait_ge(e_tmp, m * HC + (TMP_C - HC))
                        act.copy(gateB[i % 2][:], bank[6][:]).then_inc(e_gate_kept, 1)

                    for n in range(KT * NGR):
                        act.wait_ge(e_xT_made, n + 1)
                        act.copy(xTh[:, n % KT, cols(n // KT)], bank[n % 4][:]).then_inc(e_xTh, 1)
                    act.wait_ge(e_gate_made, 1 + GATE_C)
                    act.copy(gateB[0][:], bank[6][:]).then_inc(e_gate_kept, 1)
                    with act.Fori(0, E // 2) as j:
                        for i in range(STEP):
                            m = j * STEP + i
                            act.wait_ge(e_o_made, m + (O_C - 1))
                            for c in range(HC):
                                act.wait_ge(e_tmp, m * HC + (c + 1 + TMP_C))
                                act.copy(hidh[i % 2][:, c, :], hidden[c % 2][:]).then_inc(e_hi, 1)
                            keep_gates(m + 1, i + 1)

                @block.vector
                def _(dve):
                    def mask(m, i):
                        u, g = i // NGR % 2, i % NGR
                        dve.wait_ge(e_gate_made, m + (GATE_C - 1))
                        dve.scalar_tensor_tensor(masked[i % 2][:], itokf[:, cols(g)], number[u][:], ctxs[:, cols(g)],
                                                 ALU.is_equal, ALU.mult).then_inc(e_masked, 1)

                    def gated(m, i, c):
                        dve.wait_ge(e_z_made, m * HC + (c + 1))
                        dve.wait_ge(e_lo, m * HC + (c - 1 + LO_C))
                        dve.scalar_tensor_tensor(hidden[c % 2][:], bank[4 + c % 2][:], 0.0, gateB[i % 2][:],
                                                 ALU.max, ALU.mult).then_inc(e_tmp, 1)

                    def low(m, i, c):
                        dve.wait_ge(e_hi, m * HC + (c + 1))
                        dve.tensor_tensor(hidl[i % 2][:, c, :], hidden[c % 2][:], hidh[i % 2][:, c, :].bitcast(F32), ALU.subtract).then_inc(e_lo, 1)

                    def add(m, i, h):
                        if h == 0:
                            dve.wait_ge(e_o_made, m + (1 + O_C))
                            dve.wait_ge(e_acc, m * 2 + (ACC_C - 6))
                        b = i % NGR * GB + 2 * h
                        dve.tensor_tensor(flat(acc[:, b:b + 2, :]), flat(acc[:, b:b + 2, :]), bank[2 * (i % 2) + h][:], ALU.add).then_inc(e_acc, 1)

                    LN = 2 * GB + 1

                    def statistics(g):
                        for b in range(g * GB, (g + 1) * GB):
                            dve.bn_stats(stg[:, b, :], acc[:, b, :]).then_inc(e_ln, 1)
                        dve.wait_ge(e_ln, g * LN + GB)
                        for b in range(g * GB, (g + 1) * GB):
                            dve.bn_aggr(mvg[:, b, :], stg[:, b, :]).then_inc(e_ln, 1)
                        dve.wait_ge(e_ln, g * LN + 2 * GB)
                        b = slice(g * GB, (g + 1) * GB)
                        dve.tensor_scalar(varg[:, b], mvg[:, b, 1], EPS, None, ALU.add).then_inc(e_ln, 1)

                    def normalise(g):
                        dve.wait_ge(e_rstd, g + 1)
                        for b in range(g * GB, (g + 1) * GB):
                            dve.tensor_scalar(acc[:, b, :], acc[:, b, :], mvg[:, b, 0:1], rstdg[:, b:b + 1],
                                              ALU.subtract, ALU.mult).then_inc(e_done, 1)

                    for u in range(2):
                        dve.memset(number[u][:], float(u)).then_inc(e_number, 1)
                    dve.tensor_copy(itokf, itok[:]).then_inc(e_itokf, 1)
                    dve.wait_ge(e_itokf, 1)
                    dve.wait_ge(e_number, 2)
                    mask(0, 0)
                    for n in range(KT * NGR):
                        dve.wait_ge(e_xTh, n + 1)
                        dve.tensor_tensor(xTl[:, n % KT, cols(n // KT)], bank[n % 4][:], xTh[:, n % KT, cols(n // KT)].bitcast(F32),
                                          ALU.subtract).then_inc(e_xTl, 1)
                    with dve.Fori(0, E // 2) as j:
                        for i in range(STEP):
                            m = j * STEP + i
                            if (i + 1) % NGR == 0:
                                dve.wait_ge(e_number, j * 2 + ((i + 1) // NGR + 1))
                            mask(m + 1, i + 1)
                            dve.wait_ge(e_gate_kept, m + (1 + KEPT_C))
                            dve.wait_ge(e_o_made, m + (O_C - 1))
                            gated(m, i, 0)
                            gated(m, i, 1)
                            low(m, i, 0)
                            if i >= 2:
                                add(j * STEP + (i - 2), i - 2, 0)
                            gated(m, i, 2)
                            low(m, i, 1)
                            if i >= 2:
                                add(j * STEP + (i - 2), i - 2, 1)
                            gated(m, i, 3)
                            low(m, i, 2)
                            low(m, i, 3)
                            if i % NGR == 2:
                                dve.wait_ge(e_masked, m + 2)
                                dve.tensor_scalar(number[i // NGR][:], number[i // NGR][:], 2.0, None, ALU.add).then_inc(e_number, 1)
                        for i in (STEP - 2, STEP - 1):
                            for h in range(2):
                                add(j * STEP + i, i, h)
                    dve.wait_ge(e_acc, E * NGR * 2 + ACC_C)
                    for g in range(NGR):
                        statistics(g)
                        if g:
                            normalise(g - 1)
                    normalise(NGR - 1)

            scope.close()

        def routing(posu, meta, se):
            scope = ExitStack()

            def sb(name, shape, dt=F32):
                return scope.enter_context(nc.sbuf_tensor(name, shape, dt))

            rows = sb("rows", [P, NB, ROW])
            xinT = [sb(f"r_xinT_{i}", [P, KT, GB * P]) for i in range(2)]
            lg = sb("lg", [P, NB, E])

            def row(name, shape=(NB, E)):
                return sb("r_" + name, [P, *shape])

            v1, v2, c1, c2, chosen = (row(n, (NB,)) for n in ("v1", "v2", "c1", "c2", "chosen"))
            diff, e2, den, r1, r2 = (row(n, (NB,)) for n in ("diff", "e2", "den", "r1", "r2"))
            eq, cand, hit, lg2, eq2, cand2 = (row(n) for n in ("eq", "cand", "hit", "lg2", "eq2", "cand2"))
            onehot, tot, upto, full, p1, p2, p3, p4 = (row(n, (E, NB)) for n in ("onehot", "tot", "upto", "full", "p1", "p2", "p3", "p4"))
            tiles, cum, base0, base = (row(n, (E,)) for n in ("tiles", "cum", "base0", "base"))
            post, started, sef = row("post", (NB,)), row("started", (SLOTS, E)), row("sef", (SLOTS,))
            flat = lambda a: a[:].rearrange("p a b -> p (a b)")
            over = lambda a: a[:].unsqueeze(2).broadcast_to([P, NB, E])

            def logits(pe, g):
                pe.wait_ge(r_xT_kept, (g + 1) * KT)
                wait(pe, r_logit_kept, g - 1)
                for b in range(GB):
                    for k in range(KT):
                        ins = pe.matmul(bank[4 + g % 2][:, b * E:(b + 1) * E], xinT[g % 2][:, k, b * P:(b + 1) * P], wlog[:, k, :],
                                        start=k == 0, stop=k == KT - 1)
                ins.then_inc(r_logit_made, 1)

            down = descend[:].unsqueeze(1).broadcast_to([P, NB, E])

            with nc.Block() as block:
                @block.sync
                def _(sp):
                    for g in range(NGR):
                        b = slice(g * GB, (g + 1) * GB)
                        sp.dma_start(rows[:, b, 0:D], xr[b].rearrange("b p n -> p b n")).then_inc(r_loaded[g], 16)
                    sp.dma_start(rows[:, :, D:2 * D], x2.rearrange("b p n -> p b n")).then_inc(row_loaded, 16)

                @block.vector
                def _(dve):
                    for g in range(NGR):
                        dve.wait_ge(r_logit_made, g + 1)
                        dve.tensor_tensor(lg[:, g * GB:(g + 1) * GB, :], bank[4 + g % 2][:, 0:GB * E].rearrange("p (b e) -> p b e", b=GB),
                                          blog[:].unsqueeze(1).broadcast_to([P, GB, E]), ALU.add).then_inc(r_logit_kept, 1)
                    dve.wait_ge(r_logit_kept, NGR)
                    steps = [0]

                    def link(ins):
                        steps[0] += 1
                        ins.then_inc(r_step, 1)
                        dve.wait_ge(r_step, steps[0])

                    link(dve.tensor_reduce(v1[:], lg[:], AX.X, ALU.max))
                    link(dve.tensor_tensor(eq[:], lg[:], over(v1), ALU.is_equal))
                    link(dve.tensor_tensor(cand[:], eq[:], down, ALU.mult))
                    link(dve.tensor_reduce(c1[:], cand[:], AX.X, ALU.max))
                    link(dve.tensor_tensor(hit[:], down, over(c1), ALU.is_equal))
                    link(dve.scalar_tensor_tensor(flat(lg2), flat(hit), -BIG, flat(lg), ALU.mult, ALU.add))
                    link(dve.tensor_reduce(v2[:], lg2[:], AX.X, ALU.max))
                    link(dve.tensor_tensor(eq2[:], lg2[:], over(v2), ALU.is_equal))
                    link(dve.tensor_tensor(cand2[:], eq2[:], down, ALU.mult))
                    link(dve.tensor_reduce(c2[:], cand2[:], AX.X, ALU.max))
                    link(dve.tensor_tensor(chosen[:], c1[:], c2[:], ALU.min))
                    link(dve.tensor_tensor(onehot[:].rearrange("p e b -> p b e"), down, over(chosen), ALU.is_equal))
                    assert steps[0] == R_ONEHOT
                    link(dve.tensor_tensor(diff[:], v2[:], v1[:], ALU.subtract))
                    assert steps[0] == R_DIFF
                    dve.wait_ge(r_exp, 1)
                    link(dve.tensor_scalar(den[:], e2[:], 1.0, None, ALU.add))
                    link(dve.reciprocal(r1[:], den[:]))
                    link(dve.tensor_tensor(r2[:], e2[:], r1[:], ALU.mult))
                    dve.wait_ge(r_meta, 2)
                    link(dve.tensor_tensor(meta[:, :, 0], r1[:], r2[:], ALU.add))
                    dve.wait_ge(r_rank, 2)
                    link(dve.tensor_copy(flat(tot), bank[1][:, 0:E * NB]))
                    link(dve.tensor_tensor_scan(flat(upto), flat(keepmask), flat(tot), 0.0, ALU.mult, ALU.add))
                    link(dve.tensor_tensor(full[:], upto[:, :, NB - 1].unsqueeze(2).broadcast_to([P, E, NB]), iotas[:], ALU.is_gt))
                    link(dve.tensor_reduce(tiles[:], full[:], AX.X, ALU.add))
                    link(dve.tensor_tensor_scan(cum[:], ones[:, 0:E], tiles[:], 0.0, ALU.mult, ALU.add))
                    link(dve.tensor_tensor(base0[:], cum[:], tiles[:], ALU.subtract))
                    link(dve.tensor_scalar(base[:], base0[:], float(P), None, ALU.mult))
                    link(dve.tensor_tensor(flat(p1), bank[0][:, 0:E * NB], flat(upto), ALU.add))
                    link(dve.tensor_tensor(flat(p2), flat(p1), flat(tot), ALU.subtract))
                    link(dve.tensor_tensor(p3[:], p2[:], base[:].unsqueeze(2).broadcast_to([P, E, NB]), ALU.add))
                    link(dve.tensor_tensor(flat(p4), flat(p3), flat(onehot), ALU.mult))
                    link(dve.tensor_reduce(post[:], p4[:].rearrange("p e b -> p b e"), AX.X, ALU.add))
                    link(dve.tensor_copy(posu[:], post[:]))
                    dve.tensor_copy(rows[:, :, 2 * D:ROW], meta[:]).then_inc(row_meta, 1)
                    link(dve.tensor_tensor(started[:], slotn[:], cum[:].unsqueeze(1).broadcast_to([P, SLOTS, E]), ALU.is_ge))
                    link(dve.tensor_reduce(sef[:], started[:], AX.X, ALU.add))
                    link(dve.tensor_scalar(se[:], sef[:], float(E - 1), None, ALU.min))

                @block.scalar
                def _(act):
                    for g in range(NGR):
                        for k in range(KT):
                            act.wait_ge(r_xT_made, g * KT + k + 1)
                            wait(act, r_logit_made, g - 1)
                            act.copy(xinT[g % 2][:, k, :], bank[2 * (g % 2) + k][:]).then_inc(r_xT_kept, 1)
                    act.wait_ge(r_step, R_DIFF)
                    act.activation(e2[:], diff[:], ACT.Exp).then_inc(r_exp, 1)

                @block.tensor
                def _(pe):
                    for g in range(NGR):
                        pe.wait_ge(r_loaded[g], 16)
                        wait(pe, r_xT_kept, (g - 1) * KT)
                        for k in range(KT):
                            for b in range(GB):
                                ins = pe.transpose(bank[2 * (g % 2) + k][:, b * P:(b + 1) * P], rows[:, g * GB + b, k * P:(k + 1) * P], ident[:])
                            ins.then_inc(r_xT_made, 1)
                        if g:
                            logits(pe, g - 1)
                    logits(pe, NGR - 1)
                    pe.wait_ge(r_step, R_ONEHOT)
                    pe.matmul(bank[0][:, 0:E * NB], lower[:], flat(onehot), start=True, stop=True).then_inc(r_rank, 1)
                    pe.matmul(bank[1][:, 0:E * NB], ones[:], flat(onehot), start=True, stop=True).then_inc(r_rank, 1)

                @block.gpsimd
                def _(pool):
                    pool.memset(meta[:], 0.0).then_inc(r_meta, 1)
                    pool.wait_ge(r_meta, 1)
                    pool.iota(meta[:].bitcast(I32)[:, :, 1], pattern=[[P, NB]], base=0, channel_multiplier=1).then_inc(r_meta, 1)
                    pool.wait_ge(row_loaded, 16)
                    pool.wait_ge(row_meta, 1)
                    for b in range(NB):
                        pool.indirect_dma_start(out=routed[:, :], out_offset=bass.IndirectOffsetOnAxis(ap=posu[:, b:b + 1], axis=0),
                                                in_=rows[:, b, :], in_offset=None).then_inc(row_sent, 16)
                    pool.wait_ge(row_sent, 16 * NB)
            scope.close()

        def slots(se, wa, wb):
            scope = ExitStack()

            def sb(name, shape, dt=F32):
                return scope.enter_context(nc.sbuf_tensor(name, shape, dt))

            rowt = [sb(f"t_row_{i}", [P, ROW]) for i in range(4)]
            b1t = [sb(f"t_b1_{i}", [P, HID]) for i in range(4)]
            b2t = [sb(f"t_b2_{i}", [P, D]) for i in range(4)]
            part = [sb(f"t_par_{i}", [P, 2 * HC + 1]) for i in range(4)]
            xTt = sb("t_xT", [P, KT, P])
            hb = sb("t_hb", [P, HID])
            hn = [sb(f"t_hn_{i}", [P, HID]) for i in range(2)]
            hT = sb("t_hT", [P, HC, P])
            st, st2, st3 = (sb(f"t_st_{i}", [P, 6]) for i in range(3))
            mvt, mv2, mv3 = (sb(f"t_mv_{i}", [P, 2]) for i in range(3))
            var1, var2, var3 = (sb(f"t_var_{i}", [P, 1]) for i in range(3))
            rs1, rs2, rs3 = (sb(f"t_rs_{i}", [P, 1]) for i in range(3))
            ot, sel, res, nrm, ng, w3 = (sb(f"t_{n}", [P, D]) for n in ("ot", "sel", "res", "nrm", "ng", "w3"))
            token = [sb(f"t_token_{i}", [P, 1], U32) for i in range(4)]
            xpb = sb("t_xpb", [P, D])
            z = [sb(f"t_z_{i}", [P, D]) for i in range(2)]
            HB, HTB, OB, XB = bank[0:2], bank[2:4], bank[4:6], bank[6]

            def steps(eng, step):
                def s(n):
                    return (n, n % 4, n // 4) if 0 <= n < SLOTS else None

                for n in range(3):
                    step(*(s(n - back) for back in range(4)))
                with eng.Fori(0, (SLOTS - 3) // 4) as j:
                    for u in range(3, 7):
                        step(*((j * 4 + (u - back), (u - back) % 4, j + (u - back) // 4) for back in range(4)))
                for n in range(SLOTS, SLOTS + 3):
                    step(*(s(n - back) for back in range(4)))

            with nc.Block() as block:
                @block.sync
                def _(sp):
                    def load(n, i, turn):
                        e = sp.value_load(se[0:1, bass.ds(n, 1)], min_val=0, max_val=E - 1)
                        wait(sp, t_end, n * 6 - 21)
                        sp.dma_start(rowt[i][:], routed[bass.ds(n * P, P), :]).then_inc(t_loaded[i], 16)
                        sp.dma_start(b1t[i][:], t["b1"][bass.ds(e, 1)].rearrange("a n -> (a n)").partition_broadcast(P)).then_inc(t_loaded[i], 16)
                        sp.dma_start(b2t[i][:], t["b2"][bass.ds(e, 1)].rearrange("a n -> (a n)").partition_broadcast(P)).then_inc(t_loaded[i], 16)
                        sp.dma_start(part[i][:], t["par"][bass.ds(e, 1)].rearrange("a p n -> (a p) n")).then_inc(t_loaded[i], 16)

                    for n in range(4):
                        load(n, n, 0)
                    with sp.Fori(0, SLOTS // 4 - 1) as j:
                        for u in range(4):
                            load(j * 4 + (4 + u), u, j + 1)
                    for n in range(SLOTS // 4 * 4, SLOTS):
                        load(n, n % 4, n // 4)

                @block.gpsimd
                def _(pool):
                    def step(x, a, c, d):
                        if a:
                            n, i, turn = a
                            pool.wait_ge(t_h, n * 4 + 4)
                            wait(pool, t_hn, n)
                            pool.tensor_tensor(rs1[:], var1[:], minus_half[:, 0:1], ALU.pow).then_inc(t_rs1, 1)
                        if c:
                            n, i, turn = c
                            pool.wait_ge(t_loaded[i], turn * 64 + 64)
                            wait(pool, t_end, n * 6 - 3)
                            pool.tensor_tensor(xpb[:], rowt[i][:, D:2 * D], n2b[:], ALU.add).then_inc(t_xb, 1)
                        if d:
                            n, i, turn = d
                            pool.wait_ge(t_end, n * 6 + 6)
                            wait(pool, t_z, n)
                            pool.tensor_tensor(rs3[:], var3[:], minus_half[:, 0:1], ALU.pow).then_inc(t_rs3, 1)
                        if c:
                            n, i, turn = c
                            pool.wait_ge(t_y, n * 7 + (Y_C + 7))
                            pool.tensor_tensor(rs2[:], var2[:], minus_half[:, 0:1], ALU.pow).then_inc(t_rs2, 1)
                        if d:
                            n, i, turn = d
                            pool.wait_ge(t_z, n + 1)
                            pool.sem_inc(passed, 1)
                            pool.indirect_dma_start(out=x3_rows[:, :], out_offset=bass.IndirectOffsetOnAxis(
                                ap=token[i][:, 0:1], axis=0), in_=z[i % 2][:], in_offset=None,
                                bounds_check=TOK - 1, oob_is_err=False).then_inc(t_sent[i], 16)

                    steps(pool, step)
                    for i in range(4):
                        pool.wait_ge(t_sent[i], 16 * ((SLOTS - 1 - i) // 4 + 1))

                @block.tensor
                def _(pe):
                    def step(x, a, c, d):
                        if a:
                            n, i, turn = a
                            e = pe.value_load(se[0:1, bass.ds(n, 1)], min_val=0, max_val=E - 1)
                            pe.wait_ge(t_xT_kept, n + 1)
                            wait(pe, t_h, n * 4 - 7)
                            for k in range(KT):
                                ins = pe.matmul(HB[i % 2][:], xTt[:, k, :], wa[:, k, bass.ds(e, 1), :].rearrange("p a n -> p (a n)"),
                                                start=k == 0, stop=k == KT - 1)
                            ins.then_inc(t_h_made, 1)
                        if c:
                            n, i, turn = c
                            pe.wait_ge(t_hn, n + 1)
                            wait(pe, t_gelu, n * HC - HC)
                            for k in range(HC):
                                ins = pe.transpose(HTB[i % 2][:, k * P:(k + 1) * P], hn[i % 2][:, k * P:(k + 1) * P], ident[:])
                            ins.then_inc(t_hT_made, 1)
                        if x:
                            n, i, turn = x
                            pe.wait_ge(t_loaded[i], turn * 64 + 64)
                            wait(pe, t_xT_kept, n)
                            for k in range(KT):
                                ins = pe.transpose(XB[:, k * P:(k + 1) * P], rowt[i][:, k * P:(k + 1) * P], ident[:])
                            ins.then_inc(t_xT_made, 1)
                        if c:
                            n, i, turn = c
                            e = pe.value_load(se[0:1, bass.ds(n, 1)], min_val=0, max_val=E - 1)
                            wait(pe, t_y, n * 7 + (Y_C - 12))
                            for k in range(HC):
                                pe.wait_ge(t_gelu, n * HC + (k + 1))
                                ins = pe.matmul(OB[i % 2][:, 0:D], hT[:, k, :], wb[:, bass.ds(e, 1), k, :].rearrange("p a n -> p (a n)"),
                                                start=k == 0, stop=k == HC - 1)
                            ins.then_inc(t_o_made, 1)

                    steps(pe, step)

                @block.scalar
                def _(act):
                    def step(x, a, c, d):
                        if c:
                            n, i, turn = c
                            act.wait_ge(t_hT_made, n + 1)
                            wait(act, t_o_made, n)
                            for k in range(HC):
                                act.activation(hT[:, k, :], HTB[i % 2][:, k * P:(k + 1) * P], ACT.Gelu,
                                               scale=part[i][:, k:k + 1], bias=part[i][:, HC + k:HC + k + 1]).then_inc(t_gelu, 1)
                        if x:
                            n, i, turn = x
                            act.wait_ge(t_xT_made, n + 1)
                            wait(act, t_h_made, n)
                            act.copy(xTt[:], XB[:, 0:D]).then_inc(t_xT_kept, 1)

                    steps(act, step)

                @block.vector
                def _(dve):
                    def chain(done, count, more=0):
                        k = [0]

                        def link(instruction):
                            if k[0]:
                                dve.wait_ge(done, count + (more + k[0]))
                            k[0] += 1
                            instruction().then_inc(done, 1)

                        return link

                    def aggregate(mean_var, statistics):
                        dve.sem_inc(passed, 1)
                        return dve.bn_aggr(mean_var[:], statistics[:])

                    def step(x, a, c, d):
                        if a:
                            n, i, turn = a
                            first = chain(t_h, n * 4)
                            dve.wait_ge(t_h_made, n + 1)
                            wait(dve, t_hn, n)
                            first(lambda: dve.tensor_tensor(hb[:], HB[i % 2][:], b1t[i][:], ALU.add))
                        if d:
                            end = chain(t_end, d[0] * 6)
                            dve.wait_ge(t_rs2, d[0] + 1)
                            end(lambda: dve.tensor_scalar(nrm[:], res[:], mv2[:, 0:1], rs2[:], ALU.subtract, ALU.mult))
                        if a:
                            first(lambda: dve.bn_stats(st[:], hb[:]))
                        if d:
                            end(lambda: dve.tensor_tensor(ng[:], nrm[:], n2g[:], ALU.mult))
                        if a:
                            first(lambda: aggregate(mvt, st))
                        if d:
                            dve.wait_ge(t_xb, d[0] + 1)
                            wait(dve, t_z, d[0])
                            end(lambda: dve.tensor_tensor(w3[:], ng[:], xpb[:], ALU.add))
                        if a:
                            first(lambda: dve.tensor_scalar(var1[:], mvt[:, 1:2], EPS, None, ALU.add))
                        if d:
                            end(lambda: dve.bn_stats(st3[:], w3[:]))
                        if c:
                            n, i, turn = c
                            x1r, wsum = rowt[i][:, 0:D], rowt[i][:, 2 * D:2 * D + 1]
                            dve.tensor_copy(token[i][:], rowt[i][:].bitcast(U32)[:, 2 * D + 1:2 * D + 2]).then_inc(t_y, 1)
                            middle = chain(t_y, n * 7, Y_C + 1)
                        if d:
                            end(lambda: aggregate(mv3, st3))
                        if a:
                            m = a[1]
                            dve.wait_ge(t_rs1, a[0] + 1)
                            wait(dve, t_hT_made, a[0] - 1)
                            dve.tensor_scalar(hn[m % 2][:], hb[:], mvt[:, 0:1], rs1[:], ALU.subtract, ALU.mult).then_inc(t_hn, 1)
                        if c:
                            dve.wait_ge(t_o_made, n + 1)
                            middle(lambda: dve.tensor_tensor(ot[:], OB[i % 2][:, 0:D], b2t[i][:], ALU.add))
                        if c:
                            middle(lambda: dve.scalar_tensor_tensor(sel[:], ot[:], part[i][:, 2 * HC:2 * HC + 1], x1r, ALU.mult, ALU.add))
                        if d:
                            end(lambda: dve.tensor_scalar(var3[:], mv3[:, 1:2], EPS, None, ALU.add))
                        if c:
                            middle(lambda: dve.scalar_tensor_tensor(res[:], sel[:], wsum, x1r, ALU.mult, ALU.add))
                        if c:
                            middle(lambda: dve.bn_stats(st2[:], res[:]))
                        if d:
                            m = d[1]
                            dve.wait_ge(t_rs3, d[0] + 1)
                            wait(dve, t_sent[(m - 2) % 4], (d[2] + (1 if m >= 2 else 0)) * 16)
                            dve.tensor_scalar(z[m % 2][:], w3[:], mv3[:, 0:1], rs3[:], ALU.subtract, ALU.mult).then_inc(t_z, 1)
                        if c:
                            middle(lambda: aggregate(mv2, st2))
                            middle(lambda: dve.tensor_scalar(var2[:], mv2[:, 1:2], EPS, None, ALU.add))

                    steps(dve, step)
            scope.close()

        ROUTER = 19

        def experts1(w7g, w7u, w7d):
            scope = ExitStack()

            def sb(name, shape, dt=F32):
                return scope.enter_context(nc.sbuf_tensor("f_" + name, shape, dt))

            w7gh, w7gl, w7uh, w7ul = (sb(n, [P, KT, UNITS, F1], F32R) for n in ("w7gh", "w7gl", "w7uh", "w7ul"))
            w7dh, w7dl = (sb(n, [P, UNITS, D], F32R) for n in ("w7dh", "w7dl"))
            xg = sb("xg", [P, GB, D])
            xres = sb("xres", [P, GB, D])
            xgT = sb("xgT", [P, KT, GB * P])
            xTh, xTl = (sb(n, [P, KT, GB * P], F32R) for n in ("xTh", "xTl"))
            silu = [sb(f"silu_{i}", [P, GB * P]) for i in range(2)]
            prod = [sb(f"prod_{i}", [P, GB * P]) for i in range(2)]
            wB = [sb(f"wB_{i}", [P, GB * P]) for i in range(2)]
            hid = [sb(f"hid_{i}", [P, GB * P]) for i in range(2)]
            hidh, hidl = ([sb(f"hid_{n}_{i}", [P, GB * P], F32R) for i in range(2)] for n in ("high", "low"))
            yg = sb("yg", [P, GB, D])
            xog = sb("xog", [P, GB, D])
            stg = sb("stg", [P, GB, 6])
            mvg = sb("mvg", [P, GB, 2])
            varg = sb("varg", [P, GB])
            rstdg = sb("rstdg", [P, GB])
            lg, sh, es, s, eq, cand, hit, s2, eq2, cand2, hit2, drop, keep, wts = (
                sb(n, [P, GB, E]) for n in ("lg", "sh", "es", "s", "eq", "cand", "hit", "s2", "eq2", "cand2", "hit2", "drop", "keep", "wts"))
            mx, sm, rc, m1, c1, m2, c2 = (sb(n, [P, GB]) for n in ("mx", "sm", "rc", "m1", "c1", "m2", "c2"))
            flat = lambda a: a[:].rearrange("p a b -> p (a b)")
            over = lambda a: a[:].unsqueeze(2).broadcast_to([P, GB, E])
            up = ascend[:].unsqueeze(1).broadcast_to([P, GB, E])
            SHARED = UNITS - E
            GBANK, UBANK, WBANK, XBANK = bank[4], bank[5], bank[6], bank[7]

            with nc.Block() as block:
                @block.sync
                def _(sp):
                    def group(ap, g):
                        return ap[bass.ds(g * GB, GB)].rearrange("b p n -> p b n")

                    def load(g):
                        sp.wait_ge(f_xres, g + 1)
                        sp.wait_ge(f_xT_made, g * KT + KT)
                        sp.dma_start(xg[:], group(x5, g)).then_inc(f_loaded, 16)

                    def store(g):
                        sp.wait_ge(f_done, g * GB + 2 * GB)
                        sp.dma_start(group(out, g), xog[:]).then_inc(f_stored, 16)

                    load(0)
                    with sp.Fori(0, NGR - 1) as g:
                        load(g + 1)
                        store(g)
                    store(NGR - 1)
                    sp.wait_ge(f_stored, 16 * (NGR + 1))

                @block.gpsimd
                def _(pool):
                    for k in range(UNITS):
                        parts = ((w7g[:, :, k, :], w7gh[:, :, k, :], w7gl[:, :, k, :]), (w7u[:, :, k, :], w7uh[:, :, k, :], w7ul[:, :, k, :]),
                                 (w7d[:, k, :], w7dh[:, k, :], w7dl[:, k, :]))
                        for raw, high, low in parts:
                            pool.tensor_copy(high, raw).then_inc(f_whi, 1)
                        for i, (raw, high, low) in enumerate(parts):
                            pool.wait_ge(f_whi, 3 * k + i + 1)
                            pool.tensor_tensor(low, raw, high.bitcast(F32), ALU.subtract).then_inc(f_wlo, 1)
                    with pool.Fori(0, NGR) as g:
                        pool.wait_ge(f_loaded, g * 16 + 16)
                        pool.wait_ge(f_res, g * GB + GB)
                        pool.sem_inc(passed, 1)
                        pool.tensor_copy(xres[:], xg[:]).then_inc(f_xres, 1)
                        pool.wait_ge(f_ln, g * 6 + 6)
                        pool.wait_ge(f_done, g * GB + GB)
                        pool.tensor_tensor(rstdg[:], varg[:], minus_half[:, 0:GB], ALU.pow).then_inc(f_rstd, 1)

                @block.tensor
                def _(pe):
                    def transposed(g):
                        pe.wait_ge(f_loaded, g * 16 + 16)
                        pe.wait_ge(f_xT_kept, g * KT + 1)
                        pe.wait_ge(f_wB_kept, g * E + 1)
                        for k, to in enumerate((XBANK, WBANK)):
                            for b in range(GB):
                                ins = pe.transpose(to[:, b * P:(b + 1) * P], xg[:, b, k * P:(k + 1) * P], ident[:])
                            ins.then_inc(f_xT_made, 1)

                    def group(g, last):
                        def product(o, high, low, k):
                            for i in range(KT):
                                pe.matmul(o[:], high[:, i, k, :], xTh[:, i, :], start=i == 0, stop=False)
                                pe.matmul(o[:], high[:, i, k, :], xTl[:, i, :], start=False, stop=False)
                                ins = pe.matmul(o[:], low[:, i, k, :], xTh[:, i, :], start=False, stop=i == KT - 1)
                            return ins

                        def in_products(k):
                            pe.wait_ge(f_silu, g * UNITS + (k + 1))
                            if k == 0:
                                pe.wait_ge(f_split, g * (2 * KT) + 2 * KT)
                            pe.wait_ge(f_wlo, 3 * k + 3)
                            product(GBANK, w7gh, w7gl, k).then_inc(f_gate_made, 1)
                            pe.wait_ge(f_hid, g * UNITS + (k + 3))
                            product(UBANK, w7uh, w7ul, k).then_inc(f_up_made, 1)

                        def spread(k):
                            e = k - SHARED
                            if e == 0:
                                pe.wait_ge(f_step, g * ROUTER + ROUTER)
                            pe.wait_ge(f_wB_kept, g * E + (e + 1))
                            for b in range(GB):
                                ins = pe.transpose(WBANK[:, b * P:(b + 1) * P], wts[:, b, e:e + 1].broadcast_to([P, P]), ident[:])
                            ins.then_inc(f_wB_made, 1)

                        def out_product(k):
                            if k == 0:
                                pe.wait_ge(f_res, g * GB + GB)
                            pe.wait_ge(f_hi, g * UNITS + (k + 1))
                            pe.wait_ge(f_lo, g * UNITS + (k + 2))
                            for b in range(GB):
                                o, w = bank[b][:, 0:D], slice(b * P, (b + 1) * P)
                                pe.matmul(o, hidh[k % 2][:, w], w7dh[:, k, :], start=k == 0, stop=False)
                                pe.matmul(o, hidh[k % 2][:, w], w7dl[:, k, :], start=False, stop=False)
                                ins = pe.matmul(o, hidl[k % 2][:, w], w7dh[:, k, :], start=False, stop=k == UNITS - 1)
                            ins.then_inc(f_o_made, 1)

                        pe.wait_ge(f_xT_kept, g * KT + (KT + 1))
                        for b in range(GB):
                            for k in range(KT):
                                ins = pe.matmul(XBANK[:, b * E:(b + 1) * E], xgT[:, k, b * P:(b + 1) * P], w7r[:, k, :],
                                                start=k == 0, stop=k == KT - 1)
                        ins.then_inc(f_logit_made, 1)
                        for k in range(UNITS):
                            in_products(k)
                            if k + 1 >= SHARED and k + 1 < UNITS:
                                spread(k + 1)
                            if k == UNITS - 1 and not last:
                                transposed(g + 1)
                            if k:
                                out_product(k - 1)
                        out_product(UNITS - 1)

                    transposed(0)
                    with pe.Fori(0, NGR - 1) as g:
                        group(g, False)
                    group(NGR - 1, True)

                @block.scalar
                def _(act):
                    with act.Fori(0, NGR) as g:
                        for k in range(KT):
                            act.wait_ge(f_xT_made, g * KT + (k + 1 + KT))
                            act.wait_ge(f_logit_made, g + 1)
                            wait(act, f_split, g * (2 * KT))
                            act.copy(xgT[:, k, :], (XBANK, WBANK)[k][:]).then_inc(f_xT_kept, 1)
                        act.wait_ge(f_step, g * ROUTER + 3)
                        act.activation(es[:], sh[:], ACT.Exp).then_inc(f_exp, 1)
                        for k in range(UNITS):
                            act.wait_ge(f_gate_made, g * UNITS + (k + 1))
                            act.wait_ge(f_hid, g * UNITS + (k + 2))
                            act.activation(silu[k % 2][:], GBANK[:], ACT.Silu).then_inc(f_silu, 1)
                            if k + 1 >= SHARED and k + 1 < UNITS:
                                act.wait_ge(f_wB_made, g * E + (k + 1 - SHARED + 2))
                                act.copy(wB[(k + 1) % 2][:], WBANK[:]).then_inc(f_wB_kept, 1)
                            act.wait_ge(f_hid, g * UNITS + (k + 4))
                            act.wait_ge(f_o_made, g * UNITS + (k + 1))
                            act.copy(hidh[k % 2][:], hid[k % 2][:]).then_inc(f_hi, 1)

                @block.vector
                def _(dve):
                    def split(g):
                        wait(dve, f_up_made, g * UNITS)
                        for k in range(KT):
                            dve.wait_ge(f_xT_kept, g * KT + (k + 2))
                            dve.sem_inc(passed, 1)
                            dve.tensor_copy(xTh[:, k, :], xgT[:, k, :]).then_inc(f_split, 1)
                            dve.wait_ge(f_split, g * (2 * KT) + (2 * k + 1))
                            dve.tensor_tensor(xTl[:, k, :], xgT[:, k, :], xTh[:, k, :].bitcast(F32), ALU.subtract).then_inc(f_split, 1)

                    def layer_norm(g):
                        for b in range(GB):
                            dve.wait_ge(f_res, g * GB + (b + 1 + GB))
                            dve.bn_stats(stg[:, b, :], yg[:, b, :]).then_inc(f_ln, 1)
                        dve.wait_ge(f_ln, g * 6 + 4)
                        dve.sem_inc(passed, 1)
                        for b in range(GB):
                            ins = dve.bn_aggr(mvg[:, b, :], stg[:, b, :])
                        ins.then_inc(f_ln, 1)
                        dve.wait_ge(f_ln, g * 6 + 5)
                        dve.tensor_scalar(varg[:], mvg[:, :, 1], EPS, None, ALU.add).then_inc(f_ln, 1)
                        dve.wait_ge(f_rstd, g + 1)
                        dve.wait_ge(f_stored, g * 16 + 16)
                        for b in range(GB):
                            dve.tensor_scalar(xog[:, b, :], yg[:, b, :], mvg[:, b, 0:1], rstdg[:, b:b + 1],
                                              ALU.subtract, ALU.mult).then_inc(f_done, 1)

                    def group(g, first, last):
                        k_ = [0]

                        def link(ins):
                            k_[0] += 1
                            ins.then_inc(f_step, 1)
                            dve.wait_ge(f_step, g * ROUTER + k_[0])

                        def low(k):
                            dve.wait_ge(f_hi, g * UNITS + (k + 1))
                            dve.wait_ge(f_o_made, g * UNITS + (k + 1))
                            dve.tensor_tensor(hidl[k % 2][:], hid[k % 2][:], hidh[k % 2][:].bitcast(F32), ALU.subtract).then_inc(f_lo, 1)

                        dve.wait_ge(f_logit_made, g + 2)
                        link(dve.tensor_copy(flat(lg), XBANK[:, 0:GB * E]))
                        link(dve.tensor_reduce(mx[:], lg[:], AX.X, ALU.max))
                        link(dve.tensor_tensor(sh[:], lg[:], over(mx), ALU.subtract))
                        dve.wait_ge(f_exp, g + 2)
                        link(dve.tensor_reduce(sm[:], es[:], AX.X, ALU.add))
                        link(dve.reciprocal(rc[:], sm[:]))
                        link(dve.tensor_tensor(s[:], es[:], over(rc), ALU.mult))
                        link(dve.tensor_reduce(m1[:], s[:], AX.X, ALU.min))
                        link(dve.tensor_tensor(eq[:], s[:], over(m1), ALU.is_equal))
                        link(dve.tensor_tensor(cand[:], eq[:], up, ALU.mult))
                        link(dve.tensor_reduce(c1[:], cand[:], AX.X, ALU.max))
                        link(dve.tensor_tensor(hit[:], up, over(c1), ALU.is_equal))
                        link(dve.scalar_tensor_tensor(flat(s2), flat(hit), 4.0, flat(s), ALU.mult, ALU.add))
                        link(dve.tensor_reduce(m2[:], s2[:], AX.X, ALU.min))
                        link(dve.tensor_tensor(eq2[:], s2[:], over(m2), ALU.is_equal))
                        link(dve.tensor_tensor(cand2[:], eq2[:], up, ALU.mult))
                        link(dve.tensor_reduce(c2[:], cand2[:], AX.X, ALU.max))
                        link(dve.tensor_tensor(hit2[:], up, over(c2), ALU.is_equal))
                        link(dve.tensor_tensor(drop[:], hit[:], hit2[:], ALU.add))
                        dve.wait_ge(f_wB_made, g * E + 1)
                        dve.tensor_scalar(keep[:], drop[:], -1.0, 1.0, ALU.mult, ALU.add).then_inc(f_keep, 1)
                        dve.wait_ge(f_keep, g + 1)
                        link(dve.tensor_tensor(wts[:], s[:], keep[:], ALU.mult))
                        assert k_[0] == ROUTER
                        for k in range(UNITS):
                            dve.wait_ge(f_silu, g * UNITS + (k + 2))
                            dve.wait_ge(f_up_made, g * UNITS + (k + 1))
                            if k >= SHARED:
                                dve.tensor_tensor(prod[k % 2][:], UBANK[:], silu[k % 2][:], ALU.mult).then_inc(f_prod, 1)
                            if k < SHARED:
                                dve.wait_ge(f_lo, g * UNITS + k)
                                dve.tensor_tensor(hid[k % 2][:], UBANK[:], silu[k % 2][:], ALU.mult).then_inc(f_hid, 1)
                            else:
                                dve.wait_ge(f_prod, g * E + (k - SHARED + 1))
                                dve.wait_ge(f_wB_kept, g * E + (k - SHARED + 2))
                                dve.tensor_tensor(hid[k % 2][:], prod[k % 2][:], wB[k % 2][:], ALU.mult).then_inc(f_hid, 1)
                            low(k)
                            if k == SHARED - 1 and not first:
                                layer_norm(g - 1)
                        if not last:
                            split(g + 1)
                        dve.wait_ge(f_o_made, g * UNITS + (UNITS + 2))
                        dve.wait_ge(f_xres, g + 2)
                        for b in range(GB):
                            dve.tensor_tensor(yg[:, b, :], bank[b][:, 0:D], xres[:, b, :], ALU.add).then_inc(f_res, 1)

                    split(0)
                    group(0, True, False)
                    with dve.Fori(0, NGR - 2) as j:
                        group(j + 1, False, False)
                    group(NGR - 1, False, True)
                    layer_norm(NGR - 1)
            scope.close()

        prefetched = [0]
        with ExitStack() as scope:
            ctxs = scope.enter_context(nc.sbuf_tensor("ctxs", [P, TOK], F32))
            itok = scope.enter_context(nc.sbuf_tensor("itok", [P, TOK], I32))
            w_raw = scope.enter_context(nc.sbuf_tensor("w_raw", [P, KT * HID], F32))
            attention(CAUSAL, later + [(w_raw[:], t["wa0"][0]),
                                       (ctxs[:].rearrange("p (b n) -> p b n", b=NB), t["ctx"].rearrange("b p n -> p b n")),
                                       (itok[:].rearrange("p (b n) -> p b n", b=NB), t["itok"].rearrange("b p n -> p b n"))])
            experts0(ctxs, itok, w_raw)
        with ExitStack() as scope:
            wa = scope.enter_context(nc.sbuf_tensor("wa", [P, KT, E, HID], F32))
            wb = scope.enter_context(nc.sbuf_tensor("wb", [P, E, HC, D], F32))
            posu = scope.enter_context(nc.sbuf_tensor("posu", [P, NB], U32))
            meta = scope.enter_context(nc.sbuf_tensor("meta", [P, NB, ROW - 2 * D], F32))
            se = scope.enter_context(nc.sbuf_tensor("se", [P, SLOTS], I32))
            attention(SCALED, [(wa[:], t["wa1"]), (wb[:], t["wb1"])])
            routing(posu, meta, se)
            slots(se, wa, wb)
        attention(ROTARY, [])
        with ExitStack() as scope:
            w7g, w7u = (scope.enter_context(nc.sbuf_tensor(n, [P, KT, UNITS, F1], F32)) for n in ("w7g", "w7u"))
            w7d = scope.enter_context(nc.sbuf_tensor("w7d", [P, UNITS, D], F32))
            attention(CROSS, [(w7g[:], t["w7g"]), (w7u[:], t["w7u"]), (w7d[:], t["w7d"])])
            experts1(w7g, w7u, w7d)


def host_layout(inputs):
    g = {k: np.asarray(a) for k, a in inputs.items()}

    def kt(w):
        return w.reshape(w.shape[0] // P, P, w.shape[1]).transpose(1, 0, 2)

    wqkv = np.zeros((P, 4, KT, 3 * D), np.float32)
    wqkv[:, 0] = kt(g["L0_attn_w_attn"])
    for i, n in enumerate(("q", "k", "v")):
        wqkv[:, 1, :, i * D:(i + 1) * D] = kt(g[f"L0_ffn_{n}_w"])
    wqkv[:, 2] = kt(g["L1_attn_w_qkv"].T)
    wqkv[:, 3, :, 0:D] = kt(g["L1_xattn_Wq"])
    wqkv[:, 3, 0, D:2 * D] = g["L1_xattn_Wk"]
    wqkv[:, 3, 0, 2 * D:] = g["L1_xattn_Wv"]
    wo = np.stack([kt(g["L0_attn_w_proj"]), kt(g["L0_ffn_out_w"]), kt(g["L1_attn_w_out"].T), kt(g["L1_xattn_Wo"])], 1)
    key, query = np.arange(P)[:, None], np.arange(P)[None, :]
    masked = np.where(key > query, -BIG, 0.0).astype(np.float32)
    inv_freq = (1.0 / 10000.0 ** (np.arange(0, DK, 2, dtype=np.float32) / DK)).astype(np.float32)
    freqs = np.arange(P, dtype=np.float32)[:, None] * inv_freq[None, :]
    def expert_in(w):
        return w.reshape(w.shape[0], -1, P, w.shape[2]).transpose(2, 1, 0, 3)

    def expert_out(w):
        return w.reshape(w.shape[0], -1, P, w.shape[2]).transpose(2, 0, 1, 3)

    def by_expert(w):
        return w.reshape(w.shape[0], -1, P, w.shape[2]).transpose(0, 2, 1, 3).reshape(w.shape[0], P, -1)

    def shared_in(w):
        return w.reshape(D, D // F1, F1).transpose(1, 0, 2)

    par = np.concatenate([g["L0_ffn_ln_g"].reshape(E, HC, P).transpose(0, 2, 1), g["L0_ffn_ln_b"].reshape(E, HC, P).transpose(0, 2, 1),
                          np.broadcast_to(g["L0_ffn_res_scale"][:, None, None], (E, P, 1))], 2)
    t = {
        "wa0": by_expert(g["L0_xattn_proj_in"].transpose(0, 2, 1)), "wb0": by_expert(g["L0_xattn_proj_out"].transpose(0, 2, 1)),
        "wa1": expert_in(g["L0_ffn_w1"]), "wb1": expert_out(g["L0_ffn_w2"]), "b1": g["L0_ffn_b1"], "b2": g["L0_ffn_b2"], "par": par,
        "w7g": expert_in(np.concatenate([shared_in(g["L1_ffn_ws_gate"]), g["L1_ffn_w_gate"]])),
        "w7u": expert_in(np.concatenate([shared_in(g["L1_ffn_ws_up"]), g["L1_ffn_w_up"]])),
        "w7d": np.concatenate([g["L1_ffn_ws_down"].reshape(D // F1, F1, D), g["L1_ffn_w_down"]]).transpose(1, 0, 2),
        "w7r": kt(g["L1_ffn_router_w"]), "wlog": kt(g["L0_ffn_moe_gate_w"]), "b_log": g["L0_ffn_moe_gate_b"],
        "n2_g": g["L0_ffn_n2_g"], "n2_b": g["L0_ffn_n2_b"],
        "ones": np.ones((P, P), np.float32), "lower": np.triu(np.ones((P, P), np.float32), 1),
        "ascend": 1 + np.arange(E, dtype=np.float32),
        "descend": E - np.arange(E, dtype=np.float32), "iotas": np.tile(np.arange(NB, dtype=np.float32) * P, E),
        "slotn": np.repeat(np.arange(SLOTS, dtype=np.float32), E),
        "keepmask": np.tile((np.arange(NB) > 0).astype(np.float32), E),
        "x": g["x"], "ctx": g["ctx_512"], "itok": g["itok_BxS2xS_0_7"],
        "wqkv": wqkv, "wo": wo, "gatew": kt(g["L0_ffn_gate_w"]),
        "b_qkv0": g["L0_attn_b_attn"], "b_qkv3": np.concatenate([g["L1_xattn_bq"], g["L1_xattn_bk"], g["L1_xattn_bv"]]),
        "b_o0": g["L0_attn_b_proj"], "b_o2": g["L1_attn_b_out"], "b_o3": g["L1_xattn_bo"],
        "scale_w": g["L0_ffn_scale_w"].reshape(-1), "gate_b": g["L0_ffn_gate_b"],
        "n1_g": g["L0_ffn_n1_g"], "n1_b": g["L0_ffn_n1_b"],
        "ident": np.eye(P, dtype=np.float32),
        "maskq": masked.T,
        "cos": np.cos(freqs).astype(np.float32), "sin": np.stack([-np.sin(freqs), np.sin(freqs)], 1).astype(np.float32),
    }
    return {k: np.ascontiguousarray(a) for k, a in t.items()}


def kernel(**inputs):
    import concourse.bacc as bacc
    from concourse.bass_utils import run_bass_kernel_spmd

    nc = bacc.Bacc("TRN2", target_bir_lowering=False, num_devices=1)
    arrays = host_layout(inputs)
    t = {n: nc.dram_tensor(f"in_{n}", a.shape, mybir.dt.from_np(a.dtype), kind="ExternalInput").ap() for n, a in arrays.items()}
    out = nc.dram_tensor("out_dram", (NB, P, D), F32, kind="ExternalOutput").ap()
    program(nc, t, out)
    r = run_bass_kernel_spmd(nc, [{f"in_{n}": a for n, a in arrays.items()}], core_ids=[0])
    return r.results[0]["out_dram"]
```
